# Optimizing a Trainium2 kernel written in Bass

```python
import numpy as np
import jax
import jax.numpy as jnp

def _softmax(x, axis=-1):
    return jax.nn.softmax(x, axis=axis)

def _gelu(x):
    return jax.nn.gelu(x, approximate=True)

def _silu(x):
    return jax.nn.silu(x)

def _sigmoid(x):
    return jax.nn.sigmoid(x)

def _layernorm(x, axis=-1, eps=1e-05):
    m = jnp.mean(x, axis=axis, keepdims=True)
    v = jnp.var(x, axis=axis, keepdims=True)
    return (x - m) / jnp.sqrt(v + eps)

def _scatter_add(tgt, idx, src, axis=0):
    return tgt.at[idx].add(src)

def _segment_sum(src, seg, n):
    return jax.ops.segment_sum(src, seg, n)
kernel_name = 'mk_decoder_preln_d1_seqx_r2_e27f69'

def setup_inputs(seed: int=0):
    np.random.seed(seed)
    _w = jnp.asarray

    def _rec_inputs():
        import jax
        import jax.numpy as jnp
        _rk = jax.random.key(seed)
        x = -0.0002928 + 1 * jax.random.normal(jax.random.fold_in(_rk, 1), (2, 2048, 512), jnp.float32)
        _lenS = 2048 - jax.random.randint(jax.random.fold_in(_rk, 7), (2,), 0, max(1, 2048 // 4) + 1, jnp.int32)
        _lenS2 = 77 - jax.random.randint(jax.random.fold_in(_rk, 8), (2,), 0, max(1, 77 // 4) + 1, jnp.int32)
        _ctx_768P = jax.random.normal(jax.random.fold_in(_rk, 11), (2, 16, 384), jnp.float32)
        _ctx_768c = jax.random.dirichlet(jax.random.fold_in(_rk, 511), 0.3 * jnp.ones((16,), jnp.float32), (2, 77))
        _ctx_768t = jnp.einsum('bsk,bkd->bsd', _ctx_768c, _ctx_768P)
        _ctx_768t = _ctx_768t * jax.lax.rsqrt(jnp.mean(jnp.square(_ctx_768t)) + 1e-12) * 0.953939
        ctx_768 = 2.09791e-05 + 1.00001 * (_ctx_768t + 0.3 * jax.random.normal(jax.random.fold_in(_rk, 611), (2, 77, 384), jnp.float32))
        return (x, ctx_768)
    x, ctx_768 = _rec_inputs()

    def _L0_attn_setup():
        import jax, jax.numpy as jnp
        import numpy as np
        D = 512
        H = 16
        DH = D // H
        R = 256.0
        SCALE = float(np.sqrt(DH))
        NEG_INF = -1e+30
        key = jax.random.key(seed)
        ks = jax.random.split(key, 8)
        B, T = (2, 1024)
        w = lambda k, sh: jax.random.normal(k, sh, dtype=jnp.float32) * 0.02
        return {'x': jax.random.normal(ks[0], (B, T, D), dtype=jnp.float32), 'Wq': w(ks[1], (D, D)), 'Wk': w(ks[2], (D, D)), 'Wv': w(ks[3], (D, D)), 'Wo_w': w(ks[4], (D, D)), 'Wo_b': jnp.zeros((D,), jnp.float32), 'span_w': w(ks[5], (D, H)), 'span_b': jnp.zeros((H,), jnp.float32)}
    _L0_attn_all = _L0_attn_setup()
    _L0_attn_in = {k: v for k, v in _L0_attn_all.items() if k in ('Wq', 'Wk', 'Wv', 'Wo_w', 'Wo_b', 'span_w', 'span_b')}
    del _L0_attn_all

    def _L0_xattn_setup():
        import jax, jax.numpy as jnp
        import numpy as np
        HEADS = 8
        DIM_HEAD = 128
        ATTN_MATRIX_SCALE = 1.5
        SCALE = DIM_HEAD ** (-0.5)

        def _split_heads(t):
            b, n, _ = t.shape
            t = t.reshape(b, n, HEADS, DIM_HEAD)
            return t.transpose(2, 0, 1, 3).reshape(HEADS, b * n, DIM_HEAD)
        key = jax.random.key(seed)
        ks = jax.random.split(key, 7)
        b, n, m = (2, 1024, 1024)
        qd, cd, inner = (512, 384, HEADS * DIM_HEAD)
        x = jax.random.normal(ks[0], (b, n, qd), dtype=jnp.float32)
        context = jax.random.normal(ks[1], (b, m, cd), dtype=jnp.float32)
        Wq = jax.random.normal(ks[2], (qd, inner), dtype=jnp.float32) * qd ** (-0.5)
        Wk = jax.random.normal(ks[3], (cd, inner), dtype=jnp.float32) * cd ** (-0.5)
        Wv = jax.random.normal(ks[4], (cd, inner), dtype=jnp.float32) * cd ** (-0.5)
        Wout = jax.random.normal(ks[5], (inner, qd), dtype=jnp.float32) * inner ** (-0.5)
        bout = jnp.zeros((qd,), dtype=jnp.float32)
        return {'x': x, 'context': context, 'Wq': Wq, 'Wk': Wk, 'Wv': Wv, 'Wout': Wout, 'bout': bout}
    _L0_xattn_all = _L0_xattn_setup()
    _L0_xattn_in = {k: v for k, v in _L0_xattn_all.items() if k in ('Wq', 'Wk', 'Wv', 'Wout', 'bout')}
    del _L0_xattn_all

    def _L0_ffn_setup():
        import jax, jax.numpy as jnp
        import numpy as np
        B, L, D = (4, 1024, 512)
        H = 16
        E = 16
        NS = 16
        S = NS // E
        F = 2048
        EPS = 1e-05

        def _layernorm(x, g, b):
            mu = jnp.mean(x, axis=-1, keepdims=True)
            var = jnp.mean(jnp.square(x - mu), axis=-1, keepdims=True)
            return (x - mu) * jax.lax.rsqrt(var + EPS) * g + b

        def _mha(q, k, v, Wq, bq, Wk, bk, Wv, bv, Wo, bo):
            Bq, Lq, Dm = q.shape
            dh = Dm // H
            qh = (q @ Wq + bq).reshape(Bq, Lq, H, dh)
            kh = (k @ Wk + bk).reshape(Bq, -1, H, dh)
            vh = (v @ Wv + bv).reshape(Bq, -1, H, dh)
            scores = jnp.einsum('bqhd,bkhd->bhqk', qh, kh) / jnp.asarray(np.sqrt(dh), q.dtype)
            attn = jax.nn.softmax(scores, axis=-1)
            out = jnp.einsum('bhqk,bkhd->bqhd', attn, vh).reshape(Bq, Lq, Dm)
            return out @ Wo + bo
        key = jax.random.key(seed)
        ks = jax.random.split(key, 32)
        s = 0.02
        d = {}
        d['x'] = jax.random.normal(ks[0], (B, L, D), jnp.float32)
        d['slot_query'] = jax.random.normal(ks[1], (1, NS, D), jnp.float32) * 0.01
        for i, nm in enumerate(['d_Wq', 'd_Wk', 'd_Wv', 'd_Wo']):
            d[nm] = jax.random.normal(ks[2 + i], (D, D), jnp.float32) * s
        for nm in ['d_bq', 'd_bk', 'd_bv', 'd_bo']:
            d[nm] = jnp.zeros((D,), jnp.float32)
        for i, nm in enumerate(['c_Wq', 'c_Wk', 'c_Wv', 'c_Wo']):
            d[nm] = jax.random.normal(ks[6 + i], (D, D), jnp.float32) * s
        for nm in ['c_bq', 'c_bk', 'c_bv', 'c_bo']:
            d[nm] = jnp.zeros((D,), jnp.float32)
        d['e_ln_g'] = jnp.ones((E, D), jnp.float32)
        d['e_ln_b'] = jnp.zeros((E, D), jnp.float32)
        d['e_W1'] = jax.random.normal(ks[10], (E, D, F), jnp.float32) * s
        d['e_b1'] = jnp.zeros((E, F), jnp.float32)
        d['e_Wg'] = jax.random.normal(ks[11], (E, D, F), jnp.float32) * s
        d['e_bg'] = jnp.zeros((E, F), jnp.float32)
        d['e_W2'] = jax.random.normal(ks[12], (E, F, D), jnp.float32) * s
        d['e_b2'] = jnp.zeros((E, D), jnp.float32)
        return d
    _L0_ffn_all = _L0_ffn_setup()
    _L0_ffn_in = {k: v for k, v in _L0_ffn_all.items() if k in ('slot_query', 'd_Wq', 'd_Wk', 'd_Wv', 'd_Wo', 'd_bq', 'd_bk', 'd_bv', 'd_bo', 'c_Wq', 'c_Wk', 'c_Wv', 'c_Wo', 'c_bq', 'c_bk', 'c_bv', 'c_bo', 'e_ln_g', 'e_ln_b', 'e_W1', 'e_b1', 'e_Wg', 'e_bg', 'e_W2', 'e_b2')}
    del _L0_ffn_all
    return {'x': x, 'ctx_768': ctx_768, 'L0_attn_Wq': _L0_attn_in['Wq'], 'L0_attn_Wk': _L0_attn_in['Wk'], 'L0_attn_Wv': _L0_attn_in['Wv'], 'L0_attn_Wo_w': _L0_attn_in['Wo_w'], 'L0_attn_Wo_b': _L0_attn_in['Wo_b'], 'L0_attn_span_w': _L0_attn_in['span_w'], 'L0_attn_span_b': _L0_attn_in['span_b'], 'L0_xattn_Wq': _L0_xattn_in['Wq'], 'L0_xattn_Wk': _L0_xattn_in['Wk'], 'L0_xattn_Wv': _L0_xattn_in['Wv'], 'L0_xattn_Wout': _L0_xattn_in['Wout'], 'L0_xattn_bout': _L0_xattn_in['bout'], 'L0_ffn_slot_query': _L0_ffn_in['slot_query'], 'L0_ffn_d_Wq': _L0_ffn_in['d_Wq'], 'L0_ffn_d_Wk': _L0_ffn_in['d_Wk'], 'L0_ffn_d_Wv': _L0_ffn_in['d_Wv'], 'L0_ffn_d_Wo': _L0_ffn_in['d_Wo'], 'L0_ffn_d_bq': _L0_ffn_in['d_bq'], 'L0_ffn_d_bk': _L0_ffn_in['d_bk'], 'L0_ffn_d_bv': _L0_ffn_in['d_bv'], 'L0_ffn_d_bo': _L0_ffn_in['d_bo'], 'L0_ffn_c_Wq': _L0_ffn_in['c_Wq'], 'L0_ffn_c_Wk': _L0_ffn_in['c_Wk'], 'L0_ffn_c_Wv': _L0_ffn_in['c_Wv'], 'L0_ffn_c_Wo': _L0_ffn_in['c_Wo'], 'L0_ffn_c_bq': _L0_ffn_in['c_bq'], 'L0_ffn_c_bk': _L0_ffn_in['c_bk'], 'L0_ffn_c_bv': _L0_ffn_in['c_bv'], 'L0_ffn_c_bo': _L0_ffn_in['c_bo'], 'L0_ffn_e_ln_g': _L0_ffn_in['e_ln_g'], 'L0_ffn_e_ln_b': _L0_ffn_in['e_ln_b'], 'L0_ffn_e_W1': _L0_ffn_in['e_W1'], 'L0_ffn_e_b1': _L0_ffn_in['e_b1'], 'L0_ffn_e_Wg': _L0_ffn_in['e_Wg'], 'L0_ffn_e_bg': _L0_ffn_in['e_bg'], 'L0_ffn_e_W2': _L0_ffn_in['e_W2'], 'L0_ffn_e_b2': _L0_ffn_in['e_b2']}

def reference(x, ctx_768, L0_attn_Wq, L0_attn_Wk, L0_attn_Wv, L0_attn_Wo_w, L0_attn_Wo_b, L0_attn_span_w, L0_attn_span_b, L0_xattn_Wq, L0_xattn_Wk, L0_xattn_Wv, L0_xattn_Wout, L0_xattn_bout, L0_ffn_slot_query, L0_ffn_d_Wq, L0_ffn_d_Wk, L0_ffn_d_Wv, L0_ffn_d_Wo, L0_ffn_d_bq, L0_ffn_d_bk, L0_ffn_d_bv, L0_ffn_d_bo, L0_ffn_c_Wq, L0_ffn_c_Wk, L0_ffn_c_Wv, L0_ffn_c_Wo, L0_ffn_c_bq, L0_ffn_c_bk, L0_ffn_c_bv, L0_ffn_c_bo, L0_ffn_e_ln_g, L0_ffn_e_ln_b, L0_ffn_e_W1, L0_ffn_e_b1, L0_ffn_e_Wg, L0_ffn_e_bg, L0_ffn_e_W2, L0_ffn_e_b2):
    import jax
    import jax.numpy as jnp

    def _L0_attn_ref(x, Wq, Wk, Wv, Wo_w, Wo_b, span_w, span_b):
        import jax, jax.numpy as jnp
        import numpy as np
        D = 512
        H = 16
        DH = D // H
        R = 256.0
        SCALE = float(np.sqrt(DH))
        NEG_INF = -1e+30
        B, T, _ = x.shape
        q = (x @ Wq).reshape(B, T, H, DH).transpose(0, 2, 1, 3)
        k = (x @ Wk).reshape(B, T, H, DH).transpose(0, 2, 1, 3)
        v = (x @ Wv).reshape(B, T, H, DH).transpose(0, 2, 1, 3)
        z = T * jax.nn.sigmoid(x.mean(axis=1) @ span_w + span_b)
        idx = jnp.arange(T, dtype=jnp.float32)
        dist = jnp.clip(idx[:, None] - idx[None, :], 0.0, None)
        causal = idx[None, :] <= idx[:, None]
        scores = jnp.einsum('bhtd,bhsd->bhts', q, k) / SCALE
        scores = jnp.where(causal[None, None], scores, NEG_INF)
        attn = jax.nn.softmax(scores, axis=-1)
        mask = jnp.clip((R + z[:, :, None, None] - dist) / R, 0.0, 1.0)
        attn = attn * mask
        attn = attn / (attn.sum(axis=-1, keepdims=True) + 1e-08)
        out = jnp.einsum('bhts,bhsd->bhtd', attn, v)
        out = out.transpose(0, 2, 1, 3).reshape(B, T, D)
        return out @ Wo_w + Wo_b

    def _L0_xattn_ref(x, context, Wq, Wk, Wv, Wout, bout):
        import jax, jax.numpy as jnp
        import numpy as np
        HEADS = 8
        DIM_HEAD = 128
        ATTN_MATRIX_SCALE = 1.5
        SCALE = DIM_HEAD ** (-0.5)

        def _split_heads(t):
            b, n, _ = t.shape
            t = t.reshape(b, n, HEADS, DIM_HEAD)
            return t.transpose(2, 0, 1, 3).reshape(HEADS, b * n, DIM_HEAD)
        b, n, _ = x.shape
        qh = _split_heads(jnp.einsum('bnq,qi->bni', x, Wq))
        kh = _split_heads(jnp.einsum('bmc,ci->bmi', context, Wk))
        vh = _split_heads(jnp.einsum('bmc,ci->bmi', context, Wv))
        sim = jnp.einsum('hid,hjd->hij', qh, kh) * SCALE
        mean = jnp.mean(sim, axis=-1, keepdims=True)
        sim = (sim - mean) * ATTN_MATRIX_SCALE + mean
        attn = jax.nn.softmax(sim, axis=-1)
        out = jnp.einsum('hij,hjd->hid', attn, vh)
        out = out.reshape(HEADS, b, n, DIM_HEAD).transpose(1, 2, 0, 3)
        out = out.reshape(b, n, HEADS * DIM_HEAD)
        return jnp.einsum('bni,iq->bnq', out, Wout) + bout

    def _L0_ffn_ref(x, slot_query, d_Wq, d_Wk, d_Wv, d_Wo, d_bq, d_bk, d_bv, d_bo, c_Wq, c_Wk, c_Wv, c_Wo, c_bq, c_bk, c_bv, c_bo, e_ln_g, e_ln_b, e_W1, e_b1, e_Wg, e_bg, e_W2, e_b2):
        import jax, jax.numpy as jnp
        import numpy as np
        B, L, D = (4, 1024, 512)
        H = 16
        E = 16
        NS = 16
        S = NS // E
        F = 2048
        EPS = 1e-05

        def _layernorm(x, g, b):
            mu = jnp.mean(x, axis=-1, keepdims=True)
            var = jnp.mean(jnp.square(x - mu), axis=-1, keepdims=True)
            return (x - mu) * jax.lax.rsqrt(var + EPS) * g + b

        def _mha(q, k, v, Wq, bq, Wk, bk, Wv, bv, Wo, bo):
            Bq, Lq, Dm = q.shape
            dh = Dm // H
            qh = (q @ Wq + bq).reshape(Bq, Lq, H, dh)
            kh = (k @ Wk + bk).reshape(Bq, -1, H, dh)
            vh = (v @ Wv + bv).reshape(Bq, -1, H, dh)
            scores = jnp.einsum('bqhd,bkhd->bhqk', qh, kh) / jnp.asarray(np.sqrt(dh), q.dtype)
            attn = jax.nn.softmax(scores, axis=-1)
            out = jnp.einsum('bhqk,bkhd->bqhd', attn, vh).reshape(Bq, Lq, Dm)
            return out @ Wo + bo
        Bx = x.shape[0]
        q = jnp.broadcast_to(slot_query, (Bx, NS, D))
        o = q + _mha(q, x, x, d_Wq, d_bq, d_Wk, d_bk, d_Wv, d_bv, d_Wo, d_bo)
        os = o.reshape(Bx, E, S, D)
        h = _layernorm(os, e_ln_g[None, :, None, :], e_ln_b[None, :, None, :])
        u = jax.nn.silu(jnp.einsum('besd,edf->besf', h, e_W1) + e_b1[None, :, None, :])
        g = jax.nn.silu(jnp.einsum('besd,edf->besf', h, e_Wg) + e_bg[None, :, None, :])
        y = jnp.einsum('besf,efd->besd', u * g, e_W2) + e_b2[None, :, None, :]
        o = o + y.reshape(Bx, NS, D)
        out = _mha(x, o, o, c_Wq, c_bq, c_Wk, c_bk, c_Wv, c_bv, c_Wo, c_bo)
        return out
    x = x + _L0_attn_ref(_layernorm(x, axis=-1), L0_attn_Wq, L0_attn_Wk, L0_attn_Wv, L0_attn_Wo_w, L0_attn_Wo_b, L0_attn_span_w, L0_attn_span_b)
    x = x + _L0_xattn_ref(_layernorm(x, axis=-1), ctx_768, L0_xattn_Wq, L0_xattn_Wk, L0_xattn_Wv, L0_xattn_Wout, L0_xattn_bout)
    x = x + _L0_ffn_ref(_layernorm(x, axis=-1), L0_ffn_slot_query, L0_ffn_d_Wq, L0_ffn_d_Wk, L0_ffn_d_Wv, L0_ffn_d_Wo, L0_ffn_d_bq, L0_ffn_d_bk, L0_ffn_d_bv, L0_ffn_d_bo, L0_ffn_c_Wq, L0_ffn_c_Wk, L0_ffn_c_Wv, L0_ffn_c_Wo, L0_ffn_c_bq, L0_ffn_c_bk, L0_ffn_c_bv, L0_ffn_c_bo, L0_ffn_e_ln_g, L0_ffn_e_ln_b, L0_ffn_e_W1, L0_ffn_e_b1, L0_ffn_e_Wg, L0_ffn_e_bg, L0_ffn_e_W2, L0_ffn_e_b2)
    return x

_drawn_inputs = setup_inputs


def setup_inputs(seed=0):
    import zlib

    import numpy as np

    out = dict(_drawn_inputs(seed))
    spreads = {'L0_attn_Wo_b': (0.0, 0.1),
     'L0_attn_span_b': (0.0, 0.8),
     'L0_xattn_bout': (0.0, 0.1),
     'L0_ffn_d_bq': (0.0, 0.8),
     'L0_ffn_d_bk': (0.0, 2.0),
     'L0_ffn_d_bv': (0.0, 0.8),
     'L0_ffn_d_bo': (0.0, 0.412),
     'L0_ffn_c_bq': (0.0, 0.8),
     'L0_ffn_c_bk': (0.0, 2.0),
     'L0_ffn_c_bv': (0.0, 2.0),
     'L0_ffn_c_bo': (0.0, 2.0),
     'L0_ffn_e_ln_g': (1.0, 0.6),
     'L0_ffn_e_ln_b': (0.0, 0.8),
     'L0_ffn_e_b1': (0.0, 0.8),
     'L0_ffn_e_bg': (0.0, 0.8),
     'L0_ffn_e_b2': (0.0, 0.8)}
    factors = {'L0_attn_Wq': 8.0,
     'L0_attn_Wk': 8.0,
     'L0_attn_Wv': 4.404,
     'L0_attn_Wo_w': 4.371,
     'L0_attn_span_w': 8.0,
     'L0_ffn_slot_query': 8.0,
     'L0_ffn_d_Wq': 8.0,
     'L0_ffn_d_Wk': 8.0,
     'L0_ffn_d_Wv': 4.085,
     'L0_ffn_d_Wo': 3.718,
     'L0_ffn_c_Wq': 8.0,
     'L0_ffn_c_Wk': 8.0,
     'L0_ffn_e_W1': 8.0,
     'L0_ffn_e_Wg': 8.0,
     'L0_ffn_e_W2': 8.0}
    for name, (base, spread) in spreads.items():
        noise = np.random.default_rng([zlib.crc32(name.encode()), seed]).standard_normal(out[name].shape)
        drawn = base * np.exp(spread * noise) if base else spread * noise
        out[name] = jnp.asarray(drawn.astype(out[name].dtype))
    for name, factor in factors.items():
        out[name] = (out[name] * factor).astype(out[name].dtype)
    return out
```

```python
from contextlib import ExitStack

import concourse.bass as bass
from concourse import mybir

F32 = mybir.dt.float32
F32R = mybir.dt.float32r
BF16 = mybir.dt.bfloat16
I32 = mybir.dt.int32
ALU = mybir.AluOpType
ACT = mybir.ActivationFunctionType
AX = mybir.AxisListType

P = 128
B, T, D = 2, 2048, 512
KD = D // P
BLK = 512
NT = BLK // P
NBLK = B * T // BLK
BPB = T // BLK
EPS = 1e-5

HG, HPG, DH = 4, 4, 32
H = HG * HPG
RAMP = 256.0
NEG = -1e30


def carry(eng, carried):
    eng.sem_inc(carried, 1)


def identity(pool, tile, zeroed, ready):
    pool.memset(tile[:, :], 0.0).then_inc(zeroed, 1)
    pool.wait_ge(zeroed, 1)
    pool.affine_select(out=tile[:, :], in_=tile[:, :], compare_op=ALU.not_equal, fill=1.0,
                       base=0, pattern=[[-1, P]], channel_multiplier=1).then_inc(ready, 1)


def project_self_attention(nc, sem, x, Wq, Wk, Wv, span_w, span_b, q_hi, q_lo, k_hi, k_lo, v_sc, z_sc):
    xv = x.rearrange("b (c j p) d -> (b c) p j d", p=P, j=NT)
    OUT = 3 * NT
    HALF = OUT // 2
    with ExitStack() as ctx:
        sb = lambda name, shape, dt: ctx.enter_context(nc.sbuf_tensor(name, shape, dt))
        ps = lambda name, shape, dt: ctx.enter_context(nc.psum_tensor(name, shape, dt))
        ident = sb("A_ident", [P, P], F32)
        w = sb("A_w", [P, 3, KD, D], F32)
        spanw = sb("A_spanw", [P, KD, H], F32)
        spanb = sb("A_spanb", [P, H], F32)
        xin = sb("A_xin", [P, 2, NT, D], F32)
        stats = sb("A_stats", [P, NT, 6], F32)
        mv = sb("A_mv", [P, NT, 2], F32)
        vare = sb("A_vare", [P, NT], F32)
        std = sb("A_std", [P, NT], F32)
        rstd = sb("A_rstd", [P, NT], F32)
        xn = sb("A_xn", [P, NT, D], F32)
        xnT = sb("A_xnT", [P, 2, KD, BLK], F32)
        xsum = sb("A_xsum", [P, KD, NBLK + 1], F32)
        hi = sb("A_hi", [P, 2, 2 * KD, BLK], F32R)
        lo = sb("A_lo", [P, 2, 2 * KD, BLK], F32R)
        v = sb("A_v", [P, 2, NT, D], F32)
        xm = sb("A_xm", [P, B, KD], F32)
        xmb = sb("A_xmb", [P, B, KD, P], F32)
        zt = sb("A_z", [P, 4, B, H], F32)
        pT = ps("A_pT", [P, KD, BLK], F32)
        pO = ps("A_pO", [P, 4, BLK], F32)
        sp_carried = sem("A_sp_carried")
        dve_carried = sem("A_dve_carried")
        zeroed = sem("A_zeroed")
        ident_ready = sem("A_ident_ready")
        weights_loaded = sem("A_weights_loaded")
        x_loaded0 = sem("A_x_loaded0")
        x_loaded1 = sem("A_x_loaded1")
        dve_step = sem("A_dve_step")
        var_ready = sem("A_var_ready")
        std_ready = sem("A_std_ready")
        xn_ready = sem("A_xn_ready")
        transposed = sem("A_transposed")
        xnT_ready = sem("A_xnT_ready")
        out_ready = sem("A_out_ready")
        act_copied = sem("A_act_copied")
        lo_ready = sem("A_lo_ready")
        stored0 = sem("A_stored0")
        stored1 = sem("A_stored1")
        mean_ready = sem("A_mean_ready")
        z_dot = sem("A_z_dot")
        z_sum = sem("A_z_sum")
        z_exp = sem("A_z_exp")
        z_ready = sem("A_z_ready")
        z_stored = sem("A_z_stored")
        block = ctx.enter_context(nc.Block())
        x_loaded = (x_loaded0, x_loaded1)
        stored = (stored0, stored1)
        STORES = 5
        STEPS = NT + 2
        LOS = 2 * KD

        @block.sync
        def _(sp):
            for u in range(2):
                sp.dma_start(xin[:, u, :, :], xv[u]).then_inc(x_loaded[u], 16)
            for n, weight in enumerate((Wq, Wk, Wv)):
                sp.dma_start(w[:, n, :, :], weight.rearrange("(k p) n -> p k n", p=P)).then_inc(weights_loaded, 16)
            sp.dma_start(spanw[:, :, :], span_w.rearrange("(k p) h -> p k h", p=P)).then_inc(weights_loaded, 16)
            sp.dma_start(spanb[:, :], span_b.partition_broadcast(P)).then_inc(weights_loaded, 16)
            with sp.Fori(0, NBLK // 2) as i:
                for u in range(2):
                    blk = 2 * i + u
                    sp.wait_ge(xn_ready, blk + 1)
                    carry(sp, sp_carried)
                    sp.dma_start(xin[:, u, :, :], xv[(2 * i + 2 + u) % NBLK]).then_inc(x_loaded[u], 16)
                    sp.wait_ge(act_copied, (blk + 1) * OUT)
                    carry(sp, sp_carried)
                    sp.wait_ge(lo_ready, (blk + 2) * LOS)
                    for dst, src in ((q_hi, hi[:, u, 0:KD, :]), (q_lo, lo[:, u, 0:KD, :]),
                                     (k_hi, hi[:, u, KD:, :]), (k_lo, lo[:, u, KD:, :])):
                        sp.dma_start(dst[blk].rearrange("g p t -> p g t"), src.bitcast(F32)).then_inc(stored[u], 16)
                    sp.dma_start(v_sc[blk].rearrange("j p n -> p j n"), v[:, u, :, :]).then_inc(stored[u], 16)
            sp.wait_ge(z_ready, 4)
            sp.dma_start(z_sc, zt[0:1, 3, :, :].rearrange("a b h -> a (b h)")).then_inc(z_stored, 16)
            sp.wait_ge(z_stored, 16)
            for u in range(2):
                sp.wait_ge(stored[u], 16 * STORES * NBLK // 2)
                sp.wait_ge(x_loaded[u], 16 * (NBLK // 2 + 1))

        @block.gpsimd
        def _(pool):
            identity(pool, ident, zeroed, ident_ready)

        @block.vector
        def _(dve):
            def layer_norm(slot, n, loads):
                base = n * STEPS
                dve.wait_ge(x_loaded[slot], 16 * loads)
                for j in range(NT):
                    nc.vector.bn_stats(stats[:, j, :], xin[:, slot, j, :]).then_inc(dve_step, 1)
                dve.wait_ge(dve_step, base + NT)
                dve.wait_ge(xn_ready, n)
                carry(dve, dve_carried)
                for j in range(NT):
                    last = nc.vector.bn_aggr(mv[:, j, :], stats[:, j, :])
                last.then_inc(dve_step, 1)
                dve.wait_ge(dve_step, base + NT + 1)
                nc.vector.tensor_scalar_add(vare[:, :], mv[:, :, 1], EPS).then_inc(var_ready, 1)
                dve.wait_ge(std_ready, n + 1)
                nc.vector.reciprocal(rstd[:, :], std[:, :]).then_inc(dve_step, 1)
                dve.wait_ge(dve_step, base + NT + 2)
                dve.wait_ge(transposed, n)
                for j in range(NT):
                    last = nc.vector.tensor_scalar(xn[:, j, :], xin[:, slot, j, :], mv[:, j, 0:1],
                                                   rstd[:, j:j + 1], ALU.subtract, ALU.mult)
                last.then_inc(xn_ready, 1)

            dve.sem_inc(lo_ready, LOS)
            layer_norm(0, 0, 1)
            with dve.Fori(0, NBLK // 2) as i:
                for u in range(2):
                    blk = 2 * i + u
                    layer_norm(1 - u, blk + 1, i + 1 + u)
                    dve.wait_ge(stored[u], 16 * STORES * i)
                    for g in range(2 * KD):
                        dve.wait_ge(act_copied, blk * OUT + NT + g + 1)
                        nc.vector.tensor_tensor(lo[:, u, g, :], pO[:, (NT + g) % 4, :],
                                                hi[:, u, g, :].bitcast(F32), ALU.subtract).then_inc(lo_ready, 1)
            dve.wait_ge(xnT_ready, (NBLK + 1) * KD)
            for b in range(B):
                last = nc.vector.tensor_reduce(xm[:, b, :], xsum[:, :, b * BPB:(b + 1) * BPB], AX.X, ALU.add)
            last.then_inc(mean_ready, 1)
            dve.wait_ge(mean_ready, 1)
            nc.vector.tensor_scalar(xmb[:, :, :, :], xm[:, :, :].unsqueeze(3).broadcast_to([P, B, KD, P]), 1.0 / T, None,
                                    ALU.mult).then_inc(mean_ready, 1)
            dve.wait_ge(weights_loaded, 16 * 5)
            dve.wait_ge(z_dot, 1)
            nc.vector.tensor_tensor(zt[:, 0, :, :], pT[:, 0, 0:B * H].rearrange("p (b h) -> p b h", b=B),
                                    spanb[:, :].unsqueeze(1).broadcast_to([P, B, H]), ALU.add).then_inc(z_sum, 1)
            dve.wait_ge(z_exp, 1)
            nc.vector.tensor_scalar_add(zt[:, 2, :, :], zt[:, 1, :, :], 1.0).then_inc(z_ready, 1)
            dve.wait_ge(z_ready, 1)
            nc.vector.reciprocal(zt[:, 0, :, :], zt[:, 2, :, :]).then_inc(z_ready, 1)
            dve.wait_ge(z_ready, 2)
            nc.vector.tensor_scalar(zt[:, 3, :, :], zt[:, 0, :, :], T / RAMP, 1.0, ALU.mult, ALU.add).then_inc(z_ready, 2)

        @block.scalar
        def _(act):
            def root(n):
                act.wait_ge(var_ready, n + 1)
                nc.scalar.activation(std[:, :], vare[:, :], ACT.Sqrt).then_inc(std_ready, 1)

            def transposed_out(slot, n, done):
                act.wait_ge(transposed, n + 1)
                act.wait_ge(out_ready, done * OUT)
                for k in range(KD):
                    nc.scalar.activation(xnT[:, slot, k, :], pT[:, k, :], ACT.Copy,
                                         accum_out=xsum[:, k, bass.ds(n, 1)]).then_inc(xnT_ready, 1)

            def result_out(u, blk, g):
                act.wait_ge(out_ready, blk * OUT + g + 1)
                dst = v[:, u, g, :] if g < NT else hi[:, u, g - NT, :]
                nc.scalar.activation(dst, pO[:, g % 4, :], ACT.Copy).then_inc(act_copied, 1)

            root(0)
            transposed_out(0, 0, 0)
            with act.Fori(0, NBLK // 2) as i:
                for u in range(2):
                    blk = 2 * i + u
                    root(blk + 1)
                    act.wait_ge(stored[u], 16 * STORES * i)
                    for g in range(HALF):
                        result_out(u, blk, g)
                    transposed_out(1 - u, blk + 1, blk)
                    for g in range(HALF, OUT):
                        result_out(u, blk, g)
            act.wait_ge(z_sum, 1)
            nc.scalar.activation(zt[:, 1, :, :], zt[:, 0, :, :], ACT.Exp, scale=-1.0).then_inc(z_exp, 1)

        @block.tensor
        def _(pe):
            def transposes(n):
                pe.wait_ge(xn_ready, n + 1)
                pe.wait_ge(xnT_ready, n * KD)
                for k in range(KD):
                    for j in range(NT):
                        last = nc.tensor.transpose(pT[:, k, j * P:(j + 1) * P], xn[:, j, k * P:(k + 1) * P], ident[:, :])
                last.then_inc(transposed, 1)

            def product(u, blk, g):
                if g < 4:
                    pe.wait_ge(lo_ready, blk * LOS + LOS - 4 + g + 1)
                elif g - 4 < NT:
                    pe.wait_ge(act_copied, blk * OUT + g - 4 + 1)
                else:
                    pe.wait_ge(lo_ready, (blk + 1) * LOS + g - 4 - NT + 1)
                for k in range(KD):
                    if g < NT:
                        lhsT, rhs = xnT[:, u, k, g * P:(g + 1) * P], w[:, 2, k, :]
                    else:
                        n, m = divmod(g - NT, KD)
                        lhsT, rhs = w[:, n, k, m * P:(m + 1) * P], xnT[:, u, k, :]
                    last = nc.tensor.matmul(pO[:, g % 4, :], lhsT, rhs, start=(k == 0), stop=(k == KD - 1))
                last.then_inc(out_ready, 1)

            pe.wait_ge(ident_ready, 1)
            transposes(0)
            pe.wait_ge(weights_loaded, 16 * 5)
            with pe.Fori(0, NBLK // 2) as i:
                for u in range(2):
                    blk = 2 * i + u
                    pe.wait_ge(xnT_ready, (blk + 1) * KD)
                    for g in range(HALF):
                        product(u, blk, g)
                    transposes(blk + 1)
                    for g in range(HALF, OUT):
                        product(u, blk, g)
            pe.wait_ge(mean_ready, 2)
            for b in range(B):
                for k in range(KD):
                    last = nc.tensor.matmul(pT[:, 0, b * H:(b + 1) * H], xmb[:, b, k, :], spanw[:, k, :],
                                            start=(k == 0), stop=(k == KD - 1))
            last.then_inc(z_dot, 1)


KB = T // P
SCALE = float(DH) ** -0.5
SLOTS_E, SLOTS_EM = 4, 2
DEN_EPS = 1e-8


def attention_schedule():
    def maxima(qb):
        return [("max", qb, qt, h, c) for qt in range(NT) for h in range(HPG) for c in range(qb + 1)]

    steps = maxima(0) + [("rowmax", 0)]
    for qb in range(BPB):
        ahead = maxima(qb + 1) if qb + 1 < BPB else []
        n = NT * (qb + 1)
        share = -(-len(ahead) // (n - 1))
        for kb in range(n):
            steps.append(("score", qb, kb))
            steps += ahead[kb * share:(kb + 1) * share]
            if ahead and kb == n - 2:
                steps.append(("rowmax", qb + 1))
            if kb >= 1:
                steps.append(("mask", qb, kb - 1))
            if kb >= 2:
                steps.append(("mix", qb, kb - 2))
        steps += [("mask", qb, n - 1), ("mix", qb, n - 2), ("mix", qb, n - 1), ("out", qb)]
    return steps


def self_attention(nc, sem, q_hi, q_lo, k_hi, k_lo, v_sc, z_sc, a_sc):
    steps = attention_schedule()
    N = {kind: sum(s[0] == kind for s in steps) for kind in ("max", "rowmax", "score", "out")}
    UNITS = N["max"] + N["rowmax"]
    MROWS = 2 * HPG * NT
    with ExitStack() as ctx:
        sb = lambda name, shape, dt: ctx.enter_context(nc.sbuf_tensor(name, shape, dt))
        ps = lambda name, shape, dt: ctx.enter_context(nc.psum_tensor(name, shape, dt))
        ident = sb("B_ident", [P, P], F32)
        identb = sb("B_identb", [P, P], BF16)
        later_k = sb("B_later_k", [P, P], BF16)
        later_q = sb("B_later_q", [P, P], BF16)
        ones = sb("B_ones", [P, DH], F32)
        tiny = sb("B_tiny", [P, DH], F32)
        disti = sb("B_disti", [P, T], I32)
        dist = sb("B_dist", [P, T], F32)
        spans = sb("B_spans", [P, B * H], F32)
        span = sb("B_span", [P, HPG], F32)
        qs = sb("B_qs", [P, BPB, HPG, BLK], F32R)
        ks = sb("B_ks", [P, BPB, HPG, BLK], F32R)
        v = sb("B_v", [P, KB, P], F32)
        mask = sb("B_mask", [P, HPG, T], F32)
        mx = sb("B_mx", [P, HPG, NT, BPB], F32)
        nm = sb("B_nm", [P, HPG * NT], F32)
        mm = sb("B_mm", [P, 2, HPG * NT], F32R)
        mrow = sb("B_mrow", [MROWS, P], F32R)
        e = sb("B_e", [P, SLOTS_E, HPG, BLK], F32)
        em = sb("B_em", [P, SLOTS_EM, HPG, BLK], F32)
        rden = sb("B_rden", [P, BLK], F32)
        ao = sb("B_ao", [P, BLK], F32)
        pM = ps("B_pM", [P, 2, BLK], F32)
        pS = ps("B_pS", [P, 2, 2, BLK], F32)
        pN = ps("B_pN", [P, BLK], F32)
        pD = ps("B_pD", [P, BLK], F32)
        sp_carried = sem("B_sp_carried")
        pool_carried = sem("B_pool_carried")
        made = sem("B_made")
        const_ready = sem("B_const_ready")
        spans_loaded = sem("B_spans_loaded")
        span_ready = sem("B_span_ready")
        chunk_loaded = [sem(f"B_chunk_loaded{c}") for c in range(BPB)]
        max_ready = sem("B_max_ready")
        max_taken = sem("B_max_taken")
        neg_ready = sem("B_neg_ready")
        mrow_ready = sem("B_mrow_ready")
        mrow_loaded = sem("B_mrow_loaded")
        score_ready = sem("B_score_ready")
        exp_ready = sem("B_exp_ready")
        mask_ready = sem("B_mask_ready")
        mask_half = sem("B_mask_half")
        masked = sem("B_masked")
        mixed = sem("B_mixed")
        inverse = sem("B_inverse")
        out_ready = sem("B_out_ready")
        stored = sem("B_stored")
        block = ctx.enter_context(nc.Block())

        def width(qb, kb):
            return max(0, (kb - NT * qb) * P)

        LOADS = 16 * 7

        @block.sync
        def _(sp):
            sp.dma_start(spans[:, :], z_sc[0].partition_broadcast(P)).then_inc(spans_loaded, 16)
            with sp.Fori(0, B) as b:
                with sp.Fori(0, HG) as g:
                    it = b * HG + g

                    def rows(src, c):
                        return src[b * BPB + c, g].rearrange("(h d) t -> d h t", h=HPG)

                    order = []
                    seen = 0
                    for s in steps:
                        if s[0] == "score":
                            seen += 1
                            if s[1] < BPB - 1 and s[2] == NT * (s[1] + 1) - 1:
                                order.append(("q", s[1], seen))
                            if s[1] == BPB - 1 and s[2] % NT == NT - 1:
                                order.append(("k", s[2] // NT, seen))
                    order.append(("q", BPB - 1, seen))
                    for kind, c, n in order:
                        sp.wait_ge(score_ready, it * 2 * N["score"] + 2 * n)
                        carry(sp, sp_carried)
                        if kind == "q":
                            for r, src in ((0, q_hi), (1, q_lo), (2, q_hi)):
                                sp.dma_start(qs[r * DH:(r + 1) * DH, c, :, :].bitcast(F32), rows(src, c)).then_inc(chunk_loaded[c], 16)
                        else:
                            for r, src in ((0, k_hi), (1, k_hi), (2, k_lo)):
                                sp.dma_start(ks[r * DH:(r + 1) * DH, c, :, :].bitcast(F32), rows(src, c)).then_inc(chunk_loaded[c], 16)
                            sp.wait_ge(mixed, it * N["score"] + n)
                            carry(sp, sp_carried)
                            sp.dma_start(v[:, c * NT:(c + 1) * NT, :],
                                         v_sc[b * BPB + c, :, :, bass.ds(g * P, P)].rearrange("j p n -> p j n")
                                         ).then_inc(chunk_loaded[c], 16)

        @block.gpsimd
        def _(pool):
            step = [0]

            def then(ins):
                step[0] += 1
                ins.then_inc(made, 1)
                pool.wait_ge(made, step[0])

            for tile in (ident, identb):
                then(pool.memset(tile[:, :], 0.0))
                then(pool.affine_select(out=tile[:, :], in_=tile[:, :], compare_op=ALU.not_equal, fill=1.0,
                                        base=0, pattern=[[-1, P]], channel_multiplier=1))
            for tile in (later_k, later_q):
                then(pool.memset(tile[:, :], 0.0))
                sign = 1 if tile is later_k else -1
                then(pool.affine_select(out=tile[:, :], in_=tile[:, :], compare_op=ALU.is_ge, fill=NEG,
                                        base=0, pattern=[[-sign, P]], channel_multiplier=sign))
            then(pool.memset(ones[:, :], 1.0))
            then(pool.memset(tiny[:, :], DEN_EPS))
            then(pool.iota(disti[:, :], pattern=[[1, T]], base=0, channel_multiplier=-1))
            then(pool.tensor_copy(dist[:, :], disti[:, :]))
            for tile in (qs, ks):
                then(pool.memset(tile[3 * DH:P, :, :, :].bitcast(F32), 0.0))
            then(pool.memset(ks[3 * DH:3 * DH + 2, :, :, :].bitcast(F32), 1.0))
            pool.sem_inc(const_ready, 1)
            pool.wait_ge(spans_loaded, 16)
            with pool.Fori(0, B * HG) as it:
                for c in range(BPB):
                    if c == 0:
                        pool.wait_ge(masked, (it + 1) * N["score"])
                        carry(pool, pool_carried)
                        pool.tensor_copy(span[:, :], spans[:, bass.ds(it * HPG, HPG)]).then_inc(span_ready, 1)
                        pool.wait_ge(span_ready, it + 1)
                        carry(pool, pool_carried)
                    t = slice(c * BLK, (c + 1) * BLK)
                    for h in range(HPG):
                        last = pool.tensor_scalar(mask[:, h, t], dist[:, t], -1.0 / RAMP, span[:, h:h + 1], ALU.mult, ALU.add)
                    last.then_inc(mask_half, 1)
                    pool.wait_ge(mask_half, it * BPB + c + 1)
                    carry(pool, pool_carried)
                    pool.tensor_scalar(mask[:, :, t], mask[:, :, t], 0.0, 1.0, ALU.max, ALU.min).then_inc(mask_ready, 1)

        @block.vector
        def _(dve):
            dve.sem_inc(max_taken, 2)
            dve.sem_inc(masked, N["score"])
            with dve.Fori(0, B * HG) as it:
                unit = rm = mk = 0
                for s in steps:
                    if s[0] == "max":
                        _, qb, qt, h, c = s
                        w = BLK if c < qb else (qt + 1) * P
                        dve.wait_ge(max_ready, it * UNITS + unit + 1)
                        nc.vector.tensor_reduce(mx[:, h, qt, c:c + 1], pM[:, unit % 2, 0:w], AX.X, ALU.max).then_inc(max_taken, 1)
                        unit += 1
                    elif s[0] == "rowmax":
                        qb = s[1]
                        base = 3 * (it * N["rowmax"] + rm)
                        dve.wait_ge(max_taken, it * UNITS + unit + 2)
                        nc.vector.tensor_reduce(nm[:, :].rearrange("p (h q) -> p h q", h=HPG), mx[:, :, :, 0:qb + 1],
                                                AX.X, ALU.max, negate=True).then_inc(neg_ready, 1)
                        dve.wait_ge(neg_ready, base + 1)
                        nc.vector.tensor_copy(mm[:, 0, :], nm[:, :]).then_inc(neg_ready, 1)
                        dve.wait_ge(neg_ready, base + 2)
                        nc.vector.tensor_tensor(mm[:, 1, :], nm[:, :], mm[:, 0, :].bitcast(F32), ALU.subtract).then_inc(neg_ready, 1)
                        dve.wait_ge(max_ready, it * UNITS + unit + 1)
                        dve.wait_ge(mrow_loaded, 32 * (it * N["rowmax"] + rm))
                        nc.vector.tensor_copy(mrow[:, :], pM[0:MROWS, unit % 2, 0:P]).then_inc(max_taken, 1)
                        unit += 1
                        rm += 1
                    elif s[0] == "mask":
                        _, qb, kb = s
                        w0 = width(qb, kb)
                        u0 = qb * BLK - kb * P + w0
                        dve.wait_ge(exp_ready, it * 2 * N["score"] + 2 * (mk + 1) + 2)
                        if kb == 0:
                            dve.wait_ge(mask_ready, it * BPB + qb + 1)
                        dve.wait_ge(mixed, it * N["score"] + N["score"] + mk + 1 - SLOTS_EM)
                        nc.vector.tensor_tensor(em[:, mk % SLOTS_EM, :, w0:], e[:, mk % SLOTS_E, :, w0:],
                                                mask[:, :, u0:u0 + BLK - w0], ALU.mult).then_inc(masked, 1)
                        mk += 1
                    elif s[0] == "out":
                        qb = s[1]
                        n = it * N["out"] + qb
                        dve.wait_ge(mixed, it * N["score"] + N["score"] + mk)
                        nc.vector.reciprocal(rden[:, :], pD[:, :]).then_inc(inverse, 1)
                        dve.wait_ge(inverse, n + 1)
                        dve.wait_ge(stored, 16 * n)
                        nc.vector.tensor_tensor(ao[:, :], pN[:, :], rden[:, :], ALU.mult).then_inc(out_ready, 1)

        @block.scalar
        def _(act):
            act.wait_ge(const_ready, 1)
            act.sem_inc(exp_ready, 2)
            with act.Fori(0, B) as b:
                with act.Fori(0, HG) as g:
                    it = b * HG + g
                    sc = rm = 0
                    unit = 0
                    for s in steps:
                        if s[0] == "max":
                            unit += 1
                        if s[0] == "rowmax":
                            qb = s[1]
                            unit += 1
                            act.wait_ge(max_taken, it * UNITS + unit + 2)
                            for part in range(2):
                                act.dma_start(qs[3 * DH + part:3 * DH + part + 1, qb, :, :].bitcast(F32),
                                              mrow[part * HPG * NT:(part + 1) * HPG * NT, :].bitcast(F32)
                                              ).then_inc(mrow_loaded, 16)
                            rm += 1
                        elif s[0] == "score":
                            _, qb, kb = s
                            w0 = width(qb, kb)
                            act.wait_ge(mixed, it * N["score"] + N["score"] + sc + 1 - SLOTS_E)
                            for hp in range(2):
                                act.wait_ge(score_ready, it * 2 * N["score"] + 2 * N["score"] + 2 * sc + hp + 1)
                                nc.scalar.activation(e[:, sc % SLOTS_E, 2 * hp:2 * hp + 2, w0:], pS[:, hp, :, w0:],
                                                     ACT.Exp, scale=SCALE).then_inc(exp_ready, 1)
                            sc += 1
                        elif s[0] == "out":
                            qb = s[1]
                            act.wait_ge(out_ready, it * N["out"] + qb + 1)
                            act.dma_start(a_sc[b * BPB + qb, g], ao[:, :]).then_inc(stored, 16)
            act.wait_ge(stored, 16 * B * HG * N["out"])

        @block.tensor
        def _(pe):
            pe.wait_ge(const_ready, 1)
            pe.sem_inc(score_ready, 2 * N["score"])
            pe.sem_inc(mixed, N["score"])
            with pe.Fori(0, B * HG) as it:
                unit = rm = sc = mk = 0
                for s in steps:
                    if s[0] == "max":
                        _, qb, qt, h, c = s
                        w = BLK if c < qb else (qt + 1) * P
                        if (qt, h, c) == (0, 0, 0):
                            pe.wait_ge(chunk_loaded[qb], LOADS * (it + 1))
                        pe.wait_ge(max_taken, it * UNITS + unit + 1)
                        last = nc.tensor.matmul(pM[:, unit % 2, 0:w], qs[0:3 * DH, qb, h, qt * P:(qt + 1) * P], ks[0:3 * DH, c, h, 0:w],
                                                start=True, stop=(c < qb))
                        if c == qb:
                            last = nc.tensor.matmul(pM[:, unit % 2, w - P:w], identb[:, :], later_k[:, :], start=False, stop=True)
                        last.then_inc(max_ready, 1)
                        unit += 1
                    elif s[0] == "rowmax":
                        pe.wait_ge(max_taken, it * UNITS + unit + 1)
                        pe.wait_ge(neg_ready, 3 * (it * N["rowmax"] + rm + 1))
                        nc.tensor.transpose(pM[0:MROWS, unit % 2, 0:P], mm[:, :, :].bitcast(F32).rearrange("p a b -> p (a b)"),
                                            ident[:, :]).then_inc(max_ready, 1)
                        unit += 1
                        rm += 1
                    elif s[0] == "score":
                        _, qb, kb = s
                        w0 = width(qb, kb)
                        if kb == 0:
                            pe.wait_ge(mrow_loaded, 32 * (it * N["rowmax"] + qb + 1))
                        for hp in range(2):
                            pe.wait_ge(exp_ready, it * 2 * N["score"] + 2 * sc + hp + 1)
                            for j in range(2):
                                h = 2 * hp + j
                                last = nc.tensor.matmul(pS[:, hp, j, w0:], ks[:, kb // NT, h, kb % NT * P:(kb % NT + 1) * P],
                                                        qs[:, qb, h, w0:], start=True, stop=(kb < NT * qb))
                                if kb >= NT * qb:
                                    last = nc.tensor.matmul(pS[:, hp, j, w0:w0 + P], identb[:, :], later_q[:, :],
                                                            start=False, stop=True)
                            last.then_inc(score_ready, 1)
                        sc += 1
                    elif s[0] == "mix":
                        _, qb, kb = s
                        w0 = width(qb, kb)
                        first, final = kb == 0, kb == NT * (qb + 1) - 1
                        if first:
                            pe.wait_ge(out_ready, it * N["out"] + qb)
                        pe.wait_ge(masked, it * N["score"] + N["score"] + mk + 1)
                        for h in range(HPG):
                            nc.tensor.matmul(pN[h * DH:(h + 1) * DH, w0:], v[:, kb, h * DH:(h + 1) * DH],
                                             em[:, mk % SLOTS_EM, h, w0:], start=first, stop=final, tile_position=(0, h * DH))
                        for h in range(HPG):
                            nc.tensor.matmul(pD[h * DH:(h + 1) * DH, w0:], ones[:, :],
                                             em[:, mk % SLOTS_EM, h, w0:], start=first, stop=False, tile_position=(0, h * DH))
                        for h in range(HPG):
                            last = nc.tensor.matmul(pD[h * DH:(h + 1) * DH, w0:], tiny[:, :],
                                                    e[:, mk % SLOTS_E, h, w0:], start=False, stop=final, tile_position=(0, h * DH))
                        last.then_inc(mixed, 1)
                        mk += 1


XH, XDH = 8, 128
CL, CD = 77, 384
KC = CD // P
KEYS = B * CL
HB = BLK // KEYS
GROUPS = [(h, min(h + HB, XH)) for h in range(0, XH, HB)]
XK = XH * KEYS
XT = -(-XK // P)
XSCALE = float(XDH) ** -0.5
SHARPEN = 1.5
NS = 16
HS = H * NS
MS = HS // P
TILES = B * T // P


def fold_weights(nc, sem, spare, ctx768, Wq, Wk, Wv, Wout, slot_query, d_Wq, d_Wk, d_bq, d_bk, vw_sc, wkx, vwo, dqk, dqb):
    with ExitStack() as ctx:
        sb = lambda name, shape, dt: ctx.enter_context(nc.sbuf_tensor(name, shape, dt))
        wq = spare[:, 0, :].rearrange("p (k n) -> p k n", k=KD)
        wo = spare[:, 1, :].rearrange("p (h n) -> p h n", h=XH)
        wqT = spare[:, 2, :].rearrange("p (h n) -> p h n", h=XH)
        slot_weights = spare[:, 3, :].rearrange("p (w k n) -> p w k n", w=2, n=D)
        dwq, dwk = slot_weights[:, 0, :, :], slot_weights[:, 1, :, :]
        ident = sb("W_ident", [P, P], F32)
        cx = sb("W_cx", [CL, B, CD], F32)
        wk = sb("W_wk", [P, KC, XH * XDH], F32)
        wv = sb("W_wv", [P, KC, XH * XDH], F32)
        sq = sb("W_sq", [NS, D], F32)
        dbq = sb("W_dbq", [P, KD], F32)
        dbk = sb("W_dbk", [P, KD], F32)
        cT = sb("W_cT", [P, KC, KEYS], F32)
        kT = sb("W_kT", [P, XH, KEYS], F32)
        ksum = sb("W_ksum", [P, XH], F32)
        kmean = sb("W_kmean", [P, XH], F32)
        kS = sb("W_kS", [P, XH, KEYS], F32)
        vT = sb("W_vT", [P, XH, KEYS], F32)
        vw = sb("W_vw", [CL, XH, B, D], F32)
        sqT = sb("W_sqT", [P, KD, NS], F32)
        sqh = sb("W_sqh", [P, KD, NS], F32)
        qbd = sb("W_qbd", [P, KD, HPG, NS], F32)
        dwkT = sb("W_dwkT", [P, KD, D], F32)
        bank = [ctx.enter_context(nc.psum_tensor(f"W_bank{n}", [P, BLK], F32)) for n in range(8)]
        zeroed = sem("W_zeroed")
        ident_ready = sem("W_ident_ready")
        loaded = [sem(f"W_loaded{n}") for n in range(6)]
        made = sem("W_made")
        taken = sem("W_taken")
        step = sem("W_step")
        bd_zero = sem("W_bd_zero")
        vw_stored = sem("W_vw_stored")
        vwo_loaded = sem("W_vwo_loaded")
        block = ctx.enter_context(nc.Block())

        names = (["cT"] + [("kT", g) for g in range(len(GROUPS))] + [("vT", g) for g in range(len(GROUPS))]
                 + [("wqT", h) for h in range(XH)] + [("wkx", k, g) for k in range(KD) for g in range(len(GROUPS))]
                 + [("vw", h, b) for h in range(XH) for b in range(B)] + ["sqT", "sqh"]
                 + [("dwkT", m) for m in range(KD)] + [("dqk", k) for k in range(0, KD, 2)] + ["dqb"])
        nth = {name: n for n, name in enumerate(names)}

        @block.sync
        def _(sp):
            sp.dma_start(cx[:, :, :], ctx768.rearrange("b l c -> l b c")).then_inc(loaded[0], 16)
            sp.dma_start(wk[:, :, :], Wk.rearrange("(k p) n -> p k n", p=P)).then_inc(loaded[1], 16)
            sp.dma_start(wv[:, :, :], Wv.rearrange("(k p) n -> p k n", p=P)).then_inc(loaded[1], 16)
            sp.dma_start(wq[:, :, :], Wq.rearrange("(k p) n -> p k n", p=P)).then_inc(loaded[2], 16)
            sp.dma_start(wo[:, :, :], Wout.rearrange("(h p) n -> p h n", p=P)).then_inc(loaded[3], 16)
            sp.dma_start(sq[:, :], slot_query[0]).then_inc(loaded[4], 16)
            for dst, src in ((dbq, d_bq), (dbk, d_bk)):
                sp.dma_start(dst[:, :], src.rearrange("(k p) -> p k", p=P), allow_slow_non_contiguous=True).then_inc(loaded[4], 16)
            sp.dma_start(dwq[:, :, :], d_Wq.rearrange("(k p) n -> p k n", p=P)).then_inc(loaded[5], 16)
            sp.dma_start(dwk[:, :, :], d_Wk.rearrange("(k p) n -> p k n", p=P)).then_inc(loaded[5], 16)
            sp.wait_ge(taken, nth[("vw", XH - 1, B - 1)] + 1)
            sp.dma_start(vw_sc.rearrange("(h b l) n -> l h b n", h=XH, b=B), vw[:, :, :, :]).then_inc(vw_stored, 16)
            sp.wait_ge(vw_stored, 16)
            full = XK // P
            sp.dma_start(vwo[:, 0:full, :], vw_sc[0:full * P, :].rearrange("(t p) n -> p t n", p=P)).then_inc(vwo_loaded, 16)
            sp.dma_start(vwo[0:XK - full * P, full, :], vw_sc[full * P:XK, :]).then_inc(vwo_loaded, 16)
            sp.wait_ge(vwo_loaded, 32)

        @block.gpsimd
        def _(pool):
            identity(pool, ident, zeroed, ident_ready)
            pool.memset(qbd[:, :, :, :], 0.0).then_inc(bd_zero, 1)

        @block.vector
        def _(dve):
            def take(name, dst, src):
                dve.wait_ge(made, nth[name] + 1)
                nc.vector.tensor_copy(dst, src).then_inc(taken, 1)

            take("cT", cT[:, :, :], bank[0][:, 0:KC * KEYS].rearrange("p (k c) -> p k c", k=KC))
            for kind, dst in (("kT", kT), ("vT", vT)):
                for g, (h0, h1) in enumerate(GROUPS):
                    take((kind, g), dst[:, h0:h1, :],
                         bank[nth[(kind, g)] % 8][:, 0:(h1 - h0) * KEYS].rearrange("p (h c) -> p h c", c=KEYS))
            dve.wait_ge(taken, nth[("kT", len(GROUPS) - 1)] + 1)
            nc.vector.tensor_reduce(ksum[:, :], kT[:, :, :], AX.X, ALU.add).then_inc(step, 1)
            dve.wait_ge(step, 1)
            nc.vector.tensor_scalar(kmean[:, :], ksum[:, :], (1.0 - SHARPEN) / KEYS, None, ALU.mult).then_inc(step, 1)
            dve.wait_ge(step, 2)
            for h in range(XH):
                last = nc.vector.tensor_scalar(kS[:, h, :], kT[:, h, :], SHARPEN, kmean[:, h:h + 1], ALU.mult, ALU.add)
            last.then_inc(step, 1)
            for h in range(XH):
                take(("wqT", h), wqT[:, h, :], bank[nth[("wqT", h)] % 8][:, :])
            for k in range(KD):
                for g, (h0, h1) in enumerate(GROUPS):
                    take(("wkx", k, g), wkx[:, k, h0 * KEYS:h1 * KEYS], bank[nth[("wkx", k, g)] % 8][:, 0:(h1 - h0) * KEYS])
            for h in range(XH):
                for b in range(B):
                    take(("vw", h, b), vw[:, h, b, :], bank[nth[("vw", h, b)] % 8][0:CL, :])
            take("sqT", sqT[:, :, :], bank[nth["sqT"] % 8][:, 0:KD * NS].rearrange("p (k s) -> p k s", k=KD))
            dve.wait_ge(loaded[4], 48)
            dve.wait_ge(made, nth["sqh"] + 1)
            nc.vector.tensor_tensor(sqh[:, :, :], bank[nth["sqh"] % 8][:, 0:KD * NS].rearrange("p (k s) -> p k s", k=KD),
                                    dbq[:, :].unsqueeze(2).broadcast_to([P, KD, NS]), ALU.add).then_inc(taken, 1)
            dve.wait_ge(taken, nth["sqh"] + 1)
            dve.wait_ge(bd_zero, 1)
            for j in range(HPG):
                r = slice(j * DH, (j + 1) * DH)
                last = nc.vector.tensor_copy(qbd[r, :, j, :], sqh[r, :, :])
            last.then_inc(step, 1)
            for m in range(KD):
                take(("dwkT", m), dwkT[:, m, :], bank[nth[("dwkT", m)] % 8][:, :])
            for k in range(0, KD, 2):
                take(("dqk", k), dqk[:, k:k + 2, :], bank[nth[("dqk", k)] % 8][:, :].rearrange("p (k n) -> p k n", k=2))
            take("dqb", dqb[:, :], bank[nth["dqb"] % 8][:, 0:MS])

        @block.tensor
        def _(pe):
            def into(name):
                n = nth[name]
                if n >= 8:
                    pe.wait_ge(taken, n - 7)
                return bank[n % 8]

            pe.wait_ge(ident_ready, 1)
            pe.wait_ge(loaded[0], 16)
            o = into("cT")
            for k in range(KC):
                for b in range(B):
                    c0 = k * KEYS + b * CL
                    last = nc.tensor.transpose(o[:, c0:c0 + CL], cx[:, b, k * P:(k + 1) * P], ident[0:CL, 0:CL])
            last.then_inc(made, 1)
            pe.wait_ge(taken, nth["cT"] + 1)
            pe.wait_ge(loaded[1], 32)
            for kind, weight in (("kT", wk), ("vT", wv)):
                for g, (h0, h1) in enumerate(GROUPS):
                    o = into((kind, g))
                    for h in range(h0, h1):
                        for k in range(KC):
                            last = nc.tensor.matmul(o[:, (h - h0) * KEYS:(h - h0 + 1) * KEYS], weight[:, k, h * XDH:(h + 1) * XDH],
                                                    cT[:, k, :], start=(k == 0), stop=(k == KC - 1))
                    last.then_inc(made, 1)
            pe.wait_ge(loaded[2], 16)
            for h in range(XH):
                o = into(("wqT", h))
                for k in range(KD):
                    last = nc.tensor.transpose(o[:, k * P:(k + 1) * P], wq[:, k, h * XDH:(h + 1) * XDH], ident[:, :])
                last.then_inc(made, 1)
            pe.wait_ge(taken, nth[("wqT", XH - 1)] + 1)
            pe.wait_ge(step, 3)
            for k in range(KD):
                for g, (h0, h1) in enumerate(GROUPS):
                    o = into(("wkx", k, g))
                    for h in range(h0, h1):
                        last = nc.tensor.matmul(o[:, (h - h0) * KEYS:(h - h0 + 1) * KEYS], wqT[:, h, k * P:(k + 1) * P],
                                                kS[:, h, :], start=True, stop=True)
                    last.then_inc(made, 1)
            pe.wait_ge(loaded[3], 16)
            for h in range(XH):
                for b in range(B):
                    o = into(("vw", h, b))
                    nc.tensor.matmul(o[0:CL, :], vT[:, h, b * CL:(b + 1) * CL], wo[:, h, :], start=True, stop=True
                                     ).then_inc(made, 1)
            pe.wait_ge(loaded[4], 48)
            o = into("sqT")
            for k in range(KD):
                last = nc.tensor.transpose(o[:, k * NS:(k + 1) * NS], sq[:, k * P:(k + 1) * P], ident[0:NS, 0:NS])
            last.then_inc(made, 1)
            pe.wait_ge(taken, nth["sqT"] + 1)
            pe.wait_ge(loaded[5], 32)
            o = into("sqh")
            for m in range(KD):
                for k in range(KD):
                    last = nc.tensor.matmul(o[:, m * NS:(m + 1) * NS], dwq[:, k, m * P:(m + 1) * P], sqT[:, k, :],
                                            start=(k == 0), stop=(k == KD - 1))
            last.then_inc(made, 1)
            for m in range(KD):
                o = into(("dwkT", m))
                for k in range(KD):
                    last = nc.tensor.transpose(o[:, k * P:(k + 1) * P], dwk[:, k, m * P:(m + 1) * P], ident[:, :])
                last.then_inc(made, 1)
            pe.wait_ge(taken, nth[("dwkT", KD - 1)] + 1)
            pe.wait_ge(step, 4)
            for k in range(0, KD, 2):
                o = into(("dqk", k))
                for kk in range(2):
                    for m in range(KD):
                        c0 = kk * HS + m * HPG * NS
                        last = nc.tensor.matmul(o[:, c0:c0 + HPG * NS], dwkT[:, m, (k + kk) * P:(k + kk + 1) * P],
                                                qbd[:, m, :, :].rearrange("p j s -> p (j s)"), start=True, stop=True)
                last.then_inc(made, 1)
            o = into("dqb")
            for m in range(KD):
                r = m % 2 * HPG * NS
                last = nc.tensor.matmul(o[r:r + HPG * NS, m // 2:m // 2 + 1], qbd[:, m, :, :].rearrange("p j s -> p (j s)"),
                                        dbk[:, m:m + 1], start=True, stop=True, tile_position=(0, r))
            last.then_inc(made, 1)


LAG_B, LAG_C, LAG_D = 1, 2, 3


def at_least(eng, sem, value):
    if not (isinstance(value, int) and value <= 0):
        eng.wait_ge(sem, value)


def ticks(eng, body):
    there = lambda t: 0 <= t < TILES
    for n in range(NT):
        body(0, n, there)
    with eng.Fori(1, TILES // NT) as i:
        for j in range(NT):
            body(i, j, lambda t: True)
    for n in range(TILES, TILES + LAG_D):
        body(n // NT, n % NT, there)


def upto(value, most=TILES):
    return min(value, most) if isinstance(value, int) else value


def cross_attention(nc, sem, x, a_sc, Wo, Wo_b, bout, wkx, vwo, dqk, dqb, x2_sc, xn_sc, xT_sc, s_sc):
    xv = x.rearrange("b (t p) d -> (b t) p d", p=P)
    with ExitStack() as ctx:
        sb = lambda name, shape, dt: ctx.enter_context(nc.sbuf_tensor(name, shape, dt))
        ps = lambda name, shape, dt: ctx.enter_context(nc.psum_tensor(name, shape, dt))
        ident = sb("C_ident", [P, P], F32)
        power = sb("C_power", [P, 1], F32)
        wo = sb("C_wo", [P, HG, D], F32)
        wob = sb("C_wob", [P, D], F32)
        bob = sb("C_bob", [P, D], F32)
        xin = sb("C_xin", [P, NT, D], F32)
        aT = sb("C_aT", [P, NT, HG, P], F32)
        x1 = sb("C_x1", [P, 2, D], F32)
        x1b = sb("C_x1b", [P, NT, D], F32)
        stats = [sb(f"C_stats{s}", [P, 6], F32) for s in range(2)]
        mv = [sb(f"C_mv{s}", [P, 2], F32) for s in range(2)]
        vare = [sb(f"C_vare{s}", [P, 1], F32) for s in range(2)]
        rstd = [sb(f"C_rstd{s}", [P, 1], F32) for s in range(2)]
        xn2 = sb("C_xn2", [P, D], F32)
        xn2T = sb("C_xn2T", [P, 2, KD, P], F32)
        mx = sb("C_mx", [P, XH], F32)
        nmx = sb("C_nmx", [P, XH], F32)
        total = sb("C_total", [P, 2, XH], F32)
        inv = sb("C_inv", [P, XH], F32)
        prob = sb("C_prob", [P, 2, XH, KEYS], F32)
        probT = sb("C_probT", [P, 2, XT, P], F32)
        x2 = sb("C_x2", [P, 2, D], F32)
        xn3 = sb("C_xn3", [P, 2, D], F32)
        xn3T = sb("C_xn3T", [P, 2, KD, P], F32)
        pA = ps("C_pA", [P, BLK], F32)
        pX = ps("C_pX", [P, BLK], F32)
        pS = ps("C_pS", [P, len(GROUPS), BLK], F32)
        pP = ps("C_pP", [P, 2, BLK], F32)
        pO = ps("C_pO", [P, BLK], F32)
        sp_carried = sem("C_sp_carried")
        dve_carried = sem("C_dve_carried")
        zeroed = sem("C_zeroed")
        ident_ready = sem("C_ident_ready")
        weights_loaded = sem("C_weights_loaded")
        tile_loaded = [sem(f"C_tile_loaded{s}") for s in range(NT)]
        xb_ready = sem("C_xb_ready")
        projected = sem("C_projected")
        x1_ready = sem("C_x1_ready")
        x1b_ready = sem("C_x1b_ready")
        ln_step = [sem(f"C_ln_step{s}") for s in range(2)]
        var_ready = [sem(f"C_var_ready{s}") for s in range(2)]
        rstd_ready = [sem(f"C_rstd_ready{s}") for s in range(2)]
        xn_ready = [sem(f"C_xn_ready{s}") for s in range(2)]
        turned = [sem(f"C_turned{s}") for s in range(2)]
        xT_ready = [sem(f"C_xT_ready{s}") for s in range(2)]
        score_ready = sem("C_score_ready")
        max_step = sem("C_max_step")
        nmx_ready = sem("C_nmx_ready")
        exp_ready = sem("C_exp_ready")
        inv_ready = sem("C_inv_ready")
        prob_ready = sem("C_prob_ready")
        prob_turned = sem("C_prob_turned")
        probT_ready = sem("C_probT_ready")
        out_ready = sem("C_out_ready")
        x2_ready = sem("C_x2_ready")
        slot_ready = sem("C_slot_ready")
        slot_taken = sem("C_slot_taken")
        stored = [sem(f"C_stored{s}") for s in range(2)]
        storedT = [sem(f"C_storedT{s}") for s in range(2)]
        block = ctx.enter_context(nc.Block())

        TP = [range(k, min(k + NT, XT)) for k in range(0, XT, NT)]
        NP = len(TP)
        WAIT_W = 16 * 3

        @block.sync
        def _(sp):
            def load_at(blk, j):
                blk = blk % NBLK
                sp.dma_start(xin[:, j, :], xv[blk * NT + j]).then_inc(tile_loaded[j], 16)
                sp.dma_start(aT[:, j, :, :], a_sc[blk, :, :, j * P:(j + 1) * P].rearrange("g p t -> p g t")
                             ).then_inc(tile_loaded[j], 16)

            load_at(0, 0)
            sp.dma_start(wob[:, :], Wo_b.partition_broadcast(P)).then_inc(weights_loaded, 16)
            sp.dma_start(bob[:, :], bout.partition_broadcast(P)).then_inc(weights_loaded, 16)
            sp.dma_start(wo[:, :, :], Wo.rearrange("(g p) n -> p g n", p=P)).then_inc(weights_loaded, 16)
            for j in range(1, NT - 1):
                load_at(0, j)

            def tick(i, j, valid):
                n = NT * i + j
                a, c, d = n, n - LAG_C, n - LAG_D
                if valid(a):
                    at_least(sp, x1_ready, a)
                    carry(sp, sp_carried)
                    load_at(i if j == 0 else i + 1, (j + NT - 1) % NT)
                if valid(c):
                    sp.wait_ge(xn_ready[1], c + 1)
                    sp.dma_start(x2_sc[c], x2[:, j % 2, :]).then_inc(stored[j % 2], 16)
                    sp.dma_start(xn_sc[c], xn3[:, j % 2, :]).then_inc(stored[j % 2], 16)
                if valid(d):
                    s = (j + 1) % 2
                    sp.wait_ge(xT_ready[1], d + 1)
                    sp.dma_start(xT_sc[d], xn3T[:, s, :, :]).then_inc(storedT[s], 16)

            ticks(sp, tick)
            for s in range(2):
                sp.wait_ge(stored[s], 32 * TILES // 2)
                sp.wait_ge(storedT[s], 16 * TILES // 2)
            for j in range(NT - 1):
                sp.wait_ge(tile_loaded[j], 32 * (NBLK + 1))

        @block.gpsimd
        def _(pool):
            identity(pool, ident, zeroed, ident_ready)
            pool.memset(power[:, :], -0.5).then_inc(zeroed, 1)
            pool.wait_ge(zeroed, 2)
            pool.wait_ge(weights_loaded, WAIT_W)

            def root(s, t):
                pool.wait_ge(var_ready[s], t + 1)
                nc.gpsimd.tensor_tensor(rstd[s][:, :], vare[s][:, :], power[:, :], ALU.pow).then_inc(rstd_ready[s], 1)

            def tick(i, j, valid):
                n = NT * i + j
                a, b, c = n, n - LAG_B, n - LAG_C
                if valid(a):
                    pool.wait_ge(tile_loaded[j], 32 * (i + 1))
                    nc.gpsimd.tensor_tensor(xin[:, j, :], xin[:, j, :], wob[:, :], ALU.add).then_inc(xb_ready, 1)
                    root(0, a)
                    pool.wait_ge(x1_ready, a + 1)
                    nc.gpsimd.tensor_tensor(x1b[:, j, :], x1[:, j % 2, :], bob[:, :], ALU.add).then_inc(x1b_ready, 1)
                if valid(b):
                    s = (j + 1) % 2
                    pool.wait_ge(inv_ready, b + 1)
                    nc.gpsimd.tensor_tensor(prob[:, s, :, :], prob[:, s, :, :],
                                            inv[:, :].unsqueeze(2).broadcast_to([P, XH, KEYS]), ALU.mult).then_inc(prob_ready, 1)
                if valid(c):
                    root(1, c)

            ticks(pool, tick)

        @block.vector
        def _(dve):
            def layer_norm(s, t, src, dst, free_dst):
                nc.vector.bn_stats(stats[s][:, :], src).then_inc(ln_step[s], 1)
                dve.wait_ge(ln_step[s], 2 * t + 1)
                at_least(dve, xn_ready[s], t)
                carry(dve, dve_carried)
                nc.vector.bn_aggr(mv[s][:, :], stats[s][:, :]).then_inc(ln_step[s], 1)
                dve.wait_ge(ln_step[s], 2 * t + 2)
                nc.vector.tensor_scalar_add(vare[s][:, :], mv[s][:, 1:2], EPS).then_inc(var_ready[s], 1)
                dve.wait_ge(rstd_ready[s], t + 1)
                free_dst()
                nc.vector.tensor_scalar(dst, src, mv[s][:, 0:1], rstd[s][:, 0:1], ALU.subtract, ALU.mult
                                        ).then_inc(xn_ready[s], 1)

            def tick(i, j, valid):
                n = NT * i + j
                a, b, c = n, n - LAG_B, n - LAG_C
                if valid(b):
                    dve.wait_ge(score_ready, b + 1)
                    for g, (h0, h1) in enumerate(GROUPS):
                        last = nc.vector.tensor_reduce(mx[:, h0:h1], pS[:, g, 0:(h1 - h0) * KEYS].rearrange("p (h c) -> p h c", c=KEYS),
                                                       AX.X, ALU.max)
                    last.then_inc(max_step, 1)
                    dve.wait_ge(max_step, b + 1)
                    at_least(dve, exp_ready, b)
                    nc.vector.tensor_scalar(nmx[:, :], mx[:, :], -XSCALE, None, ALU.mult).then_inc(nmx_ready, 1)
                if valid(a):
                    dve.wait_ge(projected, a + 1)
                    dve.wait_ge(xb_ready, a + 1)
                    at_least(dve, x1b_ready, a - 1)
                    nc.vector.tensor_tensor(x1[:, j % 2, :], pA[:, :], xin[:, j, :], ALU.add).then_inc(x1_ready, 1)
                    dve.wait_ge(x1_ready, a + 1)
                    layer_norm(0, a, x1[:, j % 2, :], xn2[:, :], lambda: at_least(dve, turned[0], a))
                if valid(b):
                    s = (j + 1) % 2
                    dve.wait_ge(exp_ready, b + 1)
                    at_least(dve, prob_ready, b)
                    nc.vector.reciprocal(inv[:, :], total[:, s, :]).then_inc(inv_ready, 1)
                if valid(c):
                    s = j % 2
                    dve.wait_ge(out_ready, c + 1)
                    dve.wait_ge(x1b_ready, c + 1)
                    if not isinstance(c, int) or c >= 2:
                        dve.wait_ge(stored[s], 32 * (2 * i + j // 2 - 1))
                    nc.vector.tensor_tensor(x2[:, s, :], pO[:, :], x1b[:, (j + NT - LAG_C) % NT, :], ALU.add).then_inc(x2_ready, 1)
                    dve.wait_ge(x2_ready, c + 1)
                    layer_norm(1, c, x2[:, s, :], xn3[:, s, :], lambda: at_least(dve, turned[1], c - 1))

            ticks(dve, tick)

        @block.scalar
        def _(act):
            def probT_out(c, j, g):
                act.wait_ge(prob_turned, NP * c + g + 1)
                if g == 0:
                    at_least(act, out_ready, c - 1)
                n = len(TP[g])
                for rows, cols in ((P, [k for k in TP[g] if (k + 1) * P <= XK]), (XK % P, [k for k in TP[g] if (k + 1) * P > XK])):
                    if cols:
                        k0, kn = cols[0], cols[-1] + 1
                        last = nc.scalar.activation(probT[0:rows, j % 2, k0:kn, :],
                                                    pP[0:rows, (j * NP + g) % 2, (k0 - TP[g][0]) * P:(kn - TP[g][0]) * P]
                                                    .rearrange("p (k q) -> p k q", q=P), ACT.Copy)
                last.then_inc(probT_ready, 1)

            act.wait_ge(weights_loaded, WAIT_W)

            def tick(i, j, valid):
                n = NT * i + j
                a, b, c, d = n, n - LAG_B, n - LAG_C, n - LAG_D
                if valid(c):
                    probT_out(c, j, 0)
                    probT_out(c, j, 1)
                if valid(d):
                    s = (j + 1) % 2
                    act.wait_ge(turned[1], d + 1)
                    if not isinstance(d, int) or d >= 2:
                        act.wait_ge(storedT[s], 16 * (2 * i + (j + 1) // 2 - 2))
                        act.wait_ge(slot_ready, d - 1)
                    nc.scalar.activation(xn3T[:, s, :, :], pX[:, :].rearrange("p (k q) -> p k q", k=KD), ACT.Copy
                                         ).then_inc(xT_ready[1], 1)
                if valid(b):
                    s = (j + 1) % 2
                    act.wait_ge(nmx_ready, b + 1)
                    at_least(act, prob_turned, NP * (b - 1))
                    for h in range(XH):
                        last = nc.scalar.activation(prob[:, s, h, :], pS[:, h // HB, h % HB * KEYS:(h % HB + 1) * KEYS], ACT.Exp,
                                                    bias=nmx[:, h:h + 1], scale=XSCALE, accum_out=total[:, s, h:h + 1])
                    last.then_inc(exp_ready, 1)
                if valid(c):
                    probT_out(c, j, 2)
                if valid(a):
                    act.wait_ge(turned[0], a + 1)
                    at_least(act, score_ready, a - 1)
                    nc.scalar.activation(xn2T[:, j % 2, :, :], pX[:, :].rearrange("p (k q) -> p k q", k=KD), ACT.Copy
                                         ).then_inc(xT_ready[0], 1)
                if valid(d):
                    act.wait_ge(slot_ready, d + 1)
                    for m in range(MS):
                        last = nc.scalar.activation(s_sc[:, m, bass.ds(d * P, P)], pO[:, m * P:(m + 1) * P], ACT.Identity,
                                                    bias=dqb[:, m:m + 1])
                    last.then_inc(slot_taken, 1)

            ticks(act, tick)

        @block.tensor
        def _(pe):
            def turn(s, t, src):
                for k in range(KD):
                    last = nc.tensor.transpose(pX[:, k * P:(k + 1) * P], src[:, k * P:(k + 1) * P], ident[:, :])
                last.then_inc(turned[s], 1)

            def turn_prob(c, j, g):
                at_least(pe, probT_ready, NP * c + g - 1)
                if g == 0:
                    pe.wait_ge(prob_ready, c + 1)
                flat = prob[:, j % 2, :, :].rearrange("p h c -> p (h c)")
                for k in TP[g]:
                    w = min(P, XK - k * P)
                    last = nc.tensor.transpose(pP[0:w, (j * NP + g) % 2, (k - TP[g][0]) * P:(k - TP[g][0] + 1) * P],
                                               flat[:, k * P:k * P + w], ident[:, :])
                last.then_inc(prob_turned, 1)

            def outputs(c, j, g):
                pe.wait_ge(probT_ready, NP * c + g + 1)
                for k in TP[g]:
                    w = min(P, XK - k * P)
                    last = nc.tensor.matmul(pO[:, :], probT[0:w, j % 2, k, :], vwo[0:w, k, :], start=(k == 0), stop=(k == XT - 1))
                if g == NP - 1:
                    last.then_inc(out_ready, 1)

            pe.wait_ge(ident_ready, 1)
            pe.wait_ge(weights_loaded, WAIT_W)

            def tick(i, j, valid):
                n = NT * i + j
                a, b, c, d = n, n - LAG_B, n - LAG_C, n - LAG_D
                if valid(b):
                    pe.wait_ge(xT_ready[0], b + 1)
                    at_least(pe, exp_ready, b)
                    for g, (h0, h1) in enumerate(GROUPS):
                        for k in range(KD):
                            last = nc.tensor.matmul(pS[:, g, 0:(h1 - h0) * KEYS], xn2T[:, (j + 1) % 2, k, :],
                                                    wkx[:, k, h0 * KEYS:h1 * KEYS], start=(k == 0), stop=(k == KD - 1))
                    last.then_inc(score_ready, 1)
                if valid(c):
                    turn_prob(c, j, 0)
                    turn_prob(c, j, 1)
                if valid(a):
                    pe.wait_ge(tile_loaded[j], 32 * (i + 1))
                    at_least(pe, x1_ready, a)
                    for g in range(HG):
                        last = nc.tensor.matmul(pA[:, :], aT[:, j, g, :], wo[:, g, :], start=(g == 0), stop=(g == HG - 1))
                    last.then_inc(projected, 1)
                if valid(d):
                    pe.wait_ge(xn_ready[1], d + 1)
                    pe.wait_ge(xT_ready[0], upto(d + LAG_D))
                    turn(1, d, xn3[:, (j + 1) % 2, :])
                if valid(c):
                    at_least(pe, slot_taken, c - 1)
                    outputs(c, j, 0)
                    turn_prob(c, j, 2)
                    outputs(c, j, 1)
                    outputs(c, j, 2)
                if valid(a):
                    pe.wait_ge(xn_ready[0], a + 1)
                    at_least(pe, xT_ready[1], a - LAG_D + 1)
                    turn(0, a, xn2)
                if valid(d):
                    pe.wait_ge(xT_ready[1], d + 1)
                    pe.wait_ge(x2_ready, upto(d + 2))
                    for m in range(MS):
                        for k in range(KD):
                            last = nc.tensor.matmul(pO[:, m * P:(m + 1) * P], dqk[:, k, m * P:(m + 1) * P],
                                                    xn3T[:, (j + 1) % 2, k, :], start=(k == 0), stop=(k == KD - 1))
                    last.then_inc(slot_ready, 1)

            ticks(pe, tick)


F = 2048
CF = F // BLK
R = B * NS
PIECES = 2 * KD + CF
DT = B * T // NS
DTT = DT // P


def load_expert(eng, ring, loaded, e, W1, Wg, W2, pieces):
    for n in pieces:
        if n < 2 * KD:
            w = (W1, Wg)[n // KD]
            src = w[e, n % KD * P:(n % KD + 1) * P, :]
            dst = ring[:, n, :]
        else:
            c = n - 2 * KD
            src = W2[e, c * BLK:(c + 1) * BLK, :].rearrange("(j p) n -> p j n", p=P)
            dst = ring[:, n, :].rearrange("p (j n) -> p j n", n=D)
        eng.dma_start(dst, src).then_inc(loaded[n], 16)


def dispatch(nc, sem, s_sc, spare, xn_sc, slot_query, Wv, bv, Wo, bo, ln_g, ln_b, b1, bg, W1, Wg, W2, ring, piece_loaded, o, hT, bT):
    with ExitStack() as ctx:
        sb = lambda name, shape, dt: ctx.enter_context(nc.sbuf_tensor(name, shape, dt))
        CH = 4
        NCH = T // P // CH
        UN = B * NCH * MS
        ident = sb("D_ident", [P, P], F32)
        power = sb("D_power", [P, 1], F32)
        smax = sb("D_smax", [P, B, MS], F32)
        snm = sb("D_snm", [P, B, MS], F32)
        stot = sb("D_stot", [P, B, MS], F32)
        sinv = sb("D_sinv", [P, B, MS], F32)
        pT = sb("D_pT", [P, 2, CH, P], F32)
        un = sb("D_un", [P, B, MS, D], F32)
        uT = sb("D_uT", [P, KD, H, B, NS], F32)
        xn = spare[:, 0, :].rearrange("p (s t d) -> p s t d", s=2, d=D)
        weights = spare[:, 1, :].rearrange("p (w k n) -> p w k n", w=2, n=D)
        wv, wo = weights[:, 0, :, :], weights[:, 1, :, :]
        rows = sb("D_rows", [R, 5, D], F32)
        oa = sb("D_oa", [R, D], F32)
        oaT = sb("D_oaT", [P, KD, R], F32)
        stats = sb("D_stats", [R, 6], F32)
        mv = sb("D_mv", [R, 2], F32)
        vare = sb("D_vare", [R, 1], F32)
        rstd = sb("D_rstd", [R, 1], F32)
        hn = sb("D_hn", [R, 2, D], F32)
        brow = sb("D_brow", [P, 2, 2, P], F32)
        bank = [ctx.enter_context(nc.psum_tensor(f"D_bank{n}", [P, BLK], F32)) for n in range(4)]
        pU = [ctx.enter_context(nc.psum_tensor(f"D_pU{n}", [P, BLK], F32)) for n in range(4)]
        zeroed = sem("D_zeroed")
        ident_ready = sem("D_ident_ready")
        xn_loaded = [sem(f"D_xn_loaded{s}") for s in range(2)]
        rows_loaded = sem("D_rows_loaded")
        weights_loaded = sem("D_weights_loaded")
        bias_loaded = sem("D_bias_loaded")
        max_ready = sem("D_max_ready")
        exp_ready = sem("D_exp_ready")
        inv_ready = sem("D_inv_ready")
        made = sem("D_made")
        taken = sem("D_taken")
        mixed = sem("D_mixed")
        un_ready = sem("D_un_ready")
        step = sem("D_step")
        var_ready = sem("D_var_ready")
        rstd_ready = sem("D_rstd_ready")
        block = ctx.enter_context(nc.Block())

        names = ([("bT", n) for n in range(2)] + [("pT", n) for n in range(UN)] + [("uT", b, m) for b in range(B) for m in range(MS)]
                 + ["heads", "oaT", "out", "hT"])
        nth = {name: n for n, name in enumerate(names)}

        @block.sync
        def _(sp):
            def tokens(n):
                sp.dma_start(xn[:, n % 2, :, :], xn_sc[n * CH:(n + 1) * CH].rearrange("t p d -> p t d")).then_inc(xn_loaded[n % 2], 16)

            tokens(0)
            tokens(1)
            for n, src in enumerate((b1, bg)):
                sp.dma_start(brow[:, n, :, :], src.rearrange("e (q p) -> (e q) p", p=P).rearrange("(a r) p -> r a p", a=2)
                             ).then_inc(bias_loaded, 16)
            for b in range(B):
                r = slice(b * NS, (b + 1) * NS)
                for n, src in ((0, slot_query[0]), (3, ln_g), (4, ln_b)):
                    sp.dma_start(rows[r, n, :], src).then_inc(rows_loaded, 16)
            for n, src in ((1, bo), (2, bv)):
                sp.dma_start(rows[:, n, :], src.partition_broadcast(R)).then_inc(rows_loaded, 16)
            sp.dma_start(wv[:, :, :], Wv.rearrange("(k p) n -> p k n", p=P)).then_inc(weights_loaded, 16)
            sp.dma_start(wo[:, :, :], Wo.rearrange("(k p) n -> p k n", p=P)).then_inc(weights_loaded, 16)
            for n in range(2, B * NCH):
                sp.wait_ge(mixed, (n - 1) * MS)
                tokens(n)
                if n < 2 + PIECES // 3:
                    load_expert(sp, ring, piece_loaded, 0, W1, Wg, W2, range(3 * (n - 2), 3 * (n - 1)))

        @block.gpsimd
        def _(pool):
            identity(pool, ident, zeroed, ident_ready)
            pool.memset(power[:, :], -0.5).then_inc(zeroed, 1)
            pool.wait_ge(zeroed, 2)
            pool.wait_ge(rows_loaded, 16 * 8)
            nc.gpsimd.tensor_tensor(rows[:, 0, :], rows[:, 0, :], rows[:, 1, :], ALU.add).then_inc(zeroed, 1)
            pool.wait_ge(var_ready, 1)
            nc.gpsimd.tensor_tensor(rstd[:, :], vare[:, :], power[0:R, :], ALU.pow).then_inc(rstd_ready, 1)

        @block.scalar
        def _(act):
            for b in range(B):
                for m in range(MS):
                    act.wait_ge(max_ready, 2 * (b * MS + m) + 2)
                    t = s_sc[:, m, b * T:(b + 1) * T]
                    nc.scalar.activation(t, t, ACT.Exp, bias=snm[:, b, m:m + 1], scale=SCALE, accum_out=stot[:, b, m:m + 1]
                                         ).then_inc(exp_ready, 1)

        @block.vector
        def _(dve):
            def take(name, dst, src):
                dve.wait_ge(made, nth[name] + 1)
                nc.vector.tensor_copy(dst, src).then_inc(taken, 1)

            for b in range(B):
                for m in range(MS):
                    n = 2 * (b * MS + m)
                    nc.vector.tensor_reduce(smax[:, b, m:m + 1], s_sc[:, m, b * T:(b + 1) * T], AX.X, ALU.max).then_inc(max_ready, 1)
                    dve.wait_ge(max_ready, n + 1)
                    nc.vector.tensor_scalar(snm[:, b, m:m + 1], smax[:, b, m:m + 1], -SCALE, None, ALU.mult).then_inc(max_ready, 1)
            for n in range(2):
                dve.wait_ge(made, nth[("bT", n)] + 1)
                nc.vector.tensor_copy(bT[:, n, :, :, :].rearrange("p e j c -> p e c j"),
                                      bank[nth[("bT", n)] % 4][:, 0:2 * P].rearrange("p (e c j) -> p e c j", e=NS, c=CF)
                                      ).then_inc(taken, 1)
            for n in range(UN):
                dve.wait_ge(mixed, n - 1) if n >= 2 else None
                take(("pT", n), pT[:, n % 2, :, :], bank[nth[("pT", n)] % 4][:, :].rearrange("p (t r) -> p t r", t=CH))
            dve.wait_ge(exp_ready, B * MS)
            nc.vector.reciprocal(sinv[:, :, :], stot[:, :, :]).then_inc(inv_ready, 1)
            dve.wait_ge(inv_ready, 1)
            dve.wait_ge(mixed, UN)
            for b in range(B):
                for m in range(MS):
                    nc.vector.tensor_scalar(un[:, b, m, :], pU[b * MS + m][:, :], sinv[:, b, m:m + 1], None, ALU.mult
                                            ).then_inc(un_ready, 1)
            for b in range(B):
                for m in range(MS):
                    take(("uT", b, m), uT[:, :, m * H // MS:(m + 1) * H // MS, b, :],
                         bank[nth[("uT", b, m)] % 4][:, :].rearrange("p (k h s) -> p k h s", k=KD, s=NS))
            dve.wait_ge(rows_loaded, 16 * 8)
            dve.wait_ge(made, nth["heads"] + 1)
            nc.vector.tensor_tensor(oa[:, :], bank[nth["heads"] % 4][0:R, :], rows[:, 2, :], ALU.add).then_inc(taken, 1)
            take("oaT", oaT[:, :, :], bank[nth["oaT"] % 4][:, 0:KD * R].rearrange("p (k r) -> p k r", k=KD))
            dve.wait_ge(zeroed, 3)
            dve.wait_ge(made, nth["out"] + 1)
            nc.vector.tensor_tensor(o[:, :], bank[nth["out"] % 4][0:R, :], rows[:, 0, :], ALU.add).then_inc(taken, 1)
            dve.wait_ge(taken, nth["out"] + 1)
            nc.vector.bn_stats(stats[:, :], o[:, :]).then_inc(step, 1)
            dve.wait_ge(step, 1)
            nc.vector.bn_aggr(mv[:, :], stats[:, :]).then_inc(step, 1)
            dve.wait_ge(step, 2)
            nc.vector.tensor_scalar_add(vare[:, :], mv[:, 1:2], EPS).then_inc(var_ready, 1)
            dve.wait_ge(rstd_ready, 1)
            nc.vector.tensor_scalar(hn[:, 0, :], o[:, :], mv[:, 0:1], rstd[:, 0:1], ALU.subtract, ALU.mult).then_inc(step, 1)
            dve.wait_ge(step, 3)
            nc.vector.tensor_tensor(hn[:, 1, :], hn[:, 0, :], rows[:, 3, :], ALU.mult).then_inc(step, 1)
            dve.wait_ge(step, 4)
            nc.vector.tensor_tensor(hn[:, 0, :], hn[:, 1, :], rows[:, 4, :], ALU.add).then_inc(step, 1)
            take("hT", hT[:, :, :], bank[nth["hT"] % 4][:, 0:KD * R].rearrange("p (k r) -> p k r", k=KD))

        @block.tensor
        def _(pe):
            def into(name):
                n = nth[name]
                if n >= 4:
                    pe.wait_ge(taken, n - 3)
                return bank[n % 4]

            def mix(n):
                b, ch, m = n // (NCH * MS), n // MS % NCH, n % MS
                c = n // MS
                pe.wait_ge(xn_loaded[c % 2], 16 * (c // 2 + 1))
                pe.wait_ge(taken, nth[("pT", n)] + 1)
                for t in range(CH):
                    last = nc.tensor.matmul(pU[b * MS + m][:, :], pT[:, n % 2, t, :], xn[:, c % 2, t, :],
                                            start=(ch == 0 and t == 0), stop=(ch == NCH - 1 and t == CH - 1))
                last.then_inc(mixed, 1)

            pe.wait_ge(ident_ready, 1)
            pe.wait_ge(bias_loaded, 32)
            for n in range(2):
                out = into(("bT", n))
                for a in range(2):
                    last = nc.tensor.transpose(out[:, a * P:(a + 1) * P], brow[:, n, a, :], ident[:, :])
                last.then_inc(made, 1)
            for n in range(UN):
                b, ch, m = n // (NCH * MS), n // MS % NCH, n % MS
                pe.wait_ge(exp_ready, b * MS + m + 1)
                out = into(("pT", n))
                for t in range(CH):
                    c0 = b * T + (ch * CH + t) * P
                    last = nc.tensor.transpose(out[:, t * P:(t + 1) * P], s_sc[:, m, c0:c0 + P], ident[:, :])
                last.then_inc(made, 1)
                if n:
                    mix(n - 1)
            mix(UN - 1)
            for b in range(B):
                for m in range(MS):
                    pe.wait_ge(un_ready, b * MS + m + 1)
                    out = into(("uT", b, m))
                    for k in range(KD):
                        last = nc.tensor.transpose(out[:, k * P:(k + 1) * P], un[:, b, m, k * P:(k + 1) * P], ident[:, :])
                    last.then_inc(made, 1)
            pe.wait_ge(taken, nth[("uT", B - 1, MS - 1)] + 1)
            pe.wait_ge(weights_loaded, 32)
            out = into("heads")
            for h in range(H):
                for k in range(KD):
                    last = nc.tensor.matmul(out[0:R, h * DH:(h + 1) * DH], uT[:, k, h, :, :].rearrange("p b s -> p (b s)"),
                                            wv[:, k, h * DH:(h + 1) * DH], start=(k == 0), stop=(k == KD - 1))
            last.then_inc(made, 1)
            pe.wait_ge(taken, nth["heads"] + 1)
            out = into("oaT")
            for k in range(KD):
                last = nc.tensor.transpose(out[:, k * R:(k + 1) * R], oa[:, k * P:(k + 1) * P], ident[0:R, 0:R])
            last.then_inc(made, 1)
            pe.wait_ge(taken, nth["oaT"] + 1)
            out = into("out")
            for k in range(KD):
                last = nc.tensor.matmul(out[0:R, :], oaT[:, k, :], wo[:, k, :], start=(k == 0), stop=(k == KD - 1))
            last.then_inc(made, 1)
            pe.wait_ge(step, 5)
            out = into("hT")
            for k in range(KD):
                last = nc.tensor.transpose(out[:, k * R:(k + 1) * R], hn[:, 0, k * P:(k + 1) * P], ident[0:R, 0:R])
            last.then_inc(made, 1)


def experts(nc, sem, W1, Wg, W2, b2, xT_sc, c_Wq, c_bq, ring, piece_loaded, o, hT, bT, qc, o2):
    with ExitStack() as ctx:
        sb = lambda name, shape, dt: ctx.enter_context(nc.sbuf_tensor(name, shape, dt))
        ps = lambda name, shape, dt: ctx.enter_context(nc.psum_tensor(name, shape, dt))
        ident = sb("E_ident", [P, P], F32)
        fold = sb("E_fold", [P, R], F32)
        zero = sb("E_zero", [P, BLK], F32)
        rows = sb("E_rows", [R, D], F32)
        base = sb("E_base", [R, D], F32)
        cbq = sb("E_cbq", [P, KD], F32)
        wq = sb("E_wq", [P, KD, D], F32)
        xq = sb("E_xq", [P, 2, DTT, KD, P], F32)
        inner = sb("E_inner", [P, 2, BLK], F32)
        ug = sb("E_ug", [P, 2, CF * NT, B], F32)
        ex = sb("E_ex", [P, 2, CF * NT, B], F32)
        ex1 = sb("E_ex1", [P, 2, CF * NT, B], F32)
        sg = sb("E_sg", [P, 2, CF * NT, B], F32)
        si = sb("E_si", [P, 2, CF * NT, B], F32)
        vT = sb("E_vT", [P, CF * NT, B, NS], F32)
        ysb = sb("E_ysb", [P, BLK], F32)
        pI = ps("E_pI", [P, 2, BLK], F32)
        pT = ps("E_pT", [P, 2, BLK], F32)
        pY = ps("E_pY", [P, BLK], F32)
        pQ = ps("E_pQ", [P, 2, 2, DT], F32)
        pool_carried = sem("E_pool_carried")
        sp_carried = sem("E_sp_carried")
        zeroed = sem("E_zeroed")
        ident_ready = sem("E_ident_ready")
        fold_ready = sem("E_fold_ready")
        small_loaded = sem("E_small_loaded")
        xq_loaded = [sem(f"E_xq_loaded{s}") for s in range(2)]
        q_made = sem("E_q_made")
        q_taken = sem("E_q_taken")
        inner_made = sem("E_inner_made")
        inner_taken = sem("E_inner_taken")
        turned = sem("E_turned")
        ug_ready = sem("E_ug_ready")
        ex_ready = sem("E_ex_ready")
        step = sem("E_step")
        v_clear = sem("E_v_clear")
        v_ready = sem("E_v_ready")
        y_done = sem("E_y_done")
        y_copied = sem("E_y_copied")
        y_sum = sem("E_y_sum")
        o2_ready = sem("E_o2_ready")
        block = ctx.enter_context(nc.Block())

        @block.sync
        def _(sp):
            sp.dma_start(rows[:, :][0:NS, :], b2).then_inc(small_loaded, 16)
            sp.dma_start(rows[:, :][NS:R, :], b2).then_inc(small_loaded, 16)
            with sp.Fori(1, NS) as e:
                sp.wait_ge(inner_made, 2 * e - 1)
                carry(sp, sp_carried)
                load_expert(sp, ring, piece_loaded, e, W1, Wg, W2, range(0, KD))
                sp.wait_ge(inner_made, 2 * e)
                carry(sp, sp_carried)
                load_expert(sp, ring, piece_loaded, e, W1, Wg, W2, range(KD, 2 * KD))
                sp.wait_ge(y_done, e)
                carry(sp, sp_carried)
                load_expert(sp, ring, piece_loaded, e, W1, Wg, W2, range(2 * KD, PIECES))

        @block.gpsimd
        def _(pool):
            identity(pool, ident, zeroed, ident_ready)
            pool.memset(zero[:, :], 0.0).then_inc(zeroed, 1)
            pool.memset(vT[:, :, :, :], 0.0).then_inc(v_clear, 1)
            pool.wait_ge(small_loaded, 16 * 4)
            nc.gpsimd.tensor_tensor(base[:, :], o[:, :], rows[:, :], ALU.add).then_inc(zeroed, 1)
            with pool.Fori(1, NS) as e:
                pool.wait_ge(y_done, e)
                carry(pool, pool_carried)
                pool.memset(vT[:, :, :, :], 0.0).then_inc(v_clear, 1)

        @block.vector
        def _(dve):
            dve.wait_ge(ident_ready, 1)
            nc.vector.tensor_reduce(fold[:, :], ident[:, :].rearrange("p (c r) -> p r c", r=R), AX.X, ALU.add).then_inc(fold_ready, 1)
            with dve.Fori(0, NS) as e:
                dve.wait_ge(turned, e + 1)
                for n in range(2):
                    last = nc.vector.tensor_tensor(
                        ug[:, n, :, :], pT[:, n, :].rearrange("p (q b s) -> p q b s", b=B, s=NS)[:, :, :, bass.ds(e, 1)].rearrange("p q b s -> p q (b s)"),
                        bT[:, n, :, :, :].rearrange("p e j c -> p (e j c)")[:, bass.ds(e * CF * NT, CF * NT)].unsqueeze(2).broadcast_to([P, CF * NT, B]),
                        ALU.add)
                last.then_inc(ug_ready, 1)
                dve.wait_ge(ex_ready, e + 1)
                nc.vector.tensor_scalar_add(ex1[:, :, :, :], ex[:, :, :, :], 1.0).then_inc(step, 1)
                dve.wait_ge(step, 3 * e + 1)
                nc.vector.reciprocal(sg[:, :, :, :], ex1[:, :, :, :]).then_inc(step, 1)
                dve.wait_ge(step, 3 * e + 2)
                nc.vector.tensor_tensor(si[:, :, :, :], ug[:, :, :, :], sg[:, :, :, :], ALU.mult).then_inc(step, 1)
                dve.wait_ge(step, 3 * e + 3)
                dve.wait_ge(v_clear, e + 1)
                nc.vector.tensor_tensor(vT[:, :, :, bass.ds(e, 1)].rearrange("p q b s -> p q (b s)"), si[:, 0, :, :], si[:, 1, :, :],
                                        ALU.mult).then_inc(v_ready, 1)
            dve.wait_ge(y_done, NS + 1)
            nc.vector.tensor_copy(ysb[:, :], pY[:, :]).then_inc(y_copied, 1)
            dve.wait_ge(y_sum, 1)
            dve.wait_ge(zeroed, 3)
            nc.vector.tensor_tensor(o2[:, :], pI[0:R, 0, :], base[:, :], ALU.add).then_inc(o2_ready, 1)

        @block.scalar
        def _(act):
            act.dma_start(cbq[:, :], c_bq.rearrange("(k p) -> p k", p=P), allow_slow_non_contiguous=True).then_inc(small_loaded, 16)
            act.dma_start(wq[:, :, :], c_Wq.rearrange("(k p) n -> p k n", p=P)).then_inc(small_loaded, 16)
            for u in range(2):
                act.dma_start(xq[:, u, :, :, :], xT_sc[u * DTT:(u + 1) * DTT].rearrange("t p k q -> p t k q")).then_inc(xq_loaded[u], 16)
            act.wait_ge(small_loaded, 64)
            with act.Fori(0, NS // 2) as i:
                for u in range(2):
                    e = 2 * i + u
                    for g in range(2):
                        act.wait_ge(q_made, 2 * e + g + 1)
                        for mm in range(2):
                            m = 2 * g + mm
                            last = nc.scalar.activation(qc[:, m, bass.ds(e * DT, DT)], pQ[:, g, mm, :], ACT.Identity, bias=cbq[:, m:m + 1])
                        last.then_inc(q_taken, 1)
                    act.dma_start(xq[:, u, :, :, :], xT_sc[bass.ds((2 * i + 2 + u) % NS * DTT, DTT)].rearrange("t p k q -> p t k q")
                                  ).then_inc(xq_loaded[u], 16)
                    for n in range(2):
                        act.wait_ge(inner_made, 2 * e + n + 1)
                        act.wait_ge(turned, e)
                        nc.scalar.activation(inner[:, n, :], pI[:, n, :], ACT.Copy).then_inc(inner_taken, 1)
                    act.wait_ge(ug_ready, e + 1)
                    nc.scalar.activation(ex[:, :, :, :], ug[:, :, :, :], ACT.Exp, scale=-1.0).then_inc(ex_ready, 1)
            for u in range(2):
                act.wait_ge(xq_loaded[u], 16 * (NS // 2 + 1))

        @block.tensor
        def _(pe):
            pe.wait_ge(ident_ready, 1)
            pe.wait_ge(zeroed, 2)
            pe.wait_ge(v_clear, 1)
            for c in range(CF):
                nc.tensor.matmul(pY[c * R:(c + 1) * R, :], vT[:, 0, :, :].rearrange("p b s -> p (b s)"), zero[:, :], start=True, stop=False,
                                 tile_position=(0, c * R), skip_group_check=True)
            pe.wait_ge(small_loaded, 64)
            with pe.Fori(0, NS // 2) as i:
                for u in range(2):
                    e = 2 * i + u
                    pe.wait_ge(xq_loaded[u], 16 * (i + 1))
                    for g in range(2):
                        pe.wait_ge(q_taken, 2 * e)
                        for mm in range(2):
                            m = 2 * g + mm
                            for k in range(KD):
                                last = nc.tensor.matmul(pQ[:, g, mm, :], wq[:, k, m * P:(m + 1) * P], xq[:, u, :, k, :],
                                                        start=(k == 0), stop=(k == KD - 1))
                        last.then_inc(q_made, 1)
                    for n in range(2):
                        pe.wait_ge(inner_taken, 2 * e)
                        for k in range(KD):
                            pe.wait_ge(piece_loaded[n * KD + k], 16 * (e + 1))
                            for c in range(CF):
                                last = nc.tensor.matmul(pI[c * R:(c + 1) * R, n, :], hT[:, k, :], ring[:, n * KD + k, c * BLK:(c + 1) * BLK],
                                                        start=(k == 0), stop=(k == KD - 1), tile_position=(0, c * R))
                        last.then_inc(inner_made, 1)
                    pe.wait_ge(ug_ready, e)
                    pe.wait_ge(inner_taken, 2 * e + 2)
                    for n in range(2):
                        for j in range(NT):
                            last = nc.tensor.transpose(pT[:, n, j * P:(j + 1) * P], inner[:, n, j * P:(j + 1) * P], ident[:, :])
                    last.then_inc(turned, 1)
                    pe.wait_ge(v_ready, e + 1)
                    for c in range(CF):
                        pe.wait_ge(piece_loaded[2 * KD + c], 16 * (e + 1))
                    for j in range(NT):
                        for c in range(CF):
                            last = nc.tensor.matmul(pY[c * R:(c + 1) * R, :], vT[:, j * CF + c, :, :].rearrange("p b s -> p (b s)"),
                                                    ring[:, 2 * KD + c, j * D:(j + 1) * D], start=False, stop=False,
                                                    tile_position=(0, c * R), skip_group_check=True)
                    last.then_inc(y_done, 1)
            for c in range(CF):
                last = nc.tensor.matmul(pY[c * R:(c + 1) * R, :], zero[:, 0:R], zero[:, :], start=False, stop=True,
                                        tile_position=(0, c * R), skip_group_check=True)
            last.then_inc(y_done, 1)
            pe.wait_ge(y_copied, 1)
            pe.wait_ge(fold_ready, 1)
            nc.tensor.matmul(pI[0:R, 0, :], fold[:, :], ysb[:, :], start=True, stop=True).then_inc(y_sum, 1)


CSCALE = 1.0 / DH ** 0.5
TB = T // P


def combine(nc, sem, o2, qc, c_Wk, c_bk, c_Wv, c_bv, c_Wo, c_bo, x2_sc, out):
    RT = R // B
    with ExitStack() as ctx:
        sb = lambda name, shape, dt: ctx.enter_context(nc.sbuf_tensor(name, shape, dt))
        ps = lambda name, shape, dt: ctx.enter_context(nc.psum_tensor(name, shape, dt))
        ident = sb("F_ident", [P, P], F32)
        wk = sb("F_wk", [P, KD, D], F32)
        wv = sb("F_wv", [P, KD, D], F32)
        wo = sb("F_wo", [P, HG, D], F32)
        bias = sb("F_bias", [P, 2, HG], F32)
        bo = sb("F_bo", [P, D], F32)
        o2T = sb("F_o2T", [P, KD, R], F32)
        bd = sb("F_bd", [P, 2, B, HG, HPG, RT], F32)
        vo = sb("F_vo", [P, B, 2, D], F32)
        qst = sb("F_qst", [P, 2, HG, P], F32)
        x2 = sb("F_x2", [P, NT, D], F32)
        mx = sb("F_mx", [P, H], F32)
        sc = sb("F_sc", [P, H, RT], F32)
        ex = sb("F_ex", [P, 2, H, RT], F32)
        total = sb("F_total", [P, H], F32)
        inv = sb("F_inv", [P, H], F32)
        prob = sb("F_prob", [P, H, RT], F32)
        probT = sb("F_probT", [P, 2, 2, P], F32)
        res = sb("F_res", [P, 2, D], F32)
        pK = ps("F_pK", [P, 2, HG, R], F32)
        pV = ps("F_pV", [P, BLK], F32)
        pS = ps("F_pS", [P, 2, BLK], F32)
        pP = ps("F_pP", [P, BLK], F32)
        pO = ps("F_pO", [P, 2, BLK], F32)
        sp_carried = sem("F_sp_carried")
        zeroed = sem("F_zeroed")
        ident_ready = sem("F_ident_ready")
        weights_loaded = sem("F_weights_loaded")
        tile_loaded = [sem(f"F_tile_loaded{s}") for s in range(NT)]
        o2_turned = sem("F_o2_turned")
        o2T_ready = sem("F_o2T_ready")
        kv_made = sem("F_kv_made")
        bd_ready = sem("F_bd_ready")
        vo_made = sem("F_vo_made")
        vo_ready = sem("F_vo_ready")
        q_staged = sem("F_q_staged")
        xb_ready = sem("F_xb_ready")
        score_ready = sem("F_score_ready")
        max_ready = sem("F_max_ready")
        sc_ready = sem("F_sc_ready")
        ex_ready = sem("F_ex_ready")
        sum_ready = sem("F_sum_ready")
        inv_ready = sem("F_inv_ready")
        prob_ready = sem("F_prob_ready")
        prob_turned = sem("F_prob_turned")
        probT_ready = sem("F_probT_ready")
        out_ready = sem("F_out_ready")
        res_ready = sem("F_res_ready")
        stored = [sem(f"F_stored{s}") for s in range(2)]
        ov = out.rearrange("b (t p) d -> (b t) p d", p=P)
        block = ctx.enter_context(nc.Block())
        WAIT_W = 16 * 6

        @block.sync
        def _(sp):
            def load_at(t, j):
                sp.dma_start(x2[:, j, :], x2_sc[t]).then_inc(tile_loaded[j], 16)

            for weights, dst in ((c_Wk, wk), (c_Wv, wv), (c_Wo, wo)):
                sp.dma_start(dst[:, :, :], weights.rearrange("(k p) n -> p k n", p=P)).then_inc(weights_loaded, 16)
            for j in range(NT - 1):
                load_at(j, j)

            def tick(i, j, valid):
                n = NT * i + j
                a, c = n, n - LAG_C
                if valid(a):
                    at_least(sp, res_ready, a)
                    carry(sp, sp_carried)
                    load_at((a + NT - 1) % TILES, (j + NT - 1) % NT)
                if valid(c):
                    sp.wait_ge(res_ready, c + 1)
                    sp.dma_start(ov[c], res[:, j % 2, :]).then_inc(stored[j % 2], 16)

            ticks(sp, tick)
            for s in range(2):
                sp.wait_ge(stored[s], 16 * TILES // 2)
            for j in range(NT):
                sp.wait_ge(tile_loaded[j], 16 * (TILES // NT + (j < NT - 1)))

        @block.gpsimd
        def _(pool):
            pool.memset(bd[:, :, :, :, :, :], 0.0).then_inc(zeroed, 1)
            pool.memset(ident[:, :], 0.0).then_inc(zeroed, 1)
            pool.wait_ge(zeroed, 2)
            pool.affine_select(out=ident[:, :], in_=ident[:, :], compare_op=ALU.not_equal, fill=1.0,
                               base=0, pattern=[[-1, P]], channel_multiplier=1).then_inc(ident_ready, 1)
            pool.wait_ge(weights_loaded, WAIT_W)

            def tick(i, j, valid):
                n = NT * i + j
                if valid(n):
                    at_least(pool, score_ready, n - 1)
                    nc.gpsimd.tensor_copy(qst[:, j % 2, :, :], qc[:, :, bass.ds(n * P, P)]).then_inc(q_staged, 1)
                    pool.wait_ge(tile_loaded[j], 16 * (i + 1))
                    nc.gpsimd.tensor_tensor(x2[:, j, :], x2[:, j, :], bo[:, :], ALU.add).then_inc(xb_ready, 1)

            ticks(pool, tick)

        @block.vector
        def _(dve):
            dve.wait_ge(o2_turned, 1)
            nc.vector.tensor_copy(o2T[:, :, :], pV[:, 0:KD * R].rearrange("p (k r) -> p k r", k=KD)).then_inc(o2T_ready, 1)
            dve.wait_ge(zeroed, 1)
            dve.wait_ge(weights_loaded, WAIT_W)
            dve.wait_ge(kv_made, 1)
            for h in range(HPG):
                rows = slice(h * DH, (h + 1) * DH)
                for n in range(2):
                    for b in range(B):
                        last = nc.vector.tensor_tensor(bd[rows, n, b, :, h, :], pK[rows, n, :, b * RT:(b + 1) * RT],
                                                       bias[rows, n, :].unsqueeze(2).broadcast_to([DH, HG, RT]), ALU.add)
            last.then_inc(bd_ready, 1)

            def tick(i, j, valid):
                n = NT * i + j
                a, b, c = n, n - LAG_B, n - LAG_C
                if valid(a):
                    dve.wait_ge(score_ready, a + 1)
                    at_least(dve, sc_ready, a)
                    s = pS[:, j % 2, 0:H * RT].rearrange("p (h s) -> p h s", s=RT)
                    nc.vector.tensor_reduce(mx[:, :], s, AX.X, ALU.max).then_inc(max_ready, 1)
                    dve.wait_ge(max_ready, a + 1)
                    at_least(dve, ex_ready, a)
                    nc.vector.tensor_tensor(sc[:, :, :], s, mx[:, :].unsqueeze(2).broadcast_to([P, H, RT]), ALU.subtract
                                            ).then_inc(sc_ready, 1)
                if valid(b):
                    s = (j + 1) % 2
                    dve.wait_ge(ex_ready, b + 1)
                    at_least(dve, prob_ready, b)
                    nc.vector.tensor_reduce(total[:, :], ex[:, s, :, :], AX.X, ALU.add).then_inc(sum_ready, 1)
                    dve.wait_ge(sum_ready, b + 1)
                    nc.vector.reciprocal(inv[:, :], total[:, :]).then_inc(inv_ready, 1)
                    dve.wait_ge(inv_ready, b + 1)
                    at_least(dve, prob_turned, b)
                    nc.vector.tensor_tensor(prob[:, :, :], ex[:, s, :, :], inv[:, :].unsqueeze(2).broadcast_to([P, H, RT]), ALU.mult
                                            ).then_inc(prob_ready, 1)
                if valid(c):
                    s = j % 2
                    dve.wait_ge(out_ready, c + 1)
                    dve.wait_ge(xb_ready, c + 1)
                    if not isinstance(c, int) or c >= 2:
                        dve.wait_ge(stored[s], 16 * (2 * i + j // 2 - 1))
                    nc.vector.tensor_tensor(res[:, s, :], pO[:, s, :], x2[:, (j + NT - LAG_C) % NT, :], ALU.add).then_inc(res_ready, 1)

            ticks(dve, tick)

        @block.scalar
        def _(act):
            for n, b in enumerate((c_bk, c_bv)):
                act.dma_start(bias[:, n, :], b.rearrange("(g p) -> p g", p=P), allow_slow_non_contiguous=True).then_inc(weights_loaded, 16)
            act.dma_start(bo[:, :], c_bo.partition_broadcast(P)).then_inc(weights_loaded, 16)
            for b in range(B):
                act.wait_ge(vo_made, b + 1)
                nc.scalar.activation(vo[:, b, :, :], pO[:, :, :], ACT.Copy).then_inc(vo_ready, 1)

            def tick(i, j, valid):
                n = NT * i + j
                a, b = n, n - LAG_B
                if valid(a):
                    act.wait_ge(sc_ready, a + 1)
                    at_least(act, prob_ready, a - 1)
                    nc.scalar.activation(ex[:, j % 2, :, :], sc[:, :, :], ACT.Exp, scale=CSCALE).then_inc(ex_ready, 1)
                if valid(b):
                    s = (j + 1) % 2
                    act.wait_ge(prob_turned, b + 1)
                    at_least(act, out_ready, b - 1)
                    nc.scalar.activation(probT[:, s, :, :], pP[:, 0:2 * P].rearrange("p (g q) -> p g q", g=2), ACT.Copy
                                         ).then_inc(probT_ready, 1)

            ticks(act, tick)

        @block.tensor
        def _(pe):
            pe.wait_ge(ident_ready, 1)
            for k in range(KD):
                last = nc.tensor.transpose(pV[:, k * R:(k + 1) * R], o2[:, k * P:(k + 1) * P], ident[0:R, 0:R])
            last.then_inc(o2_turned, 1)
            pe.wait_ge(o2T_ready, 1)
            pe.wait_ge(weights_loaded, WAIT_W)
            for n, w in enumerate((wk, wv)):
                for g in range(HG):
                    for k in range(KD):
                        last = nc.tensor.matmul(pK[:, n, g, :], w[:, k, g * P:(g + 1) * P], o2T[:, k, :],
                                                start=(k == 0), stop=(k == KD - 1))
            last.then_inc(kv_made, 1)
            pe.wait_ge(bd_ready, 1)
            for b in range(B):
                if b:
                    pe.wait_ge(vo_ready, b)
                for g in range(HG):
                    r = g % 2 * HPG * RT
                    last = nc.tensor.matmul(pO[r:r + HPG * RT, g // 2, :], bd[:, 1, b, g, :, :].rearrange("p h s -> p (h s)"),
                                            wo[:, g, :], start=True, stop=True, tile_position=(0, r))
                last.then_inc(vo_made, 1)
            pe.wait_ge(vo_ready, B)

            def tick(i, j, valid):
                n = NT * i + j
                a, b, c = n, n - LAG_B, n - LAG_C
                if valid(a):
                    pe.wait_ge(q_staged, a + 1)
                    at_least(pe, sc_ready, a - 1)
                    for g in range(HG):
                        last = nc.tensor.matmul(pS[:, j % 2, g * HPG * RT:(g + 1) * HPG * RT], qst[:, j % 2, g, :],
                                                bd[:, 0, a // TB, g, :, :].rearrange("p h s -> p (h s)") if isinstance(a, int) else
                                                bd[:, 0, bass.ds(a // TB, 1), g, :, :].rearrange("p o h s -> p (o h s)"),
                                                start=True, stop=True)
                    last.then_inc(score_ready, 1)
                if valid(c):
                    s = j % 2
                    pe.wait_ge(probT_ready, c + 1)
                    at_least(pe, res_ready, c - 1)
                    for g in range(2):
                        last = nc.tensor.matmul(pO[:, s, :], probT[:, s, g, :], vo[:, c // TB, g, :] if isinstance(c, int) else
                                                vo[:, bass.ds(c // TB, 1), g, :].rearrange("p o d -> p (o d)"),
                                                start=(g == 0), stop=(g == 1))
                    last.then_inc(out_ready, 1)
                if valid(b):
                    pe.wait_ge(prob_ready, b + 1)
                    at_least(pe, probT_ready, b)
                    for g in range(2):
                        last = nc.tensor.transpose(pP[:, g * P:(g + 1) * P],
                                                   prob[:, g * H // 2:(g + 1) * H // 2, :].rearrange("p h s -> p (h s)"), ident[:, :])
                    last.then_inc(prob_turned, 1)

            ticks(pe, tick)


def decoder_layer(nc, names, args):
    a = dict(zip(names, args))
    out = args[-1]

    def phase(program, *operands):
        taken = []

        def sem(name):
            taken.append(nc.alloc_semaphore(name))
            return taken[-1]

        program(nc, sem, *operands)
        nc.clear_and_free_semaphores(taken)
        nc.all_engine_barrier()

    dram = lambda name, *shape: nc.dram_tensor(name, shape, F32, kind="Internal").ap()
    heads = (NBLK, HG, P, BLK)
    q_hi, q_lo, k_hi, k_lo = [dram(name, *heads) for name in ("q_hi", "q_lo", "k_hi", "k_lo")]
    v_sc = dram("v_sc", NBLK, NT, P, D)
    z_sc = dram("z_sc", 1, B * H)
    a_sc = dram("a_sc", *heads)
    vw_sc = dram("vw_sc", XK, D)
    x2_sc = dram("x2_sc", TILES, P, D)
    xn_sc = dram("xn_sc", TILES, P, D)
    xT_sc = dram("xT_sc", TILES, P, KD, P)

    attn = lambda name: a["L0_attn_" + name]
    xattn = lambda name: a["L0_xattn_" + name]
    ffn = lambda name: a["L0_ffn_" + name]

    phase(project_self_attention, a["x"], attn("Wq"), attn("Wk"), attn("Wv"), attn("span_w"), attn("span_b"),
                           q_hi, q_lo, k_hi, k_lo, v_sc, z_sc)
    phase(self_attention, q_hi, q_lo, k_hi, k_lo, v_sc, z_sc, a_sc)

    with ExitStack() as ffn_memory:
        qc = ffn_memory.enter_context(nc.sbuf_tensor("qc", [P, KD, B * T], F32))
        slot_scores, spare = qc[:, 0:MS, :], qc[:, MS:, :]
        with ExitStack() as folded:
            sb = lambda name, shape: folded.enter_context(nc.sbuf_tensor(name, shape, F32))
            wkx = sb("wkx", [P, KD, XK])
            vwo = sb("vwo", [P, XT, D])
            dqk = sb("dqk", [P, KD, HS])
            dqb = sb("dqb", [P, MS])
            phase(fold_weights, qc, a["ctx_768"], xattn("Wq"), xattn("Wk"), xattn("Wv"), xattn("Wout"), ffn("slot_query"),
                         ffn("d_Wq"), ffn("d_Wk"), ffn("d_bq"), ffn("d_bk"), vw_sc, wkx, vwo, dqk, dqb)
            phase(cross_attention, a["x"], a_sc, attn("Wo_w"), attn("Wo_b"), xattn("bout"), wkx, vwo, dqk, dqb,
                            x2_sc, xn_sc, xT_sc, slot_scores)
        o2 = ffn_memory.enter_context(nc.sbuf_tensor("o2", [R, D], F32))
        with ExitStack() as expert_memory:
            sb = lambda name, shape: expert_memory.enter_context(nc.sbuf_tensor(name, shape, F32))
            ring = sb("ring", [P, PIECES, F])
            o = sb("o", [R, D])
            hT = sb("hT", [P, KD, R])
            bT = sb("bT", [P, 2, NS, NT, CF])
            piece_loaded = [nc.alloc_semaphore(f"piece_loaded{n}") for n in range(PIECES)]
            phase(dispatch, slot_scores, spare, xn_sc, ffn("slot_query"), ffn("d_Wv"), ffn("d_bv"), ffn("d_Wo"), ffn("d_bo"),
                     ffn("e_ln_g"), ffn("e_ln_b"), ffn("e_b1"), ffn("e_bg"), ffn("e_W1"), ffn("e_Wg"), ffn("e_W2"),
                     ring, piece_loaded, o, hT, bT)
            phase(experts, ffn("e_W1"), ffn("e_Wg"), ffn("e_W2"), ffn("e_b2"), xT_sc, ffn("c_Wq"), ffn("c_bq"),
                    ring, piece_loaded, o, hT, bT, qc, o2)
        phase(combine, o2, qc, ffn("c_Wk"), ffn("c_bk"), ffn("c_Wv"), ffn("c_bv"), ffn("c_Wo"), ffn("c_bo"), x2_sc, out)


_INS = ["x",
        "ctx_768",
        "L0_attn_Wq",
        "L0_attn_Wk",
        "L0_attn_Wv",
        "L0_attn_Wo_w",
        "L0_attn_Wo_b",
        "L0_attn_span_w",
        "L0_attn_span_b",
        "L0_xattn_Wq",
        "L0_xattn_Wk",
        "L0_xattn_Wv",
        "L0_xattn_Wout",
        "L0_xattn_bout",
        "L0_ffn_slot_query",
        "L0_ffn_d_Wq",
        "L0_ffn_d_Wk",
        "L0_ffn_d_Wv",
        "L0_ffn_d_Wo",
        "L0_ffn_d_bq",
        "L0_ffn_d_bk",
        "L0_ffn_d_bv",
        "L0_ffn_d_bo",
        "L0_ffn_c_Wq",
        "L0_ffn_c_Wk",
        "L0_ffn_c_Wv",
        "L0_ffn_c_Wo",
        "L0_ffn_c_bq",
        "L0_ffn_c_bk",
        "L0_ffn_c_bv",
        "L0_ffn_c_bo",
        "L0_ffn_e_ln_g",
        "L0_ffn_e_ln_b",
        "L0_ffn_e_W1",
        "L0_ffn_e_b1",
        "L0_ffn_e_Wg",
        "L0_ffn_e_bg",
        "L0_ffn_e_W2",
        "L0_ffn_e_b2"]


def kernel(**inputs):
    import numpy as _np
    import concourse.bacc as _bacc
    from concourse import mybir as _mybir
    from concourse.bass_utils import run_bass_kernel_spmd as _run

    nc = _bacc.Bacc("TRN2", target_bir_lowering=False, num_devices=1)
    arrays, args = {}, []
    for name in _INS:
        a = _np.ascontiguousarray(inputs[name])
        arrays[f"in_{name}_dram"] = a
        args.append(nc.dram_tensor(f"in_{name}_dram", a.shape, _mybir.dt.from_np(a.dtype), kind="ExternalInput").ap())
    args.append(nc.dram_tensor("out_0_dram", (2, 2048, 512), _mybir.dt.float32, kind="ExternalOutput").ap())
    decoder_layer(nc, _INS, args)
    r = _run(nc, [arrays], core_ids=[0])
    return r.results[0]["out_0_dram"]
```

```python
from contextlib import ExitStack

import concourse.bass as bass
from concourse import mybir

F32 = mybir.dt.float32
F32R = mybir.dt.float32r
BF16 = mybir.dt.bfloat16
I32 = mybir.dt.int32
ALU = mybir.AluOpType
ACT = mybir.ActivationFunctionType
AX = mybir.AxisListType

P = 128
B, T, D = 2, 2048, 512
KD = D // P
BLK = 512
NT = BLK // P
NBLK = B * T // BLK
BPB = T // BLK
EPS = 1e-5

HG, HPG, DH = 4, 4, 32
H = HG * HPG
RAMP = 256.0
NEG = -1e30


def carry(eng, carried):
    eng.sem_inc(carried, 1)


def identity(pool, tile, zeroed, ready):
    pool.memset(tile[:, :], 0.0).then_inc(zeroed, 1)
    pool.wait_ge(zeroed, 1)
    pool.affine_select(out=tile[:, :], in_=tile[:, :], compare_op=ALU.not_equal, fill=1.0,
                       base=0, pattern=[[-1, P]], channel_multiplier=1).then_inc(ready, 1)


def project_self_attention(nc, sem, x, Wq, Wk, Wv, span_w, span_b, q_hi, q_lo, k_hi, k_lo, v_sc, z_sc):
    xv = x.rearrange("b (c j p) d -> (b c) p j d", p=P, j=NT)
    OUT = 3 * NT
    HALF = OUT // 2
    with ExitStack() as ctx:
        sb = lambda name, shape, dt: ctx.enter_context(nc.sbuf_tensor(name, shape, dt))
        ps = lambda name, shape, dt: ctx.enter_context(nc.psum_tensor(name, shape, dt))
        ident = sb("A_ident", [P, P], F32)
        w = sb("A_w", [P, 3, KD, D], F32)
        spanw = sb("A_spanw", [P, KD, H], F32)
        spanb = sb("A_spanb", [P, H], F32)
        xin = sb("A_xin", [P, 2, NT, D], F32)
        stats = sb("A_stats", [P, NT, 6], F32)
        mv = sb("A_mv", [P, NT, 2], F32)
        vare = sb("A_vare", [P, NT], F32)
        std = sb("A_std", [P, NT], F32)
        rstd = sb("A_rstd", [P, NT], F32)
        xn = sb("A_xn", [P, NT, D], F32)
        xnT = sb("A_xnT", [P, 2, KD, BLK], F32)
        xsum = sb("A_xsum", [P, KD, NBLK + 1], F32)
        hi = sb("A_hi", [P, 2, 2 * KD, BLK], F32R)
        lo = sb("A_lo", [P, 2, 2 * KD, BLK], F32R)
        v = sb("A_v", [P, 2, NT, D], F32)
        xm = sb("A_xm", [P, B, KD], F32)
        xmb = sb("A_xmb", [P, B, KD, P], F32)
        zt = sb("A_z", [P, 4, B, H], F32)
        pT = ps("A_pT", [P, KD, BLK], F32)
        pO = ps("A_pO", [P, 4, BLK], F32)
        sp_carried = sem("A_sp_carried")
        dve_carried = sem("A_dve_carried")
        zeroed = sem("A_zeroed")
        ident_ready = sem("A_ident_ready")
        weights_loaded = sem("A_weights_loaded")
        x_loaded0 = sem("A_x_loaded0")
        x_loaded1 = sem("A_x_loaded1")
        dve_step = sem("A_dve_step")
        var_ready = sem("A_var_ready")
        std_ready = sem("A_std_ready")
        xn_ready = sem("A_xn_ready")
        transposed = sem("A_transposed")
        xnT_ready = sem("A_xnT_ready")
        out_ready = sem("A_out_ready")
        act_copied = sem("A_act_copied")
        lo_ready = sem("A_lo_ready")
        stored0 = sem("A_stored0")
        stored1 = sem("A_stored1")
        mean_ready = sem("A_mean_ready")
        z_dot = sem("A_z_dot")
        z_sum = sem("A_z_sum")
        z_exp = sem("A_z_exp")
        z_ready = sem("A_z_ready")
        z_stored = sem("A_z_stored")
        block = ctx.enter_context(nc.Block())
        x_loaded = (x_loaded0, x_loaded1)
        stored = (stored0, stored1)
        STORES = 5
        STEPS = NT + 2
        LOS = 2 * KD

        @block.sync
        def _(sp):
            for u in range(2):
                sp.dma_start(xin[:, u, :, :], xv[u]).then_inc(x_loaded[u], 16)
            for n, weight in enumerate((Wq, Wk, Wv)):
                sp.dma_start(w[:, n, :, :], weight.rearrange("(k p) n -> p k n", p=P)).then_inc(weights_loaded, 16)
            sp.dma_start(spanw[:, :, :], span_w.rearrange("(k p) h -> p k h", p=P)).then_inc(weights_loaded, 16)
            sp.dma_start(spanb[:, :], span_b.partition_broadcast(P)).then_inc(weights_loaded, 16)
            with sp.Fori(0, NBLK // 2) as i:
                for u in range(2):
                    blk = 2 * i + u
                    sp.wait_ge(xn_ready, blk + 1)
                    carry(sp, sp_carried)
                    sp.dma_start(xin[:, u, :, :], xv[(2 * i + 2 + u) % NBLK]).then_inc(x_loaded[u], 16)
                    sp.wait_ge(act_copied, (blk + 1) * OUT)
                    carry(sp, sp_carried)
                    sp.wait_ge(lo_ready, (blk + 2) * LOS)
                    for dst, src in ((q_hi, hi[:, u, 0:KD, :]), (q_lo, lo[:, u, 0:KD, :]),
                                     (k_hi, hi[:, u, KD:, :]), (k_lo, lo[:, u, KD:, :])):
                        sp.dma_start(dst[blk].rearrange("g p t -> p g t"), src.bitcast(F32)).then_inc(stored[u], 16)
                    sp.dma_start(v_sc[blk].rearrange("j p n -> p j n"), v[:, u, :, :]).then_inc(stored[u], 16)
            sp.wait_ge(z_ready, 4)
            sp.dma_start(z_sc, zt[0:1, 3, :, :].rearrange("a b h -> a (b h)")).then_inc(z_stored, 16)
            sp.wait_ge(z_stored, 16)
            for u in range(2):
                sp.wait_ge(stored[u], 16 * STORES * NBLK // 2)
                sp.wait_ge(x_loaded[u], 16 * (NBLK // 2 + 1))

        @block.gpsimd
        def _(pool):
            identity(pool, ident, zeroed, ident_ready)

        @block.vector
        def _(dve):
            def layer_norm(slot, n, loads):
                base = n * STEPS
                dve.wait_ge(x_loaded[slot], 16 * loads)
                for j in range(NT):
                    nc.vector.bn_stats(stats[:, j, :], xin[:, slot, j, :]).then_inc(dve_step, 1)
                dve.wait_ge(dve_step, base + NT)
                dve.wait_ge(xn_ready, n)
                carry(dve, dve_carried)
                for j in range(NT):
                    last = nc.vector.bn_aggr(mv[:, j, :], stats[:, j, :])
                last.then_inc(dve_step, 1)
                dve.wait_ge(dve_step, base + NT + 1)
                nc.vector.tensor_scalar_add(vare[:, :], mv[:, :, 1], EPS).then_inc(var_ready, 1)
                dve.wait_ge(std_ready, n + 1)
                nc.vector.reciprocal(rstd[:, :], std[:, :]).then_inc(dve_step, 1)
                dve.wait_ge(dve_step, base + NT + 2)
                dve.wait_ge(transposed, n)
                for j in range(NT):
                    last = nc.vector.tensor_scalar(xn[:, j, :], xin[:, slot, j, :], mv[:, j, 0:1],
                                                   rstd[:, j:j + 1], ALU.subtract, ALU.mult)
                last.then_inc(xn_ready, 1)

            dve.sem_inc(lo_ready, LOS)
            layer_norm(0, 0, 1)
            with dve.Fori(0, NBLK // 2) as i:
                for u in range(2):
                    blk = 2 * i + u
                    layer_norm(1 - u, blk + 1, i + 1 + u)
                    dve.wait_ge(stored[u], 16 * STORES * i)
                    for g in range(2 * KD):
                        dve.wait_ge(act_copied, blk * OUT + NT + g + 1)
                        nc.vector.tensor_tensor(lo[:, u, g, :], pO[:, (NT + g) % 4, :],
                                                hi[:, u, g, :].bitcast(F32), ALU.subtract).then_inc(lo_ready, 1)
            dve.wait_ge(xnT_ready, (NBLK + 1) * KD)
            for b in range(B):
                last = nc.vector.tensor_reduce(xm[:, b, :], xsum[:, :, b * BPB:(b + 1) * BPB], AX.X, ALU.add)
            last.then_inc(mean_ready, 1)
            dve.wait_ge(mean_ready, 1)
            nc.vector.tensor_scalar(xmb[:, :, :, :], xm[:, :, :].unsqueeze(3).broadcast_to([P, B, KD, P]), 1.0 / T, None,
                                    ALU.mult).then_inc(mean_ready, 1)
            dve.wait_ge(weights_loaded, 16 * 5)
            dve.wait_ge(z_dot, 1)
            nc.vector.tensor_tensor(zt[:, 0, :, :], pT[:, 0, 0:B * H].rearrange("p (b h) -> p b h", b=B),
                                    spanb[:, :].unsqueeze(1).broadcast_to([P, B, H]), ALU.add).then_inc(z_sum, 1)
            dve.wait_ge(z_exp, 1)
            nc.vector.tensor_scalar_add(zt[:, 2, :, :], zt[:, 1, :, :], 1.0).then_inc(z_ready, 1)
            dve.wait_ge(z_ready, 1)
            nc.vector.reciprocal(zt[:, 0, :, :], zt[:, 2, :, :]).then_inc(z_ready, 1)
            dve.wait_ge(z_ready, 2)
            nc.vector.tensor_scalar(zt[:, 3, :, :], zt[:, 0, :, :], T / RAMP, 1.0, ALU.mult, ALU.add).then_inc(z_ready, 2)

        @block.scalar
        def _(act):
            def root(n):
                act.wait_ge(var_ready, n + 1)
                nc.scalar.activation(std[:, :], vare[:, :], ACT.Sqrt).then_inc(std_ready, 1)

            def transposed_out(slot, n, done):
                act.wait_ge(transposed, n + 1)
                act.wait_ge(out_ready, done * OUT)
                for k in range(KD):
                    nc.scalar.activation(xnT[:, slot, k, :], pT[:, k, :], ACT.Copy,
                                         accum_out=xsum[:, k, bass.ds(n, 1)]).then_inc(xnT_ready, 1)

            def result_out(u, blk, g):
                act.wait_ge(out_ready, blk * OUT + g + 1)
                dst = v[:, u, g, :] if g < NT else hi[:, u, g - NT, :]
                nc.scalar.activation(dst, pO[:, g % 4, :], ACT.Copy).then_inc(act_copied, 1)

            root(0)
            transposed_out(0, 0, 0)
            with act.Fori(0, NBLK // 2) as i:
                for u in range(2):
                    blk = 2 * i + u
                    root(blk + 1)
                    act.wait_ge(stored[u], 16 * STORES * i)
                    for g in range(HALF):
                        result_out(u, blk, g)
                    transposed_out(1 - u, blk + 1, blk)
                    for g in range(HALF, OUT):
                        result_out(u, blk, g)
            act.wait_ge(z_sum, 1)
            nc.scalar.activation(zt[:, 1, :, :], zt[:, 0, :, :], ACT.Exp, scale=-1.0).then_inc(z_exp, 1)

        @block.tensor
        def _(pe):
            def transposes(n):
                pe.wait_ge(xn_ready, n + 1)
                pe.wait_ge(xnT_ready, n * KD)
                for k in range(KD):
                    for j in range(NT):
                        last = nc.tensor.transpose(pT[:, k, j * P:(j + 1) * P], xn[:, j, k * P:(k + 1) * P], ident[:, :])
                last.then_inc(transposed, 1)

            def product(u, blk, g):
                if g < 4:
                    pe.wait_ge(lo_ready, blk * LOS + LOS - 4 + g + 1)
                elif g - 4 < NT:
                    pe.wait_ge(act_copied, blk * OUT + g - 4 + 1)
                else:
                    pe.wait_ge(lo_ready, (blk + 1) * LOS + g - 4 - NT + 1)
                for k in range(KD):
                    if g < NT:
                        lhsT, rhs = xnT[:, u, k, g * P:(g + 1) * P], w[:, 2, k, :]
                    else:
                        n, m = divmod(g - NT, KD)
                        lhsT, rhs = w[:, n, k, m * P:(m + 1) * P], xnT[:, u, k, :]
                    last = nc.tensor.matmul(pO[:, g % 4, :], lhsT, rhs, start=(k == 0), stop=(k == KD - 1))
                last.then_inc(out_ready, 1)

            pe.wait_ge(ident_ready, 1)
            transposes(0)
            pe.wait_ge(weights_loaded, 16 * 5)
            with pe.Fori(0, NBLK // 2) as i:
                for u in range(2):
                    blk = 2 * i + u
                    pe.wait_ge(xnT_ready, (blk + 1) * KD)
                    for g in range(HALF):
                        product(u, blk, g)
                    transposes(blk + 1)
                    for g in range(HALF, OUT):
                        product(u, blk, g)
            pe.wait_ge(mean_ready, 2)
            for b in range(B):
                for k in range(KD):
                    last = nc.tensor.matmul(pT[:, 0, b * H:(b + 1) * H], xmb[:, b, k, :], spanw[:, k, :],
                                            start=(k == 0), stop=(k == KD - 1))
            last.then_inc(z_dot, 1)


KB = T // P
SCALE = float(DH) ** -0.5
SLOTS_E, SLOTS_EM = 4, 2
MBANKS, SBANKS = 4, 2
DEN_EPS = 1e-8


def attention_schedule():
    flat = [(qb, kb) for qb in range(BPB) for kb in range(NT * (qb + 1))]
    steps = len(flat)
    ends = [f for f, (qb, kb) in enumerate(flat) if kb == NT * (qb + 1) - 1]
    ahead, until = steps - 10, steps + 21
    units = [(qb, ("max", qb, qt, h, c)) for qb in range(BPB) for qt in range(NT) for h in range(HPG) for c in range(qb + 1)]
    slots = {f: [] for f in range(2 * steps + 2)}
    for n, (qb, unit) in enumerate(units):
        f = ahead + n * (until - ahead) // len(units)
        slots[f].append(unit)
        if n + 1 == len(units) or units[n + 1][0] != qb:
            slots[f].append(("rowmax", qb))
            slots[f + 1].append(("turn", qb))
            slots[f + 2].append(("rowdma", qb))
    before = [s for f in range(steps + 2) for s in slots[f]]
    before += [("score", f, h) for f in range(2) for h in range(HPG)] + [("span",), ("mask", 0, 0), ("mask", 0, 1)]
    body = []
    for f in range(2, steps + 2):
        mine = slots[f] + slots[f + steps]
        fixed = [("score", f, 0), ("score", f, 1), ("mask", f - 1, 0), ("mix", f - 2, 0), ("score", f, 2), ("mask", f - 1, 1),
                 ("mix", f - 2, 1), ("score", f, 3), ("mix", f - 2, 2)]
        if f - 1 == steps:
            fixed.insert(2, ("span",))
        gaps = [1, 3, 4, 6, 7, 8]
        for n, step in enumerate(fixed):
            body.append(step)
            for k in range(len(mine)):
                if gaps[min(k, 5)] == n:
                    body.append(mine[k])
        body += [("fill", 1 + n // HPG, n % HPG) for n in (2 * f - 4, 2 * f - 3) if n < (BPB - 1) * HPG]
        if f - 3 in ends and f > 4:
            body.append(("divide", flat[f - 3][0]))
        if flat[f - 2][1] == NT * (flat[f - 2][0] + 1) - 1:
            body.append(("out", flat[f - 2][0]))
    body.append(("divide", BPB - 1))
    return flat, before, body


def self_attention(nc, sem, q_hi, q_lo, k_hi, k_lo, v_sc, z_sc, a_sc):
    flat, before, body = attention_schedule()
    STEPS = len(flat)
    uses = lambda steps: sum(s[0] in ("max", "turn") for s in steps)
    U0, UNITS = uses(before), uses(body)
    R0 = sum(s[0] == "turn" for s in before)
    assert UNITS % MBANKS == 0 and STEPS % SLOTS_E == 0
    MROWS = 2 * HPG * NT
    FILLS = (BPB - 1) * HPG
    ITS = B * HG
    with ExitStack() as ctx:
        sb = lambda name, shape, dt: ctx.enter_context(nc.sbuf_tensor(name, shape, dt))
        ps = lambda name, shape, dt: ctx.enter_context(nc.psum_tensor(name, shape, dt))
        ident = sb("B_ident", [P, P], F32)
        identb = sb("B_identb", [P, P], BF16)
        later_k = sb("B_later_k", [P, P], BF16)
        later_q = sb("B_later_q", [P, P], BF16)
        ones = sb("B_ones", [P, DH], F32)
        tiny = sb("B_tiny", [P, DH], F32)
        disti = sb("B_disti", [P, T], I32)
        dist = sb("B_dist", [P, T], F32)
        spans = sb("B_spans", [P, B * H], F32)
        span = sb("B_span", [P, HPG], F32)
        qs = sb("B_qs", [P, BPB, HPG, BLK], F32R)
        ks = sb("B_ks", [P, BPB, HPG, BLK], F32R)
        v = sb("B_v", [P, KB, P], F32)
        mask = sb("B_mask", [P, HPG, T], F32)
        mx = sb("B_mx", [P, HPG, NT, BPB], F32)
        nm = sb("B_nm", [P, HPG * NT], F32)
        mm = sb("B_mm", [P, 2, HPG * NT], F32R)
        mrow = sb("B_mrow", [MROWS, P], F32R)
        e = sb("B_e", [P, SLOTS_E, HPG, BLK], F32)
        em = sb("B_em", [P, SLOTS_EM, HPG, BLK], F32)
        sums = sb("B_sums", [P, 2, BLK], F32)
        ao = sb("B_ao", [P, BLK], F32)
        pM = ps("B_pM", [P, MBANKS, BLK], F32)
        pS = ps("B_pS", [P, SBANKS, BLK], F32)
        pN = ps("B_pN", [P, BLK], F32)
        pD = ps("B_pD", [P, BLK], F32)
        sp_carried = sem("B_sp_carried")
        pool_carried = sem("B_pool_carried")
        made = sem("B_made")
        const_ready = sem("B_const_ready")
        spans_loaded = sem("B_spans_loaded")
        span_step = sem("B_span_step")
        chunk_loaded = [sem(f"B_chunk_loaded{c}") for c in range(BPB)]
        v_loaded = [sem(f"B_v_loaded{c}") for c in range(BPB)]
        max_ready = sem("B_max_ready")
        max_taken = sem("B_max_taken")
        neg_ready = sem("B_neg_ready")
        mrow_loaded = sem("B_mrow_loaded")
        score_ready = sem("B_score_ready")
        exp_ready = sem("B_exp_ready")
        mask_half = sem("B_mask_half")
        mask_ready = sem("B_mask_ready")
        masked = sem("B_masked")
        masked_last = sem("B_masked_last")
        mixed = sem("B_mixed")
        summed = sem("B_summed")
        inverse = sem("B_inverse")
        out_ready = sem("B_out_ready")
        stored = sem("B_stored")
        block = ctx.enter_context(nc.Block())

        def width(f):
            qb, kb = flat[f % STEPS]
            return max(0, (kb - NT * qb) * P)

        a_rows = a_sc.rearrange("k g p t -> (k g) p t")
        LOADS = 16 * 6
        q_rows, k_rows = [[t.rearrange("k g p t -> (k g) p t") for t in ts] for ts in ((q_hi, q_lo, q_hi), (k_hi, k_hi, k_lo))]

        @block.sync
        def _(sp):
            def load_rows(dst, srcs, g, c):
                for r, src in enumerate(srcs):
                    sp.dma_start(dst[r * DH:(r + 1) * DH, c, :, :].bitcast(F32),
                                 src[g + (BPB - 1) * HG * (g // HG) + c * HG].rearrange("(h d) t -> d h t", h=HPG)
                                 ).then_inc(chunk_loaded[c], 16)

            def load_v(g, c):
                sp.dma_start(v[:, c * NT:(c + 1) * NT, :],
                             v_sc[g // HG * BPB + c, :, :, bass.ds(g % HG * P, P)].rearrange("j p n -> p j n")
                             ).then_inc(v_loaded[c], 16)

            sp.dma_start(spans[:, :], z_sc[0].partition_broadcast(P)).then_inc(spans_loaded, 16)
            for c in range(BPB):
                load_rows(qs, q_rows, 0, c)
                load_rows(ks, k_rows, 0, c)
                load_v(0, c)
            with sp.Fori(0, ITS) as it:
                g = (it + 1) % ITS
                last = [("q", qb, f) for f, (qb, kb) in enumerate(flat) if kb == NT * (qb + 1) - 1 and qb < BPB - 1]
                last += [("k", kb // NT, f) for f, (qb, kb) in enumerate(flat) if qb == BPB - 1 and kb % NT == NT - 1]
                last.append(("q", BPB - 1, STEPS - 1))
                for kind, c, f in last:
                    sp.wait_ge(score_ready, it * HPG * STEPS + HPG * (f + 1))
                    carry(sp, sp_carried)
                    load_rows(*((qs, q_rows) if kind == "q" else (ks, k_rows)), g, c)
                    if kind == "k":
                        sp.wait_ge(mixed, (it + 1) * STEPS + f + 1)
                        carry(sp, sp_carried)
                        load_v(g, c)
                    if kind == "q":
                        sp.wait_ge(out_ready, it * BPB + c + 1)
                        carry(sp, sp_carried)
                        sp.dma_start(a_rows[it + (BPB - 1) * HG * (it // HG) + c * HG], ao[:, :]).then_inc(stored, 16)
            sp.wait_ge(stored, 16 * ITS * BPB)
            for c in range(BPB):
                sp.wait_ge(chunk_loaded[c], LOADS * (ITS + 1))
                sp.wait_ge(v_loaded[c], 16 * (ITS + 1))

        @block.gpsimd
        def _(pool):
            step = [0]

            def then(ins):
                step[0] += 1
                ins.then_inc(made, 1)
                pool.wait_ge(made, step[0])

            for tile in (ident, identb):
                then(pool.memset(tile[:, :], 0.0))
                then(pool.affine_select(out=tile[:, :], in_=tile[:, :], compare_op=ALU.not_equal, fill=1.0,
                                        base=0, pattern=[[-1, P]], channel_multiplier=1))
            for tile in (later_k, later_q):
                then(pool.memset(tile[:, :], 0.0))
                sign = 1 if tile is later_k else -1
                then(pool.affine_select(out=tile[:, :], in_=tile[:, :], compare_op=ALU.is_ge, fill=NEG,
                                        base=0, pattern=[[-sign, P]], channel_multiplier=sign))
            pool.sem_inc(const_ready, 1)
            for tile in (qs, ks):
                then(pool.memset(tile[3 * DH:P, :, :, :].bitcast(F32), 0.0))
            then(pool.memset(ks[3 * DH:3 * DH + 2, :, :, :].bitcast(F32), 1.0))
            then(pool.memset(ones[:, :], 1.0))
            then(pool.memset(tiny[:, :], DEN_EPS))
            then(pool.iota(disti[:, :], pattern=[[1, T]], base=0, channel_multiplier=-1))
            then(pool.tensor_copy(dist[:, :], disti[:, :]))
            pool.sem_inc(const_ready, 1)
            pool.sem_inc(masked_last, STEPS)

            def program(it, steps):
                for s in steps:
                    if s[0] == "fill":
                        _, c, h = s
                        n = it * FILLS + (c - 1) * HPG + h
                        t = slice(c * BLK, (c + 1) * BLK)
                        if (c, h) == (1, 0):
                            pool.wait_ge(span_step, 3 * (it + 1))
                            carry(pool, pool_carried)
                        pool.tensor_scalar(mask[:, h, t], dist[:, t], -1.0 / RAMP, span[:, h:h + 1], ALU.mult, ALU.add).then_inc(mask_half, 1)
                        pool.wait_ge(mask_half, n + 1)
                        carry(pool, pool_carried)
                        pool.tensor_scalar(mask[:, h, t], mask[:, h, t], 0.0, 1.0, ALU.max, ALU.min).then_inc(mask_ready, 1)
                    elif s[0] == "mask" and s[2] == 1:
                        f = s[1]
                        w0 = width(f)
                        qb, kb = flat[f % STEPS]
                        u0 = qb * BLK - kb * P + w0
                        if f % STEPS == 0:
                            pool.wait_ge(span_step, 3 * (it + f // STEPS + 1))
                        if kb == 0 and qb > 0:
                            pool.wait_ge(mask_ready, it * FILLS + qb * HPG)
                        pool.wait_ge(exp_ready, it * HPG * STEPS + HPG * (f + 1) + SBANKS)
                        pool.wait_ge(mixed, it * STEPS + STEPS + f + 1 - SLOTS_EM)
                        nc.gpsimd.tensor_tensor(em[:, f % SLOTS_EM, HPG - 1, w0:], e[:, f % SLOTS_E, HPG - 1, w0:],
                                                mask[:, HPG - 1, u0:u0 + BLK - w0], ALU.mult).then_inc(masked_last, 1)
                    elif s[0] == "divide":
                        n = it * BPB + s[1]
                        pool.wait_ge(inverse, n + 1)
                        pool.wait_ge(stored, 16 * n)
                        nc.gpsimd.tensor_tensor(ao[:, :], sums[:, 0, :], sums[:, 1, :], ALU.mult).then_inc(out_ready, 1)

            program(0, before)
            with pool.Fori(0, ITS) as it:
                program(it, body)

        @block.vector
        def _(dve):
            dve.sem_inc(max_taken, MBANKS)

            def program(it, steps, unit, rm):
                for s in steps:
                    if s[0] == "max":
                        _, qb, qt, h, c = s
                        w = BLK if c < qb else (qt + 1) * P
                        dve.wait_ge(max_ready, it * UNITS + unit + 1)
                        nc.vector.tensor_reduce(mx[:, h, qt, c:c + 1], pM[:, unit % MBANKS, 0:w], AX.X, ALU.max).then_inc(max_taken, 1)
                        unit += 1
                    elif s[0] == "rowmax":
                        qb = s[1]
                        base = 3 * (it * BPB + rm)
                        dve.wait_ge(max_taken, it * UNITS + unit + MBANKS)
                        nc.vector.tensor_reduce(nm[:, :].rearrange("p (h q) -> p h q", h=HPG), mx[:, :, :, 0:qb + 1],
                                                AX.X, ALU.max, negate=True).then_inc(neg_ready, 1)
                        dve.wait_ge(neg_ready, base + 1)
                        nc.vector.tensor_copy(mm[:, 0, :], nm[:, :]).then_inc(neg_ready, 1)
                        dve.wait_ge(neg_ready, base + 2)
                        nc.vector.tensor_tensor(mm[:, 1, :], nm[:, :], mm[:, 0, :].bitcast(F32), ALU.subtract).then_inc(neg_ready, 1)
                    elif s[0] == "turn":
                        dve.wait_ge(max_ready, it * UNITS + unit + 1)
                        if not (isinstance(it, int) and rm == 0):
                            dve.wait_ge(mrow_loaded, 32 * (it * BPB + rm))
                        nc.vector.tensor_copy(mrow[:, :], pM[0:MROWS, unit % MBANKS, 0:P]).then_inc(max_taken, 1)
                        unit += 1
                        rm += 1
                    elif s[0] == "span":
                        n = it if isinstance(it, int) else it + 1
                        dve.wait_ge(masked, 2 * STEPS * (n + 1))
                        dve.wait_ge(masked_last, STEPS * (n + 1))
                        if isinstance(it, int):
                            dve.wait_ge(const_ready, 2)
                            dve.wait_ge(spans_loaded, 16)
                        if not isinstance(it, int):
                            dve.wait_ge(mask_ready, FILLS * n)
                        at = 0 if isinstance(it, int) else n % ITS * HPG
                        nc.vector.tensor_copy(span[:, :], spans[:, bass.ds(at, HPG)]).then_inc(span_step, 1)
                        dve.wait_ge(span_step, 3 * n + 1)
                        for h in range(HPG):
                            last = nc.vector.tensor_scalar(mask[:, h, 0:BLK], dist[:, 0:BLK], -1.0 / RAMP, span[:, h:h + 1], ALU.mult, ALU.add)
                        last.then_inc(span_step, 1)
                        dve.wait_ge(span_step, 3 * n + 2)
                        nc.vector.tensor_scalar(mask[:, :, 0:BLK], mask[:, :, 0:BLK], 0.0, 1.0, ALU.max, ALU.min).then_inc(span_step, 1)
                        dve.wait_ge(span_step, 3 * n + 3)
                    elif s[0] == "divide":
                        n = it * BPB + s[1]
                        dve.wait_ge(summed, n + 1)
                        nc.vector.reciprocal(sums[:, 1, :], sums[:, 1, :]).then_inc(inverse, 1)
                    elif s[0] == "mask":
                        _, f, pair = s
                        w0 = width(f)
                        qb, kb = flat[f % STEPS]
                        u0 = qb * BLK - kb * P + w0
                        hs = slice(2 * pair, min(2 * pair + 2, HPG - 1))
                        dve.wait_ge(exp_ready, it * HPG * STEPS + HPG * f + hs.stop + SBANKS)
                        if kb == 0 and qb > 0 and pair == 0:
                            dve.wait_ge(mask_ready, it * FILLS + qb * HPG)
                        if pair == 0:
                            dve.wait_ge(mixed, it * STEPS + STEPS + f + 1 - SLOTS_EM)
                        nc.vector.tensor_tensor(em[:, f % SLOTS_EM, hs, w0:], e[:, f % SLOTS_E, hs, w0:],
                                                mask[:, hs, u0:u0 + BLK - w0], ALU.mult).then_inc(masked, 1)

            dve.sem_inc(masked, 2 * STEPS)
            program(0, before, 0, 0)
            with dve.Fori(0, ITS) as it:
                program(it, body, U0, R0)

        @block.scalar
        def _(act):
            act.wait_ge(const_ready, 2)
            act.sem_inc(exp_ready, SBANKS)

            def program(it, steps, unit, turned):
                for s in steps:
                    if s[0] == "max":
                        unit += 1
                    elif s[0] == "turn":
                        unit += 1
                        turned = unit
                    elif s[0] == "rowdma":
                        act.wait_ge(max_taken, it * UNITS + turned + MBANKS)
                        for part in range(2):
                            act.dma_start(qs[3 * DH + part:3 * DH + part + 1, s[1], :, :].bitcast(F32),
                                          mrow[part * HPG * NT:(part + 1) * HPG * NT, :].bitcast(F32)
                                          ).then_inc(mrow_loaded, 16)
                    elif s[0] == "score":
                        _, f, h = s
                        w0 = width(f)
                        if h == 0:
                            act.wait_ge(mixed, it * STEPS + STEPS + f + 1 - SLOTS_E)
                        act.wait_ge(score_ready, it * HPG * STEPS + HPG * f + h + 1)
                        nc.scalar.activation(e[:, f % SLOTS_E, h, w0:], pS[:, h % SBANKS, w0:],
                                             ACT.Exp, scale=SCALE).then_inc(exp_ready, 1)
                    elif s[0] == "out":
                        qb = s[1]
                        act.wait_ge(mixed, it * STEPS + STEPS + flat.index((qb, NT * (qb + 1) - 1)) + 1)
                        n = it * BPB + qb
                        act.wait_ge(out_ready, n)
                        nc.scalar.activation(sums[:, 0, :], pN[:, :], ACT.Copy)
                        nc.scalar.activation(sums[:, 1, :], pD[:, :], ACT.Copy).then_inc(summed, 1)

            program(0, before, 0, 0)
            with act.Fori(0, ITS) as it:
                program(it, body, U0, uses(before[:max(n for n, s in enumerate(before) if s[0] == "turn") + 1]))
            act.wait_ge(mrow_loaded, 32 * (sum(s[0] == "rowdma" for s in before) + ITS * BPB))

        @block.tensor
        def _(pe):
            pe.wait_ge(const_ready, 1)
            pe.sem_inc(mixed, STEPS)

            def program(it, steps, unit, rm):
                for s in steps:
                    if s[0] == "max":
                        _, qb, qt, h, c = s
                        w = BLK if c < qb else (qt + 1) * P
                        if (qt, h, c) == (0, 0, 0):
                            n = 1 if isinstance(it, int) else it + 1 + next_group[qb]
                            pe.wait_ge(chunk_loaded[qb], LOADS * n)
                        pe.wait_ge(max_taken, it * UNITS + unit + 1)
                        last = nc.tensor.matmul(pM[:, unit % MBANKS, 0:w], qs[0:3 * DH, qb, h, qt * P:(qt + 1) * P], ks[0:3 * DH, c, h, 0:w],
                                                start=True, stop=(c < qb))
                        if c == qb:
                            last = nc.tensor.matmul(pM[:, unit % MBANKS, w - P:w], identb[:, :], later_k[:, :], start=False, stop=True)
                        last.then_inc(max_ready, 1)
                        unit += 1
                    elif s[0] == "turn":
                        pe.wait_ge(max_taken, it * UNITS + unit + 1)
                        pe.wait_ge(neg_ready, 3 * (it * BPB + rm + 1))
                        nc.tensor.transpose(pM[0:MROWS, unit % MBANKS, 0:P], mm[:, :, :].bitcast(F32).rearrange("p a b -> p (a b)"),
                                            ident[:, :]).then_inc(max_ready, 1)
                        unit += 1
                        rm += 1
                    elif s[0] == "score":
                        _, f, h = s
                        w0 = width(f)
                        qb, kb = flat[f % STEPS]
                        if isinstance(it, int) and (f, h) == (0, 0):
                            pe.wait_ge(const_ready, 2)
                        if kb == 0 and h == 0:
                            pe.wait_ge(mrow_loaded, 32 * (it * BPB + f // STEPS * BPB + qb + 1))
                        pe.wait_ge(exp_ready, it * HPG * STEPS + HPG * f + h + 1)
                        last = nc.tensor.matmul(pS[:, h % SBANKS, w0:], ks[:, kb // NT, h, kb % NT * P:(kb % NT + 1) * P],
                                                qs[:, qb, h, w0:], start=True, stop=(kb < NT * qb))
                        if kb >= NT * qb:
                            last = nc.tensor.matmul(pS[:, h % SBANKS, w0:w0 + P], identb[:, :], later_q[:, :],
                                                    start=False, stop=True)
                        last.then_inc(score_ready, 1)
                    elif s[0] == "mix":
                        _, f, part = s
                        w0 = width(f)
                        qb, kb = flat[f]
                        first, final = kb == 0, kb == NT * (qb + 1) - 1
                        if part == 0:
                            if kb == NT * qb:
                                pe.wait_ge(v_loaded[qb], 16 * (it + 1))
                            if first:
                                pe.wait_ge(summed, it * BPB + qb)
                            pe.wait_ge(masked, it * 2 * STEPS + 2 * STEPS + 2 * (f + 1))
                            pe.wait_ge(masked_last, it * STEPS + STEPS + f + 1)
                        out, weights, values = ((pN, None, em[:, f % SLOTS_EM]), (pD, ones, em[:, f % SLOTS_EM]),
                                                (pD, tiny, e[:, f % SLOTS_E]))[part]
                        for h in range(HPG):
                            cols = slice(h * DH, (h + 1) * DH)
                            last = nc.tensor.matmul(out[cols, w0:], v[:, kb, cols] if part == 0 else weights[:, :], values[:, h, w0:],
                                                    start=first and part < 2, stop=final and part != 1, tile_position=(0, h * DH))
                        if part == 2:
                            last.then_inc(mixed, 1)

            next_group = {qb: int(("max", qb, 0, 0, 0) in before) for qb in range(BPB)}
            program(0, before, 0, 0)
            with pe.Fori(0, ITS) as it:
                program(it, body, U0, R0)


XH, XDH = 8, 128
CL, CD = 77, 384
KC = CD // P
KEYS = B * CL
HB = BLK // KEYS
GROUPS = [(h, min(h + HB, XH)) for h in range(0, XH, HB)]
XK = XH * KEYS
XT = -(-XK // P)
XSCALE = float(XDH) ** -0.5
SHARPEN = 1.5
NS = 16
HS = H * NS
MS = HS // P
TILES = B * T // P


def fold_weights(nc, sem, spare, ctx768, Wq, Wk, Wv, Wout, slot_query, d_Wq, d_Wk, d_bq, d_bk, vw_sc, wkx, vwo, dqk, dqb):
    with ExitStack() as ctx:
        sb = lambda name, shape, dt: ctx.enter_context(nc.sbuf_tensor(name, shape, dt))
        wq = spare[:, 0, :].rearrange("p (k n) -> p k n", k=KD)
        wo = spare[:, 1, :].rearrange("p (h n) -> p h n", h=XH)
        wqT = spare[:, 2, :].rearrange("p (h n) -> p h n", h=XH)
        slot_weights = spare[:, 3, :].rearrange("p (w k n) -> p w k n", w=2, n=D)
        dwq, dwk = slot_weights[:, 0, :, :], slot_weights[:, 1, :, :]
        ident = sb("W_ident", [P, P], F32)
        cx = sb("W_cx", [CL, B, CD], F32)
        wk = sb("W_wk", [P, KC, XH * XDH], F32)
        wv = sb("W_wv", [P, KC, XH * XDH], F32)
        sq = sb("W_sq", [NS, D], F32)
        dbq = sb("W_dbq", [P, KD], F32)
        dbk = sb("W_dbk", [P, KD], F32)
        cT = sb("W_cT", [P, KC, KEYS], F32)
        kT = sb("W_kT", [P, XH, KEYS], F32)
        ksum = sb("W_ksum", [P, XH], F32)
        kmean = sb("W_kmean", [P, XH], F32)
        kS = sb("W_kS", [P, XH, KEYS], F32)
        vT = sb("W_vT", [P, XH, KEYS], F32)
        vw = sb("W_vw", [CL, XH, B, D], F32)
        sqT = sb("W_sqT", [P, KD, NS], F32)
        sqh = sb("W_sqh", [P, KD, NS], F32)
        qbd = sb("W_qbd", [P, KD, HPG, NS], F32)
        dwkT = sb("W_dwkT", [P, KD, D], F32)
        bank = [ctx.enter_context(nc.psum_tensor(f"W_bank{n}", [P, BLK], F32)) for n in range(8)]
        zeroed = sem("W_zeroed")
        ident_ready = sem("W_ident_ready")
        loaded = [sem(f"W_loaded{n}") for n in range(6)]
        made = sem("W_made")
        taken = sem("W_taken")
        step = sem("W_step")
        bd_zero = sem("W_bd_zero")
        vw_stored = sem("W_vw_stored")
        vwo_loaded = sem("W_vwo_loaded")
        block = ctx.enter_context(nc.Block())

        names = (["cT"] + [("kT", g) for g in range(len(GROUPS))] + [("vT", g) for g in range(len(GROUPS))]
                 + [("wqT", h) for h in range(XH)] + [("wkx", k, g) for k in range(KD) for g in range(len(GROUPS))]
                 + [("vw", h, b) for h in range(XH) for b in range(B)] + ["sqT", "sqh"]
                 + [("dwkT", m) for m in range(KD)] + [("dqk", k) for k in range(0, KD, 2)] + ["dqb"])
        nth = {name: n for n, name in enumerate(names)}

        @block.sync
        def _(sp):
            sp.dma_start(cx[:, :, :], ctx768.rearrange("b l c -> l b c")).then_inc(loaded[0], 16)
            sp.dma_start(wk[:, :, :], Wk.rearrange("(k p) n -> p k n", p=P)).then_inc(loaded[1], 16)
            sp.dma_start(wv[:, :, :], Wv.rearrange("(k p) n -> p k n", p=P)).then_inc(loaded[1], 16)
            sp.dma_start(wq[:, :, :], Wq.rearrange("(k p) n -> p k n", p=P)).then_inc(loaded[2], 16)
            sp.dma_start(wo[:, :, :], Wout.rearrange("(h p) n -> p h n", p=P)).then_inc(loaded[3], 16)
            sp.dma_start(sq[:, :], slot_query[0]).then_inc(loaded[4], 16)
            for dst, src in ((dbq, d_bq), (dbk, d_bk)):
                sp.dma_start(dst[:, :], src.rearrange("(k p) -> p k", p=P), allow_slow_non_contiguous=True).then_inc(loaded[4], 16)
            sp.dma_start(dwq[:, :, :], d_Wq.rearrange("(k p) n -> p k n", p=P)).then_inc(loaded[5], 16)
            sp.dma_start(dwk[:, :, :], d_Wk.rearrange("(k p) n -> p k n", p=P)).then_inc(loaded[5], 16)
            sp.wait_ge(taken, nth[("vw", XH - 1, B - 1)] + 1)
            sp.dma_start(vw_sc.rearrange("(h b l) n -> l h b n", h=XH, b=B), vw[:, :, :, :]).then_inc(vw_stored, 16)
            sp.wait_ge(vw_stored, 16)
            full = XK // P
            sp.dma_start(vwo[:, 0:full, :], vw_sc[0:full * P, :].rearrange("(t p) n -> p t n", p=P)).then_inc(vwo_loaded, 16)
            sp.dma_start(vwo[0:XK - full * P, full, :], vw_sc[full * P:XK, :]).then_inc(vwo_loaded, 16)
            sp.wait_ge(vwo_loaded, 32)

        @block.gpsimd
        def _(pool):
            identity(pool, ident, zeroed, ident_ready)
            pool.memset(qbd[:, :, :, :], 0.0).then_inc(bd_zero, 1)

        @block.vector
        def _(dve):
            def take(name, dst, src):
                dve.wait_ge(made, nth[name] + 1)
                nc.vector.tensor_copy(dst, src).then_inc(taken, 1)

            take("cT", cT[:, :, :], bank[0][:, 0:KC * KEYS].rearrange("p (k c) -> p k c", k=KC))
            for kind, dst in (("kT", kT), ("vT", vT)):
                for g, (h0, h1) in enumerate(GROUPS):
                    take((kind, g), dst[:, h0:h1, :],
                         bank[nth[(kind, g)] % 8][:, 0:(h1 - h0) * KEYS].rearrange("p (h c) -> p h c", c=KEYS))
            dve.wait_ge(taken, nth[("kT", len(GROUPS) - 1)] + 1)
            nc.vector.tensor_reduce(ksum[:, :], kT[:, :, :], AX.X, ALU.add).then_inc(step, 1)
            dve.wait_ge(step, 1)
            nc.vector.tensor_scalar(kmean[:, :], ksum[:, :], (1.0 - SHARPEN) / KEYS, None, ALU.mult).then_inc(step, 1)
            dve.wait_ge(step, 2)
            for h in range(XH):
                last = nc.vector.tensor_scalar(kS[:, h, :], kT[:, h, :], SHARPEN, kmean[:, h:h + 1], ALU.mult, ALU.add)
            last.then_inc(step, 1)
            for h in range(XH):
                take(("wqT", h), wqT[:, h, :], bank[nth[("wqT", h)] % 8][:, :])
            for k in range(KD):
                for g, (h0, h1) in enumerate(GROUPS):
                    take(("wkx", k, g), wkx[:, k, h0 * KEYS:h1 * KEYS], bank[nth[("wkx", k, g)] % 8][:, 0:(h1 - h0) * KEYS])
            for h in range(XH):
                for b in range(B):
                    take(("vw", h, b), vw[:, h, b, :], bank[nth[("vw", h, b)] % 8][0:CL, :])
            take("sqT", sqT[:, :, :], bank[nth["sqT"] % 8][:, 0:KD * NS].rearrange("p (k s) -> p k s", k=KD))
            dve.wait_ge(loaded[4], 48)
            dve.wait_ge(made, nth["sqh"] + 1)
            nc.vector.tensor_tensor(sqh[:, :, :], bank[nth["sqh"] % 8][:, 0:KD * NS].rearrange("p (k s) -> p k s", k=KD),
                                    dbq[:, :].unsqueeze(2).broadcast_to([P, KD, NS]), ALU.add).then_inc(taken, 1)
            dve.wait_ge(taken, nth["sqh"] + 1)
            dve.wait_ge(bd_zero, 1)
            for j in range(HPG):
                r = slice(j * DH, (j + 1) * DH)
                last = nc.vector.tensor_copy(qbd[r, :, j, :], sqh[r, :, :])
            last.then_inc(step, 1)
            for m in range(KD):
                take(("dwkT", m), dwkT[:, m, :], bank[nth[("dwkT", m)] % 8][:, :])
            for k in range(0, KD, 2):
                take(("dqk", k), dqk[:, k:k + 2, :], bank[nth[("dqk", k)] % 8][:, :].rearrange("p (k n) -> p k n", k=2))
            take("dqb", dqb[:, :], bank[nth["dqb"] % 8][:, 0:MS])

        @block.tensor
        def _(pe):
            def into(name):
                n = nth[name]
                if n >= 8:
                    pe.wait_ge(taken, n - 7)
                return bank[n % 8]

            pe.wait_ge(ident_ready, 1)
            pe.wait_ge(loaded[0], 16)
            o = into("cT")
            for k in range(KC):
                for b in range(B):
                    c0 = k * KEYS + b * CL
                    last = nc.tensor.transpose(o[:, c0:c0 + CL], cx[:, b, k * P:(k + 1) * P], ident[0:CL, 0:CL])
            last.then_inc(made, 1)
            pe.wait_ge(taken, nth["cT"] + 1)
            pe.wait_ge(loaded[1], 32)
            for kind, weight in (("kT", wk), ("vT", wv)):
                for g, (h0, h1) in enumerate(GROUPS):
                    o = into((kind, g))
                    for h in range(h0, h1):
                        for k in range(KC):
                            last = nc.tensor.matmul(o[:, (h - h0) * KEYS:(h - h0 + 1) * KEYS], weight[:, k, h * XDH:(h + 1) * XDH],
                                                    cT[:, k, :], start=(k == 0), stop=(k == KC - 1))
                    last.then_inc(made, 1)
            pe.wait_ge(loaded[2], 16)
            for h in range(XH):
                o = into(("wqT", h))
                for k in range(KD):
                    last = nc.tensor.transpose(o[:, k * P:(k + 1) * P], wq[:, k, h * XDH:(h + 1) * XDH], ident[:, :])
                last.then_inc(made, 1)
            pe.wait_ge(taken, nth[("wqT", XH - 1)] + 1)
            pe.wait_ge(step, 3)
            for k in range(KD):
                for g, (h0, h1) in enumerate(GROUPS):
                    o = into(("wkx", k, g))
                    for h in range(h0, h1):
                        last = nc.tensor.matmul(o[:, (h - h0) * KEYS:(h - h0 + 1) * KEYS], wqT[:, h, k * P:(k + 1) * P],
                                                kS[:, h, :], start=True, stop=True)
                    last.then_inc(made, 1)
            pe.wait_ge(loaded[3], 16)
            for h in range(XH):
                for b in range(B):
                    o = into(("vw", h, b))
                    nc.tensor.matmul(o[0:CL, :], vT[:, h, b * CL:(b + 1) * CL], wo[:, h, :], start=True, stop=True
                                     ).then_inc(made, 1)
            pe.wait_ge(loaded[4], 48)
            o = into("sqT")
            for k in range(KD):
                last = nc.tensor.transpose(o[:, k * NS:(k + 1) * NS], sq[:, k * P:(k + 1) * P], ident[0:NS, 0:NS])
            last.then_inc(made, 1)
            pe.wait_ge(taken, nth["sqT"] + 1)
            pe.wait_ge(loaded[5], 32)
            o = into("sqh")
            for m in range(KD):
                for k in range(KD):
                    last = nc.tensor.matmul(o[:, m * NS:(m + 1) * NS], dwq[:, k, m * P:(m + 1) * P], sqT[:, k, :],
                                            start=(k == 0), stop=(k == KD - 1))
            last.then_inc(made, 1)
            for m in range(KD):
                o = into(("dwkT", m))
                for k in range(KD):
                    last = nc.tensor.transpose(o[:, k * P:(k + 1) * P], dwk[:, k, m * P:(m + 1) * P], ident[:, :])
                last.then_inc(made, 1)
            pe.wait_ge(taken, nth[("dwkT", KD - 1)] + 1)
            pe.wait_ge(step, 4)
            for k in range(0, KD, 2):
                o = into(("dqk", k))
                for kk in range(2):
                    for m in range(KD):
                        c0 = kk * HS + m * HPG * NS
                        last = nc.tensor.matmul(o[:, c0:c0 + HPG * NS], dwkT[:, m, (k + kk) * P:(k + kk + 1) * P],
                                                qbd[:, m, :, :].rearrange("p j s -> p (j s)"), start=True, stop=True)
                last.then_inc(made, 1)
            o = into("dqb")
            for m in range(KD):
                r = m % 2 * HPG * NS
                last = nc.tensor.matmul(o[r:r + HPG * NS, m // 2:m // 2 + 1], qbd[:, m, :, :].rearrange("p j s -> p (j s)"),
                                        dbk[:, m:m + 1], start=True, stop=True, tile_position=(0, r))
            last.then_inc(made, 1)


LAG_B, LAG_C, LAG_D = 1, 2, 3


def at_least(eng, sem, value):
    if not (isinstance(value, int) and value <= 0):
        eng.wait_ge(sem, value)


def ticks(eng, body):
    there = lambda t: 0 <= t < TILES
    for n in range(NT):
        body(0, n, there)
    with eng.Fori(1, TILES // NT) as i:
        for j in range(NT):
            body(i, j, lambda t: True)
    for n in range(TILES, TILES + LAG_D):
        body(n // NT, n % NT, there)


def upto(value, most=TILES):
    return min(value, most) if isinstance(value, int) else value


def cross_attention(nc, sem, x, a_sc, Wo, Wo_b, bout, wkx, vwo, dqk, dqb, x2_sc, xn_sc, xT_sc, s_sc):
    xv = x.rearrange("b (t p) d -> (b t) p d", p=P)
    with ExitStack() as ctx:
        sb = lambda name, shape, dt: ctx.enter_context(nc.sbuf_tensor(name, shape, dt))
        ps = lambda name, shape, dt: ctx.enter_context(nc.psum_tensor(name, shape, dt))
        ident = sb("C_ident", [P, P], F32)
        power = sb("C_power", [P, 1], F32)
        wo = sb("C_wo", [P, HG, D], F32)
        wob = sb("C_wob", [P, D], F32)
        bob = sb("C_bob", [P, D], F32)
        xin = sb("C_xin", [P, NT, D], F32)
        aT = sb("C_aT", [P, NT, HG, P], F32)
        x1 = sb("C_x1", [P, 2, D], F32)
        x1b = sb("C_x1b", [P, NT, D], F32)
        stats = [sb(f"C_stats{s}", [P, 6], F32) for s in range(2)]
        mv = [sb(f"C_mv{s}", [P, 2], F32) for s in range(2)]
        vare = [sb(f"C_vare{s}", [P, 1], F32) for s in range(2)]
        rstd = [sb(f"C_rstd{s}", [P, 1], F32) for s in range(2)]
        xn2 = sb("C_xn2", [P, D], F32)
        xn2T = sb("C_xn2T", [P, 2, KD, P], F32)
        mx = sb("C_mx", [P, XH], F32)
        nmx = sb("C_nmx", [P, XH], F32)
        total = sb("C_total", [P, 2, XH], F32)
        inv = sb("C_inv", [P, XH], F32)
        prob = sb("C_prob", [P, 2, XH, KEYS], F32)
        probT = sb("C_probT", [P, 2, XT, P], F32)
        x2 = sb("C_x2", [P, 2, D], F32)
        xn3 = sb("C_xn3", [P, 2, D], F32)
        xn3T = sb("C_xn3T", [P, 2, KD, P], F32)
        pA = ps("C_pA", [P, BLK], F32)
        pX = ps("C_pX", [P, BLK], F32)
        pS = ps("C_pS", [P, len(GROUPS), BLK], F32)
        pP = ps("C_pP", [P, 2, BLK], F32)
        pO = ps("C_pO", [P, BLK], F32)
        sp_carried = sem("C_sp_carried")
        dve_carried = sem("C_dve_carried")
        zeroed = sem("C_zeroed")
        ident_ready = sem("C_ident_ready")
        weights_loaded = sem("C_weights_loaded")
        tile_loaded = [sem(f"C_tile_loaded{s}") for s in range(NT)]
        xb_ready = sem("C_xb_ready")
        projected = sem("C_projected")
        x1_ready = sem("C_x1_ready")
        x1b_ready = sem("C_x1b_ready")
        ln_step = [sem(f"C_ln_step{s}") for s in range(2)]
        var_ready = [sem(f"C_var_ready{s}") for s in range(2)]
        rstd_ready = [sem(f"C_rstd_ready{s}") for s in range(2)]
        xn_ready = [sem(f"C_xn_ready{s}") for s in range(2)]
        turned = [sem(f"C_turned{s}") for s in range(2)]
        xT_ready = [sem(f"C_xT_ready{s}") for s in range(2)]
        score_ready = sem("C_score_ready")
        max_step = sem("C_max_step")
        nmx_ready = sem("C_nmx_ready")
        exp_ready = sem("C_exp_ready")
        inv_ready = sem("C_inv_ready")
        prob_ready = sem("C_prob_ready")
        prob_turned = sem("C_prob_turned")
        probT_ready = sem("C_probT_ready")
        out_ready = sem("C_out_ready")
        x2_ready = sem("C_x2_ready")
        slot_ready = sem("C_slot_ready")
        slot_taken = sem("C_slot_taken")
        stored = [sem(f"C_stored{s}") for s in range(2)]
        storedT = [sem(f"C_storedT{s}") for s in range(2)]
        block = ctx.enter_context(nc.Block())

        TP = [range(k, min(k + NT, XT)) for k in range(0, XT, NT)]
        NP = len(TP)
        WAIT_W = 16 * 3

        @block.sync
        def _(sp):
            def load_at(blk, j):
                blk = blk % NBLK
                sp.dma_start(xin[:, j, :], xv[blk * NT + j]).then_inc(tile_loaded[j], 16)
                sp.dma_start(aT[:, j, :, :], a_sc[blk, :, :, j * P:(j + 1) * P].rearrange("g p t -> p g t")
                             ).then_inc(tile_loaded[j], 16)

            load_at(0, 0)
            sp.dma_start(wob[:, :], Wo_b.partition_broadcast(P)).then_inc(weights_loaded, 16)
            sp.dma_start(bob[:, :], bout.partition_broadcast(P)).then_inc(weights_loaded, 16)
            sp.dma_start(wo[:, :, :], Wo.rearrange("(g p) n -> p g n", p=P)).then_inc(weights_loaded, 16)
            for j in range(1, NT - 1):
                load_at(0, j)

            def tick(i, j, valid):
                n = NT * i + j
                a, c, d = n, n - LAG_C, n - LAG_D
                if valid(a):
                    at_least(sp, x1_ready, a)
                    carry(sp, sp_carried)
                    load_at(i if j == 0 else i + 1, (j + NT - 1) % NT)
                if valid(c):
                    sp.wait_ge(xn_ready[1], c + 1)
                    sp.dma_start(x2_sc[c], x2[:, j % 2, :]).then_inc(stored[j % 2], 16)
                    sp.dma_start(xn_sc[c], xn3[:, j % 2, :]).then_inc(stored[j % 2], 16)
                if valid(d):
                    s = (j + 1) % 2
                    sp.wait_ge(xT_ready[1], d + 1)
                    sp.dma_start(xT_sc[d], xn3T[:, s, :, :]).then_inc(storedT[s], 16)

            ticks(sp, tick)
            for s in range(2):
                sp.wait_ge(stored[s], 32 * TILES // 2)
                sp.wait_ge(storedT[s], 16 * TILES // 2)
            for j in range(NT - 1):
                sp.wait_ge(tile_loaded[j], 32 * (NBLK + 1))

        @block.gpsimd
        def _(pool):
            identity(pool, ident, zeroed, ident_ready)
            pool.memset(power[:, :], -0.5).then_inc(zeroed, 1)
            pool.wait_ge(zeroed, 2)
            pool.wait_ge(weights_loaded, WAIT_W)

            def root(s, t):
                pool.wait_ge(var_ready[s], t + 1)
                nc.gpsimd.tensor_tensor(rstd[s][:, :], vare[s][:, :], power[:, :], ALU.pow).then_inc(rstd_ready[s], 1)

            def tick(i, j, valid):
                n = NT * i + j
                a, b, c = n, n - LAG_B, n - LAG_C
                if valid(a):
                    pool.wait_ge(tile_loaded[j], 32 * (i + 1))
                    nc.gpsimd.tensor_tensor(xin[:, j, :], xin[:, j, :], wob[:, :], ALU.add).then_inc(xb_ready, 1)
                    root(0, a)
                    pool.wait_ge(x1_ready, a + 1)
                    nc.gpsimd.tensor_tensor(x1b[:, j, :], x1[:, j % 2, :], bob[:, :], ALU.add).then_inc(x1b_ready, 1)
                if valid(b):
                    s = (j + 1) % 2
                    pool.wait_ge(inv_ready, b + 1)
                    nc.gpsimd.tensor_tensor(prob[:, s, :, :], prob[:, s, :, :],
                                            inv[:, :].unsqueeze(2).broadcast_to([P, XH, KEYS]), ALU.mult).then_inc(prob_ready, 1)
                if valid(c):
                    root(1, c)

            ticks(pool, tick)

        @block.vector
        def _(dve):
            def layer_norm(s, t, src, dst, free_dst):
                nc.vector.bn_stats(stats[s][:, :], src).then_inc(ln_step[s], 1)
                dve.wait_ge(ln_step[s], 2 * t + 1)
                at_least(dve, xn_ready[s], t)
                carry(dve, dve_carried)
                nc.vector.bn_aggr(mv[s][:, :], stats[s][:, :]).then_inc(ln_step[s], 1)
                dve.wait_ge(ln_step[s], 2 * t + 2)
                nc.vector.tensor_scalar_add(vare[s][:, :], mv[s][:, 1:2], EPS).then_inc(var_ready[s], 1)
                dve.wait_ge(rstd_ready[s], t + 1)
                free_dst()
                nc.vector.tensor_scalar(dst, src, mv[s][:, 0:1], rstd[s][:, 0:1], ALU.subtract, ALU.mult
                                        ).then_inc(xn_ready[s], 1)

            def tick(i, j, valid):
                n = NT * i + j
                a, b, c = n, n - LAG_B, n - LAG_C
                if valid(b):
                    dve.wait_ge(score_ready, b + 1)
                    for g, (h0, h1) in enumerate(GROUPS):
                        last = nc.vector.tensor_reduce(mx[:, h0:h1], pS[:, g, 0:(h1 - h0) * KEYS].rearrange("p (h c) -> p h c", c=KEYS),
                                                       AX.X, ALU.max)
                    last.then_inc(max_step, 1)
                    dve.wait_ge(max_step, b + 1)
                    at_least(dve, exp_ready, b)
                    nc.vector.tensor_scalar(nmx[:, :], mx[:, :], -XSCALE, None, ALU.mult).then_inc(nmx_ready, 1)
                if valid(a):
                    dve.wait_ge(projected, a + 1)
                    dve.wait_ge(xb_ready, a + 1)
                    at_least(dve, x1b_ready, a - 1)
                    nc.vector.tensor_tensor(x1[:, j % 2, :], pA[:, :], xin[:, j, :], ALU.add).then_inc(x1_ready, 1)
                    dve.wait_ge(x1_ready, a + 1)
                    layer_norm(0, a, x1[:, j % 2, :], xn2[:, :], lambda: at_least(dve, turned[0], a))
                if valid(b):
                    s = (j + 1) % 2
                    dve.wait_ge(exp_ready, b + 1)
                    at_least(dve, prob_ready, b)
                    nc.vector.reciprocal(inv[:, :], total[:, s, :]).then_inc(inv_ready, 1)
                if valid(c):
                    s = j % 2
                    dve.wait_ge(out_ready, c + 1)
                    dve.wait_ge(x1b_ready, c + 1)
                    if not isinstance(c, int) or c >= 2:
                        dve.wait_ge(stored[s], 32 * (2 * i + j // 2 - 1))
                    nc.vector.tensor_tensor(x2[:, s, :], pO[:, :], x1b[:, (j + NT - LAG_C) % NT, :], ALU.add).then_inc(x2_ready, 1)
                    dve.wait_ge(x2_ready, c + 1)
                    layer_norm(1, c, x2[:, s, :], xn3[:, s, :], lambda: at_least(dve, turned[1], c - 1))

            ticks(dve, tick)

        @block.scalar
        def _(act):
            def probT_out(c, j, g):
                act.wait_ge(prob_turned, NP * c + g + 1)
                if g == 0:
                    at_least(act, out_ready, c - 1)
                n = len(TP[g])
                for rows, cols in ((P, [k for k in TP[g] if (k + 1) * P <= XK]), (XK % P, [k for k in TP[g] if (k + 1) * P > XK])):
                    if cols:
                        k0, kn = cols[0], cols[-1] + 1
                        last = nc.scalar.activation(probT[0:rows, j % 2, k0:kn, :],
                                                    pP[0:rows, (j * NP + g) % 2, (k0 - TP[g][0]) * P:(kn - TP[g][0]) * P]
                                                    .rearrange("p (k q) -> p k q", q=P), ACT.Copy)
                last.then_inc(probT_ready, 1)

            act.wait_ge(weights_loaded, WAIT_W)

            def tick(i, j, valid):
                n = NT * i + j
                a, b, c, d = n, n - LAG_B, n - LAG_C, n - LAG_D
                if valid(c):
                    probT_out(c, j, 0)
                    probT_out(c, j, 1)
                if valid(d):
                    s = (j + 1) % 2
                    act.wait_ge(turned[1], d + 1)
                    if not isinstance(d, int) or d >= 2:
                        act.wait_ge(storedT[s], 16 * (2 * i + (j + 1) // 2 - 2))
                        act.wait_ge(slot_ready, d - 1)
                    nc.scalar.activation(xn3T[:, s, :, :], pX[:, :].rearrange("p (k q) -> p k q", k=KD), ACT.Copy
                                         ).then_inc(xT_ready[1], 1)
                if valid(b):
                    s = (j + 1) % 2
                    act.wait_ge(nmx_ready, b + 1)
                    at_least(act, prob_turned, NP * (b - 1))
                    for h in range(XH):
                        last = nc.scalar.activation(prob[:, s, h, :], pS[:, h // HB, h % HB * KEYS:(h % HB + 1) * KEYS], ACT.Exp,
                                                    bias=nmx[:, h:h + 1], scale=XSCALE, accum_out=total[:, s, h:h + 1])
                    last.then_inc(exp_ready, 1)
                if valid(c):
                    probT_out(c, j, 2)
                if valid(a):
                    act.wait_ge(turned[0], a + 1)
                    at_least(act, score_ready, a - 1)
                    nc.scalar.activation(xn2T[:, j % 2, :, :], pX[:, :].rearrange("p (k q) -> p k q", k=KD), ACT.Copy
                                         ).then_inc(xT_ready[0], 1)
                if valid(d):
                    act.wait_ge(slot_ready, d + 1)
                    for m in range(MS):
                        last = nc.scalar.activation(s_sc[:, m, bass.ds(d * P, P)], pO[:, m * P:(m + 1) * P], ACT.Identity,
                                                    bias=dqb[:, m:m + 1])
                    last.then_inc(slot_taken, 1)

            ticks(act, tick)

        @block.tensor
        def _(pe):
            def turn(s, t, src):
                for k in range(KD):
                    last = nc.tensor.transpose(pX[:, k * P:(k + 1) * P], src[:, k * P:(k + 1) * P], ident[:, :])
                last.then_inc(turned[s], 1)

            def turn_prob(c, j, g):
                at_least(pe, probT_ready, NP * c + g - 1)
                if g == 0:
                    pe.wait_ge(prob_ready, c + 1)
                flat = prob[:, j % 2, :, :].rearrange("p h c -> p (h c)")
                for k in TP[g]:
                    w = min(P, XK - k * P)
                    last = nc.tensor.transpose(pP[0:w, (j * NP + g) % 2, (k - TP[g][0]) * P:(k - TP[g][0] + 1) * P],
                                               flat[:, k * P:k * P + w], ident[:, :])
                last.then_inc(prob_turned, 1)

            def outputs(c, j, g):
                pe.wait_ge(probT_ready, NP * c + g + 1)
                for k in TP[g]:
                    w = min(P, XK - k * P)
                    last = nc.tensor.matmul(pO[:, :], probT[0:w, j % 2, k, :], vwo[0:w, k, :], start=(k == 0), stop=(k == XT - 1))
                if g == NP - 1:
                    last.then_inc(out_ready, 1)

            pe.wait_ge(ident_ready, 1)
            pe.wait_ge(weights_loaded, WAIT_W)

            def tick(i, j, valid):
                n = NT * i + j
                a, b, c, d = n, n - LAG_B, n - LAG_C, n - LAG_D
                if valid(b):
                    pe.wait_ge(xT_ready[0], b + 1)
                    at_least(pe, exp_ready, b)
                    for g, (h0, h1) in enumerate(GROUPS):
                        for k in range(KD):
                            last = nc.tensor.matmul(pS[:, g, 0:(h1 - h0) * KEYS], xn2T[:, (j + 1) % 2, k, :],
                                                    wkx[:, k, h0 * KEYS:h1 * KEYS], start=(k == 0), stop=(k == KD - 1))
                    last.then_inc(score_ready, 1)
                if valid(c):
                    turn_prob(c, j, 0)
                    turn_prob(c, j, 1)
                if valid(a):
                    pe.wait_ge(tile_loaded[j], 32 * (i + 1))
                    at_least(pe, x1_ready, a)
                    for g in range(HG):
                        last = nc.tensor.matmul(pA[:, :], aT[:, j, g, :], wo[:, g, :], start=(g == 0), stop=(g == HG - 1))
                    last.then_inc(projected, 1)
                if valid(d):
                    pe.wait_ge(xn_ready[1], d + 1)
                    pe.wait_ge(xT_ready[0], upto(d + LAG_D))
                    turn(1, d, xn3[:, (j + 1) % 2, :])
                if valid(c):
                    at_least(pe, slot_taken, c - 1)
                    outputs(c, j, 0)
                    turn_prob(c, j, 2)
                    outputs(c, j, 1)
                    outputs(c, j, 2)
                if valid(a):
                    pe.wait_ge(xn_ready[0], a + 1)
                    at_least(pe, xT_ready[1], a - LAG_D + 1)
                    turn(0, a, xn2)
                if valid(d):
                    pe.wait_ge(xT_ready[1], d + 1)
                    pe.wait_ge(x2_ready, upto(d + 2))
                    for m in range(MS):
                        for k in range(KD):
                            last = nc.tensor.matmul(pO[:, m * P:(m + 1) * P], dqk[:, k, m * P:(m + 1) * P],
                                                    xn3T[:, (j + 1) % 2, k, :], start=(k == 0), stop=(k == KD - 1))
                    last.then_inc(slot_ready, 1)

            ticks(pe, tick)


F = 2048
CF = F // BLK
R = B * NS
PIECES = 2 * KD + CF
DT = B * T // NS
DTT = DT // P


def load_expert(eng, ring, loaded, e, W1, Wg, W2, pieces):
    for n in pieces:
        if n < 2 * KD:
            w = (W1, Wg)[n // KD]
            src = w[e, n % KD * P:(n % KD + 1) * P, :]
            dst = ring[:, n, :]
        else:
            c = n - 2 * KD
            src = W2[e, c * BLK:(c + 1) * BLK, :].rearrange("(j p) n -> p j n", p=P)
            dst = ring[:, n, :].rearrange("p (j n) -> p j n", n=D)
        eng.dma_start(dst, src).then_inc(loaded[n], 16)


def dispatch(nc, sem, s_sc, spare, xn_sc, slot_query, Wv, bv, Wo, bo, ln_g, ln_b, b1, bg, W1, Wg, W2, ring, piece_loaded, o, hT, bT):
    with ExitStack() as ctx:
        sb = lambda name, shape, dt: ctx.enter_context(nc.sbuf_tensor(name, shape, dt))
        CH = 4
        NCH = T // P // CH
        UN = B * NCH * MS
        ident = sb("D_ident", [P, P], F32)
        power = sb("D_power", [P, 1], F32)
        smax = sb("D_smax", [P, B, MS], F32)
        snm = sb("D_snm", [P, B, MS], F32)
        stot = sb("D_stot", [P, B, MS], F32)
        sinv = sb("D_sinv", [P, B, MS], F32)
        pT = sb("D_pT", [P, 2, CH, P], F32)
        un = sb("D_un", [P, B, MS, D], F32)
        uT = sb("D_uT", [P, KD, H, B, NS], F32)
        xn = spare[:, 0, :].rearrange("p (s t d) -> p s t d", s=2, d=D)
        weights = spare[:, 1, :].rearrange("p (w k n) -> p w k n", w=2, n=D)
        wv, wo = weights[:, 0, :, :], weights[:, 1, :, :]
        rows = sb("D_rows", [R, 5, D], F32)
        oa = sb("D_oa", [R, D], F32)
        oaT = sb("D_oaT", [P, KD, R], F32)
        stats = sb("D_stats", [R, 6], F32)
        mv = sb("D_mv", [R, 2], F32)
        vare = sb("D_vare", [R, 1], F32)
        rstd = sb("D_rstd", [R, 1], F32)
        hn = sb("D_hn", [R, 2, D], F32)
        brow = sb("D_brow", [P, 2, 2, P], F32)
        bank = [ctx.enter_context(nc.psum_tensor(f"D_bank{n}", [P, BLK], F32)) for n in range(4)]
        pU = [ctx.enter_context(nc.psum_tensor(f"D_pU{n}", [P, BLK], F32)) for n in range(4)]
        zeroed = sem("D_zeroed")
        ident_ready = sem("D_ident_ready")
        xn_loaded = [sem(f"D_xn_loaded{s}") for s in range(2)]
        rows_loaded = sem("D_rows_loaded")
        weights_loaded = sem("D_weights_loaded")
        bias_loaded = sem("D_bias_loaded")
        max_ready = sem("D_max_ready")
        exp_ready = sem("D_exp_ready")
        inv_ready = sem("D_inv_ready")
        made = sem("D_made")
        taken = sem("D_taken")
        mixed = sem("D_mixed")
        un_ready = sem("D_un_ready")
        step = sem("D_step")
        var_ready = sem("D_var_ready")
        rstd_ready = sem("D_rstd_ready")
        block = ctx.enter_context(nc.Block())

        names = ([("bT", n) for n in range(2)] + [("pT", n) for n in range(UN)] + [("uT", b, m) for b in range(B) for m in range(MS)]
                 + ["heads", "oaT", "out", "hT"])
        nth = {name: n for n, name in enumerate(names)}

        @block.sync
        def _(sp):
            def tokens(n):
                sp.dma_start(xn[:, n % 2, :, :], xn_sc[n * CH:(n + 1) * CH].rearrange("t p d -> p t d")).then_inc(xn_loaded[n % 2], 16)

            tokens(0)
            tokens(1)
            for n, src in enumerate((b1, bg)):
                sp.dma_start(brow[:, n, :, :], src.rearrange("e (q p) -> (e q) p", p=P).rearrange("(a r) p -> r a p", a=2)
                             ).then_inc(bias_loaded, 16)
            for b in range(B):
                r = slice(b * NS, (b + 1) * NS)
                for n, src in ((0, slot_query[0]), (3, ln_g), (4, ln_b)):
                    sp.dma_start(rows[r, n, :], src).then_inc(rows_loaded, 16)
            for n, src in ((1, bo), (2, bv)):
                sp.dma_start(rows[:, n, :], src.partition_broadcast(R)).then_inc(rows_loaded, 16)
            sp.dma_start(wv[:, :, :], Wv.rearrange("(k p) n -> p k n", p=P)).then_inc(weights_loaded, 16)
            sp.dma_start(wo[:, :, :], Wo.rearrange("(k p) n -> p k n", p=P)).then_inc(weights_loaded, 16)
            for n in range(2, B * NCH):
                sp.wait_ge(mixed, (n - 1) * MS)
                tokens(n)
                if n < 2 + PIECES // 3:
                    load_expert(sp, ring, piece_loaded, 0, W1, Wg, W2, range(3 * (n - 2), 3 * (n - 1)))

        @block.gpsimd
        def _(pool):
            identity(pool, ident, zeroed, ident_ready)
            pool.memset(power[:, :], -0.5).then_inc(zeroed, 1)
            pool.wait_ge(zeroed, 2)
            pool.wait_ge(rows_loaded, 16 * 8)
            nc.gpsimd.tensor_tensor(rows[:, 0, :], rows[:, 0, :], rows[:, 1, :], ALU.add).then_inc(zeroed, 1)
            pool.wait_ge(var_ready, 1)
            nc.gpsimd.tensor_tensor(rstd[:, :], vare[:, :], power[0:R, :], ALU.pow).then_inc(rstd_ready, 1)

        @block.scalar
        def _(act):
            for b in range(B):
                for m in range(MS):
                    act.wait_ge(max_ready, 2 * (b * MS + m) + 2)
                    t = s_sc[:, m, b * T:(b + 1) * T]
                    nc.scalar.activation(t, t, ACT.Exp, bias=snm[:, b, m:m + 1], scale=SCALE, accum_out=stot[:, b, m:m + 1]
                                         ).then_inc(exp_ready, 1)

        @block.vector
        def _(dve):
            def take(name, dst, src):
                dve.wait_ge(made, nth[name] + 1)
                nc.vector.tensor_copy(dst, src).then_inc(taken, 1)

            for b in range(B):
                for m in range(MS):
                    n = 2 * (b * MS + m)
                    nc.vector.tensor_reduce(smax[:, b, m:m + 1], s_sc[:, m, b * T:(b + 1) * T], AX.X, ALU.max).then_inc(max_ready, 1)
                    dve.wait_ge(max_ready, n + 1)
                    nc.vector.tensor_scalar(snm[:, b, m:m + 1], smax[:, b, m:m + 1], -SCALE, None, ALU.mult).then_inc(max_ready, 1)
            for n in range(2):
                dve.wait_ge(made, nth[("bT", n)] + 1)
                nc.vector.tensor_copy(bT[:, n, :, :, :].rearrange("p e j c -> p e c j"),
                                      bank[nth[("bT", n)] % 4][:, 0:2 * P].rearrange("p (e c j) -> p e c j", e=NS, c=CF)
                                      ).then_inc(taken, 1)
            for n in range(UN):
                dve.wait_ge(mixed, n - 1) if n >= 2 else None
                take(("pT", n), pT[:, n % 2, :, :], bank[nth[("pT", n)] % 4][:, :].rearrange("p (t r) -> p t r", t=CH))
            dve.wait_ge(exp_ready, B * MS)
            nc.vector.reciprocal(sinv[:, :, :], stot[:, :, :]).then_inc(inv_ready, 1)
            dve.wait_ge(inv_ready, 1)
            dve.wait_ge(mixed, UN)
            for b in range(B):
                for m in range(MS):
                    nc.vector.tensor_scalar(un[:, b, m, :], pU[b * MS + m][:, :], sinv[:, b, m:m + 1], None, ALU.mult
                                            ).then_inc(un_ready, 1)
            for b in range(B):
                for m in range(MS):
                    take(("uT", b, m), uT[:, :, m * H // MS:(m + 1) * H // MS, b, :],
                         bank[nth[("uT", b, m)] % 4][:, :].rearrange("p (k h s) -> p k h s", k=KD, s=NS))
            dve.wait_ge(rows_loaded, 16 * 8)
            dve.wait_ge(made, nth["heads"] + 1)
            nc.vector.tensor_tensor(oa[:, :], bank[nth["heads"] % 4][0:R, :], rows[:, 2, :], ALU.add).then_inc(taken, 1)
            take("oaT", oaT[:, :, :], bank[nth["oaT"] % 4][:, 0:KD * R].rearrange("p (k r) -> p k r", k=KD))
            dve.wait_ge(zeroed, 3)
            dve.wait_ge(made, nth["out"] + 1)
            nc.vector.tensor_tensor(o[:, :], bank[nth["out"] % 4][0:R, :], rows[:, 0, :], ALU.add).then_inc(taken, 1)
            dve.wait_ge(taken, nth["out"] + 1)
            nc.vector.bn_stats(stats[:, :], o[:, :]).then_inc(step, 1)
            dve.wait_ge(step, 1)
            nc.vector.bn_aggr(mv[:, :], stats[:, :]).then_inc(step, 1)
            dve.wait_ge(step, 2)
            nc.vector.tensor_scalar_add(vare[:, :], mv[:, 1:2], EPS).then_inc(var_ready, 1)
            dve.wait_ge(rstd_ready, 1)
            nc.vector.tensor_scalar(hn[:, 0, :], o[:, :], mv[:, 0:1], rstd[:, 0:1], ALU.subtract, ALU.mult).then_inc(step, 1)
            dve.wait_ge(step, 3)
            nc.vector.tensor_tensor(hn[:, 1, :], hn[:, 0, :], rows[:, 3, :], ALU.mult).then_inc(step, 1)
            dve.wait_ge(step, 4)
            nc.vector.tensor_tensor(hn[:, 0, :], hn[:, 1, :], rows[:, 4, :], ALU.add).then_inc(step, 1)
            take("hT", hT[:, :, :], bank[nth["hT"] % 4][:, 0:KD * R].rearrange("p (k r) -> p k r", k=KD))

        @block.tensor
        def _(pe):
            def into(name):
                n = nth[name]
                if n >= 4:
                    pe.wait_ge(taken, n - 3)
                return bank[n % 4]

            def mix(n):
                b, ch, m = n // (NCH * MS), n // MS % NCH, n % MS
                c = n // MS
                pe.wait_ge(xn_loaded[c % 2], 16 * (c // 2 + 1))
                pe.wait_ge(taken, nth[("pT", n)] + 1)
                for t in range(CH):
                    last = nc.tensor.matmul(pU[b * MS + m][:, :], pT[:, n % 2, t, :], xn[:, c % 2, t, :],
                                            start=(ch == 0 and t == 0), stop=(ch == NCH - 1 and t == CH - 1))
                last.then_inc(mixed, 1)

            pe.wait_ge(ident_ready, 1)
            pe.wait_ge(bias_loaded, 32)
            for n in range(2):
                out = into(("bT", n))
                for a in range(2):
                    last = nc.tensor.transpose(out[:, a * P:(a + 1) * P], brow[:, n, a, :], ident[:, :])
                last.then_inc(made, 1)
            for n in range(UN):
                b, ch, m = n // (NCH * MS), n // MS % NCH, n % MS
                pe.wait_ge(exp_ready, b * MS + m + 1)
                out = into(("pT", n))
                for t in range(CH):
                    c0 = b * T + (ch * CH + t) * P
                    last = nc.tensor.transpose(out[:, t * P:(t + 1) * P], s_sc[:, m, c0:c0 + P], ident[:, :])
                last.then_inc(made, 1)
                if n:
                    mix(n - 1)
            mix(UN - 1)
            for b in range(B):
                for m in range(MS):
                    pe.wait_ge(un_ready, b * MS + m + 1)
                    out = into(("uT", b, m))
                    for k in range(KD):
                        last = nc.tensor.transpose(out[:, k * P:(k + 1) * P], un[:, b, m, k * P:(k + 1) * P], ident[:, :])
                    last.then_inc(made, 1)
            pe.wait_ge(taken, nth[("uT", B - 1, MS - 1)] + 1)
            pe.wait_ge(weights_loaded, 32)
            out = into("heads")
            for h in range(H):
                for k in range(KD):
                    last = nc.tensor.matmul(out[0:R, h * DH:(h + 1) * DH], uT[:, k, h, :, :].rearrange("p b s -> p (b s)"),
                                            wv[:, k, h * DH:(h + 1) * DH], start=(k == 0), stop=(k == KD - 1))
            last.then_inc(made, 1)
            pe.wait_ge(taken, nth["heads"] + 1)
            out = into("oaT")
            for k in range(KD):
                last = nc.tensor.transpose(out[:, k * R:(k + 1) * R], oa[:, k * P:(k + 1) * P], ident[0:R, 0:R])
            last.then_inc(made, 1)
            pe.wait_ge(taken, nth["oaT"] + 1)
            out = into("out")
            for k in range(KD):
                last = nc.tensor.matmul(out[0:R, :], oaT[:, k, :], wo[:, k, :], start=(k == 0), stop=(k == KD - 1))
            last.then_inc(made, 1)
            pe.wait_ge(step, 5)
            out = into("hT")
            for k in range(KD):
                last = nc.tensor.transpose(out[:, k * R:(k + 1) * R], hn[:, 0, k * P:(k + 1) * P], ident[0:R, 0:R])
            last.then_inc(made, 1)


def experts(nc, sem, W1, Wg, W2, b2, xT_sc, c_Wq, c_bq, ring, piece_loaded, o, hT, bT, qc, o2):
    with ExitStack() as ctx:
        sb = lambda name, shape, dt: ctx.enter_context(nc.sbuf_tensor(name, shape, dt))
        ps = lambda name, shape, dt: ctx.enter_context(nc.psum_tensor(name, shape, dt))
        ident = sb("E_ident", [P, P], F32)
        fold = sb("E_fold", [P, R], F32)
        zero = sb("E_zero", [P, BLK], F32)
        rows = sb("E_rows", [R, D], F32)
        base = sb("E_base", [R, D], F32)
        cbq = sb("E_cbq", [P, KD], F32)
        wq = sb("E_wq", [P, KD, D], F32)
        xq = sb("E_xq", [P, 2, DTT, KD, P], F32)
        inner = sb("E_inner", [P, 2, BLK], F32)
        ug = sb("E_ug", [P, 2, CF * NT, B], F32)
        ex = sb("E_ex", [P, 2, CF * NT, B], F32)
        ex1 = sb("E_ex1", [P, 2, CF * NT, B], F32)
        sg = sb("E_sg", [P, 2, CF * NT, B], F32)
        si = sb("E_si", [P, 2, CF * NT, B], F32)
        vT = sb("E_vT", [P, CF * NT, B, NS], F32)
        ysb = sb("E_ysb", [P, BLK], F32)
        pI = ps("E_pI", [P, 2, BLK], F32)
        pT = ps("E_pT", [P, 2, BLK], F32)
        pY = ps("E_pY", [P, BLK], F32)
        pQ = ps("E_pQ", [P, 2, 2, DT], F32)
        pool_carried = sem("E_pool_carried")
        sp_carried = sem("E_sp_carried")
        zeroed = sem("E_zeroed")
        ident_ready = sem("E_ident_ready")
        fold_ready = sem("E_fold_ready")
        small_loaded = sem("E_small_loaded")
        xq_loaded = [sem(f"E_xq_loaded{s}") for s in range(2)]
        q_made = sem("E_q_made")
        q_taken = sem("E_q_taken")
        inner_made = sem("E_inner_made")
        inner_taken = sem("E_inner_taken")
        turned = sem("E_turned")
        ug_ready = sem("E_ug_ready")
        ex_ready = sem("E_ex_ready")
        step = sem("E_step")
        v_clear = sem("E_v_clear")
        v_ready = sem("E_v_ready")
        y_done = sem("E_y_done")
        y_copied = sem("E_y_copied")
        y_sum = sem("E_y_sum")
        o2_ready = sem("E_o2_ready")
        block = ctx.enter_context(nc.Block())

        @block.sync
        def _(sp):
            sp.dma_start(rows[:, :][0:NS, :], b2).then_inc(small_loaded, 16)
            sp.dma_start(rows[:, :][NS:R, :], b2).then_inc(small_loaded, 16)
            with sp.Fori(1, NS) as e:
                sp.wait_ge(inner_made, 2 * e - 1)
                carry(sp, sp_carried)
                load_expert(sp, ring, piece_loaded, e, W1, Wg, W2, range(0, KD))
                sp.wait_ge(inner_made, 2 * e)
                carry(sp, sp_carried)
                load_expert(sp, ring, piece_loaded, e, W1, Wg, W2, range(KD, 2 * KD))
                sp.wait_ge(y_done, e)
                carry(sp, sp_carried)
                load_expert(sp, ring, piece_loaded, e, W1, Wg, W2, range(2 * KD, PIECES))

        @block.gpsimd
        def _(pool):
            identity(pool, ident, zeroed, ident_ready)
            pool.memset(zero[:, :], 0.0).then_inc(zeroed, 1)
            pool.memset(vT[:, :, :, :], 0.0).then_inc(v_clear, 1)
            pool.wait_ge(small_loaded, 16 * 4)
            nc.gpsimd.tensor_tensor(base[:, :], o[:, :], rows[:, :], ALU.add).then_inc(zeroed, 1)
            with pool.Fori(1, NS) as e:
                pool.wait_ge(y_done, e)
                carry(pool, pool_carried)
                pool.memset(vT[:, :, :, :], 0.0).then_inc(v_clear, 1)

        @block.vector
        def _(dve):
            dve.wait_ge(ident_ready, 1)
            nc.vector.tensor_reduce(fold[:, :], ident[:, :].rearrange("p (c r) -> p r c", r=R), AX.X, ALU.add).then_inc(fold_ready, 1)
            with dve.Fori(0, NS) as e:
                dve.wait_ge(turned, e + 1)
                for n in range(2):
                    last = nc.vector.tensor_tensor(
                        ug[:, n, :, :], pT[:, n, :].rearrange("p (q b s) -> p q b s", b=B, s=NS)[:, :, :, bass.ds(e, 1)].rearrange("p q b s -> p q (b s)"),
                        bT[:, n, :, :, :].rearrange("p e j c -> p (e j c)")[:, bass.ds(e * CF * NT, CF * NT)].unsqueeze(2).broadcast_to([P, CF * NT, B]),
                        ALU.add)
                last.then_inc(ug_ready, 1)
                dve.wait_ge(ex_ready, e + 1)
                nc.vector.tensor_scalar_add(ex1[:, :, :, :], ex[:, :, :, :], 1.0).then_inc(step, 1)
                dve.wait_ge(step, 3 * e + 1)
                nc.vector.reciprocal(sg[:, :, :, :], ex1[:, :, :, :]).then_inc(step, 1)
                dve.wait_ge(step, 3 * e + 2)
                nc.vector.tensor_tensor(si[:, :, :, :], ug[:, :, :, :], sg[:, :, :, :], ALU.mult).then_inc(step, 1)
                dve.wait_ge(step, 3 * e + 3)
                dve.wait_ge(v_clear, e + 1)
                nc.vector.tensor_tensor(vT[:, :, :, bass.ds(e, 1)].rearrange("p q b s -> p q (b s)"), si[:, 0, :, :], si[:, 1, :, :],
                                        ALU.mult).then_inc(v_ready, 1)
            dve.wait_ge(y_done, NS + 1)
            nc.vector.tensor_copy(ysb[:, :], pY[:, :]).then_inc(y_copied, 1)
            dve.wait_ge(y_sum, 1)
            dve.wait_ge(zeroed, 3)
            nc.vector.tensor_tensor(o2[:, :], pI[0:R, 0, :], base[:, :], ALU.add).then_inc(o2_ready, 1)

        @block.scalar
        def _(act):
            act.dma_start(cbq[:, :], c_bq.rearrange("(k p) -> p k", p=P), allow_slow_non_contiguous=True).then_inc(small_loaded, 16)
            act.dma_start(wq[:, :, :], c_Wq.rearrange("(k p) n -> p k n", p=P)).then_inc(small_loaded, 16)
            for u in range(2):
                act.dma_start(xq[:, u, :, :, :], xT_sc[u * DTT:(u + 1) * DTT].rearrange("t p k q -> p t k q")).then_inc(xq_loaded[u], 16)
            act.wait_ge(small_loaded, 64)
            with act.Fori(0, NS // 2) as i:
                for u in range(2):
                    e = 2 * i + u
                    for g in range(2):
                        act.wait_ge(q_made, 2 * e + g + 1)
                        for mm in range(2):
                            m = 2 * g + mm
                            last = nc.scalar.activation(qc[:, m, bass.ds(e * DT, DT)], pQ[:, g, mm, :], ACT.Identity, bias=cbq[:, m:m + 1])
                        last.then_inc(q_taken, 1)
                    act.dma_start(xq[:, u, :, :, :], xT_sc[bass.ds((2 * i + 2 + u) % NS * DTT, DTT)].rearrange("t p k q -> p t k q")
                                  ).then_inc(xq_loaded[u], 16)
                    for n in range(2):
                        act.wait_ge(inner_made, 2 * e + n + 1)
                        act.wait_ge(turned, e)
                        nc.scalar.activation(inner[:, n, :], pI[:, n, :], ACT.Copy).then_inc(inner_taken, 1)
                    act.wait_ge(ug_ready, e + 1)
                    nc.scalar.activation(ex[:, :, :, :], ug[:, :, :, :], ACT.Exp, scale=-1.0).then_inc(ex_ready, 1)
            for u in range(2):
                act.wait_ge(xq_loaded[u], 16 * (NS // 2 + 1))

        @block.tensor
        def _(pe):
            pe.wait_ge(ident_ready, 1)
            pe.wait_ge(zeroed, 2)
            pe.wait_ge(v_clear, 1)
            for c in range(CF):
                nc.tensor.matmul(pY[c * R:(c + 1) * R, :], vT[:, 0, :, :].rearrange("p b s -> p (b s)"), zero[:, :], start=True, stop=False,
                                 tile_position=(0, c * R), skip_group_check=True)
            pe.wait_ge(small_loaded, 64)
            with pe.Fori(0, NS // 2) as i:
                for u in range(2):
                    e = 2 * i + u
                    pe.wait_ge(xq_loaded[u], 16 * (i + 1))
                    for g in range(2):
                        pe.wait_ge(q_taken, 2 * e)
                        for mm in range(2):
                            m = 2 * g + mm
                            for k in range(KD):
                                last = nc.tensor.matmul(pQ[:, g, mm, :], wq[:, k, m * P:(m + 1) * P], xq[:, u, :, k, :],
                                                        start=(k == 0), stop=(k == KD - 1))
                        last.then_inc(q_made, 1)
                    for n in range(2):
                        pe.wait_ge(inner_taken, 2 * e)
                        for k in range(KD):
                            pe.wait_ge(piece_loaded[n * KD + k], 16 * (e + 1))
                            for c in range(CF):
                                last = nc.tensor.matmul(pI[c * R:(c + 1) * R, n, :], hT[:, k, :], ring[:, n * KD + k, c * BLK:(c + 1) * BLK],
                                                        start=(k == 0), stop=(k == KD - 1), tile_position=(0, c * R))
                        last.then_inc(inner_made, 1)
                    pe.wait_ge(ug_ready, e)
                    pe.wait_ge(inner_taken, 2 * e + 2)
                    for n in range(2):
                        for j in range(NT):
                            last = nc.tensor.transpose(pT[:, n, j * P:(j + 1) * P], inner[:, n, j * P:(j + 1) * P], ident[:, :])
                    last.then_inc(turned, 1)
                    pe.wait_ge(v_ready, e + 1)
                    for c in range(CF):
                        pe.wait_ge(piece_loaded[2 * KD + c], 16 * (e + 1))
                    for j in range(NT):
                        for c in range(CF):
                            last = nc.tensor.matmul(pY[c * R:(c + 1) * R, :], vT[:, j * CF + c, :, :].rearrange("p b s -> p (b s)"),
                                                    ring[:, 2 * KD + c, j * D:(j + 1) * D], start=False, stop=False,
                                                    tile_position=(0, c * R), skip_group_check=True)
                    last.then_inc(y_done, 1)
            for c in range(CF):
                last = nc.tensor.matmul(pY[c * R:(c + 1) * R, :], zero[:, 0:R], zero[:, :], start=False, stop=True,
                                        tile_position=(0, c * R), skip_group_check=True)
            last.then_inc(y_done, 1)
            pe.wait_ge(y_copied, 1)
            pe.wait_ge(fold_ready, 1)
            nc.tensor.matmul(pI[0:R, 0, :], fold[:, :], ysb[:, :], start=True, stop=True).then_inc(y_sum, 1)


CSCALE = 1.0 / DH ** 0.5
TB = T // P


def combine(nc, sem, o2, qc, c_Wk, c_bk, c_Wv, c_bv, c_Wo, c_bo, x2_sc, out):
    RT = R // B
    with ExitStack() as ctx:
        sb = lambda name, shape, dt: ctx.enter_context(nc.sbuf_tensor(name, shape, dt))
        ps = lambda name, shape, dt: ctx.enter_context(nc.psum_tensor(name, shape, dt))
        ident = sb("F_ident", [P, P], F32)
        wk = sb("F_wk", [P, KD, D], F32)
        wv = sb("F_wv", [P, KD, D], F32)
        wo = sb("F_wo", [P, HG, D], F32)
        bias = sb("F_bias", [P, 2, HG], F32)
        bo = sb("F_bo", [P, D], F32)
        o2T = sb("F_o2T", [P, KD, R], F32)
        bd = sb("F_bd", [P, 2, B, HG, HPG, RT], F32)
        vo = sb("F_vo", [P, B, 2, D], F32)
        qst = sb("F_qst", [P, 2, HG, P], F32)
        x2 = sb("F_x2", [P, NT, D], F32)
        mx = sb("F_mx", [P, H], F32)
        sc = sb("F_sc", [P, H, RT], F32)
        ex = sb("F_ex", [P, 2, H, RT], F32)
        total = sb("F_total", [P, H], F32)
        inv = sb("F_inv", [P, H], F32)
        prob = sb("F_prob", [P, H, RT], F32)
        probT = sb("F_probT", [P, 2, 2, P], F32)
        res = sb("F_res", [P, 2, D], F32)
        pK = ps("F_pK", [P, 2, HG, R], F32)
        pV = ps("F_pV", [P, BLK], F32)
        pS = ps("F_pS", [P, 2, BLK], F32)
        pP = ps("F_pP", [P, BLK], F32)
        pO = ps("F_pO", [P, 2, BLK], F32)
        sp_carried = sem("F_sp_carried")
        zeroed = sem("F_zeroed")
        ident_ready = sem("F_ident_ready")
        weights_loaded = sem("F_weights_loaded")
        tile_loaded = [sem(f"F_tile_loaded{s}") for s in range(NT)]
        o2_turned = sem("F_o2_turned")
        o2T_ready = sem("F_o2T_ready")
        kv_made = sem("F_kv_made")
        bd_ready = sem("F_bd_ready")
        vo_made = sem("F_vo_made")
        vo_ready = sem("F_vo_ready")
        q_staged = sem("F_q_staged")
        xb_ready = sem("F_xb_ready")
        score_ready = sem("F_score_ready")
        max_ready = sem("F_max_ready")
        sc_ready = sem("F_sc_ready")
        ex_ready = sem("F_ex_ready")
        sum_ready = sem("F_sum_ready")
        inv_ready = sem("F_inv_ready")
        prob_ready = sem("F_prob_ready")
        prob_turned = sem("F_prob_turned")
        probT_ready = sem("F_probT_ready")
        out_ready = sem("F_out_ready")
        res_ready = sem("F_res_ready")
        stored = [sem(f"F_stored{s}") for s in range(2)]
        ov = out.rearrange("b (t p) d -> (b t) p d", p=P)
        block = ctx.enter_context(nc.Block())
        WAIT_W = 16 * 6

        @block.sync
        def _(sp):
            def load_at(t, j):
                sp.dma_start(x2[:, j, :], x2_sc[t]).then_inc(tile_loaded[j], 16)

            for weights, dst in ((c_Wk, wk), (c_Wv, wv), (c_Wo, wo)):
                sp.dma_start(dst[:, :, :], weights.rearrange("(k p) n -> p k n", p=P)).then_inc(weights_loaded, 16)
            for j in range(NT - 1):
                load_at(j, j)

            def tick(i, j, valid):
                n = NT * i + j
                a, c = n, n - LAG_C
                if valid(a):
                    at_least(sp, res_ready, a)
                    carry(sp, sp_carried)
                    load_at((a + NT - 1) % TILES, (j + NT - 1) % NT)
                if valid(c):
                    sp.wait_ge(res_ready, c + 1)
                    sp.dma_start(ov[c], res[:, j % 2, :]).then_inc(stored[j % 2], 16)

            ticks(sp, tick)
            for s in range(2):
                sp.wait_ge(stored[s], 16 * TILES // 2)
            for j in range(NT):
                sp.wait_ge(tile_loaded[j], 16 * (TILES // NT + (j < NT - 1)))

        @block.gpsimd
        def _(pool):
            pool.memset(bd[:, :, :, :, :, :], 0.0).then_inc(zeroed, 1)
            pool.memset(ident[:, :], 0.0).then_inc(zeroed, 1)
            pool.wait_ge(zeroed, 2)
            pool.affine_select(out=ident[:, :], in_=ident[:, :], compare_op=ALU.not_equal, fill=1.0,
                               base=0, pattern=[[-1, P]], channel_multiplier=1).then_inc(ident_ready, 1)
            pool.wait_ge(weights_loaded, WAIT_W)

            def tick(i, j, valid):
                n = NT * i + j
                if valid(n):
                    at_least(pool, score_ready, n - 1)
                    nc.gpsimd.tensor_copy(qst[:, j % 2, :, :], qc[:, :, bass.ds(n * P, P)]).then_inc(q_staged, 1)
                    pool.wait_ge(tile_loaded[j], 16 * (i + 1))
                    nc.gpsimd.tensor_tensor(x2[:, j, :], x2[:, j, :], bo[:, :], ALU.add).then_inc(xb_ready, 1)

            ticks(pool, tick)

        @block.vector
        def _(dve):
            dve.wait_ge(o2_turned, 1)
            nc.vector.tensor_copy(o2T[:, :, :], pV[:, 0:KD * R].rearrange("p (k r) -> p k r", k=KD)).then_inc(o2T_ready, 1)
            dve.wait_ge(zeroed, 1)
            dve.wait_ge(weights_loaded, WAIT_W)
            dve.wait_ge(kv_made, 1)
            for h in range(HPG):
                rows = slice(h * DH, (h + 1) * DH)
                for n in range(2):
                    for b in range(B):
                        last = nc.vector.tensor_tensor(bd[rows, n, b, :, h, :], pK[rows, n, :, b * RT:(b + 1) * RT],
                                                       bias[rows, n, :].unsqueeze(2).broadcast_to([DH, HG, RT]), ALU.add)
            last.then_inc(bd_ready, 1)

            def tick(i, j, valid):
                n = NT * i + j
                a, b, c = n, n - LAG_B, n - LAG_C
                if valid(a):
                    dve.wait_ge(score_ready, a + 1)
                    at_least(dve, sc_ready, a)
                    s = pS[:, j % 2, 0:H * RT].rearrange("p (h s) -> p h s", s=RT)
                    nc.vector.tensor_reduce(mx[:, :], s, AX.X, ALU.max).then_inc(max_ready, 1)
                    dve.wait_ge(max_ready, a + 1)
                    at_least(dve, ex_ready, a)
                    nc.vector.tensor_tensor(sc[:, :, :], s, mx[:, :].unsqueeze(2).broadcast_to([P, H, RT]), ALU.subtract
                                            ).then_inc(sc_ready, 1)
                if valid(b):
                    s = (j + 1) % 2
                    dve.wait_ge(ex_ready, b + 1)
                    at_least(dve, prob_ready, b)
                    nc.vector.tensor_reduce(total[:, :], ex[:, s, :, :], AX.X, ALU.add).then_inc(sum_ready, 1)
                    dve.wait_ge(sum_ready, b + 1)
                    nc.vector.reciprocal(inv[:, :], total[:, :]).then_inc(inv_ready, 1)
                    dve.wait_ge(inv_ready, b + 1)
                    at_least(dve, prob_turned, b)
                    nc.vector.tensor_tensor(prob[:, :, :], ex[:, s, :, :], inv[:, :].unsqueeze(2).broadcast_to([P, H, RT]), ALU.mult
                                            ).then_inc(prob_ready, 1)
                if valid(c):
                    s = j % 2
                    dve.wait_ge(out_ready, c + 1)
                    dve.wait_ge(xb_ready, c + 1)
                    if not isinstance(c, int) or c >= 2:
                        dve.wait_ge(stored[s], 16 * (2 * i + j // 2 - 1))
                    nc.vector.tensor_tensor(res[:, s, :], pO[:, s, :], x2[:, (j + NT - LAG_C) % NT, :], ALU.add).then_inc(res_ready, 1)

            ticks(dve, tick)

        @block.scalar
        def _(act):
            for n, b in enumerate((c_bk, c_bv)):
                act.dma_start(bias[:, n, :], b.rearrange("(g p) -> p g", p=P), allow_slow_non_contiguous=True).then_inc(weights_loaded, 16)
            act.dma_start(bo[:, :], c_bo.partition_broadcast(P)).then_inc(weights_loaded, 16)
            for b in range(B):
                act.wait_ge(vo_made, b + 1)
                nc.scalar.activation(vo[:, b, :, :], pO[:, :, :], ACT.Copy).then_inc(vo_ready, 1)

            def tick(i, j, valid):
                n = NT * i + j
                a, b = n, n - LAG_B
                if valid(a):
                    act.wait_ge(sc_ready, a + 1)
                    at_least(act, prob_ready, a - 1)
                    nc.scalar.activation(ex[:, j % 2, :, :], sc[:, :, :], ACT.Exp, scale=CSCALE).then_inc(ex_ready, 1)
                if valid(b):
                    s = (j + 1) % 2
                    act.wait_ge(prob_turned, b + 1)
                    at_least(act, out_ready, b - 1)
                    nc.scalar.activation(probT[:, s, :, :], pP[:, 0:2 * P].rearrange("p (g q) -> p g q", g=2), ACT.Copy
                                         ).then_inc(probT_ready, 1)

            ticks(act, tick)

        @block.tensor
        def _(pe):
            pe.wait_ge(ident_ready, 1)
            for k in range(KD):
                last = nc.tensor.transpose(pV[:, k * R:(k + 1) * R], o2[:, k * P:(k + 1) * P], ident[0:R, 0:R])
            last.then_inc(o2_turned, 1)
            pe.wait_ge(o2T_ready, 1)
            pe.wait_ge(weights_loaded, WAIT_W)
            for n, w in enumerate((wk, wv)):
                for g in range(HG):
                    for k in range(KD):
                        last = nc.tensor.matmul(pK[:, n, g, :], w[:, k, g * P:(g + 1) * P], o2T[:, k, :],
                                                start=(k == 0), stop=(k == KD - 1))
            last.then_inc(kv_made, 1)
            pe.wait_ge(bd_ready, 1)
            for b in range(B):
                if b:
                    pe.wait_ge(vo_ready, b)
                for g in range(HG):
                    r = g % 2 * HPG * RT
                    last = nc.tensor.matmul(pO[r:r + HPG * RT, g // 2, :], bd[:, 1, b, g, :, :].rearrange("p h s -> p (h s)"),
                                            wo[:, g, :], start=True, stop=True, tile_position=(0, r))
                last.then_inc(vo_made, 1)
            pe.wait_ge(vo_ready, B)

            def tick(i, j, valid):
                n = NT * i + j
                a, b, c = n, n - LAG_B, n - LAG_C
                if valid(a):
                    pe.wait_ge(q_staged, a + 1)
                    at_least(pe, sc_ready, a - 1)
                    for g in range(HG):
                        last = nc.tensor.matmul(pS[:, j % 2, g * HPG * RT:(g + 1) * HPG * RT], qst[:, j % 2, g, :],
                                                bd[:, 0, a // TB, g, :, :].rearrange("p h s -> p (h s)") if isinstance(a, int) else
                                                bd[:, 0, bass.ds(a // TB, 1), g, :, :].rearrange("p o h s -> p (o h s)"),
                                                start=True, stop=True)
                    last.then_inc(score_ready, 1)
                if valid(c):
                    s = j % 2
                    pe.wait_ge(probT_ready, c + 1)
                    at_least(pe, res_ready, c - 1)
                    for g in range(2):
                        last = nc.tensor.matmul(pO[:, s, :], probT[:, s, g, :], vo[:, c // TB, g, :] if isinstance(c, int) else
                                                vo[:, bass.ds(c // TB, 1), g, :].rearrange("p o d -> p (o d)"),
                                                start=(g == 0), stop=(g == 1))
                    last.then_inc(out_ready, 1)
                if valid(b):
                    pe.wait_ge(prob_ready, b + 1)
                    at_least(pe, probT_ready, b)
                    for g in range(2):
                        last = nc.tensor.transpose(pP[:, g * P:(g + 1) * P],
                                                   prob[:, g * H // 2:(g + 1) * H // 2, :].rearrange("p h s -> p (h s)"), ident[:, :])
                    last.then_inc(prob_turned, 1)

            ticks(pe, tick)


def decoder_layer(nc, names, args):
    a = dict(zip(names, args))
    out = args[-1]

    def phase(program, *operands):
        taken = []

        def sem(name):
            taken.append(nc.alloc_semaphore(name))
            return taken[-1]

        program(nc, sem, *operands)
        nc.clear_and_free_semaphores(taken)
        nc.all_engine_barrier()

    dram = lambda name, *shape: nc.dram_tensor(name, shape, F32, kind="Internal").ap()
    heads = (NBLK, HG, P, BLK)
    q_hi, q_lo, k_hi, k_lo = [dram(name, *heads) for name in ("q_hi", "q_lo", "k_hi", "k_lo")]
    v_sc = dram("v_sc", NBLK, NT, P, D)
    z_sc = dram("z_sc", 1, B * H)
    a_sc = dram("a_sc", *heads)
    vw_sc = dram("vw_sc", XK, D)
    x2_sc = dram("x2_sc", TILES, P, D)
    xn_sc = dram("xn_sc", TILES, P, D)
    xT_sc = dram("xT_sc", TILES, P, KD, P)

    attn = lambda name: a["L0_attn_" + name]
    xattn = lambda name: a["L0_xattn_" + name]
    ffn = lambda name: a["L0_ffn_" + name]

    phase(project_self_attention, a["x"], attn("Wq"), attn("Wk"), attn("Wv"), attn("span_w"), attn("span_b"),
                           q_hi, q_lo, k_hi, k_lo, v_sc, z_sc)
    phase(self_attention, q_hi, q_lo, k_hi, k_lo, v_sc, z_sc, a_sc)

    with ExitStack() as ffn_memory:
        qc = ffn_memory.enter_context(nc.sbuf_tensor("qc", [P, KD, B * T], F32))
        slot_scores, spare = qc[:, 0:MS, :], qc[:, MS:, :]
        with ExitStack() as folded:
            sb = lambda name, shape: folded.enter_context(nc.sbuf_tensor(name, shape, F32))
            wkx = sb("wkx", [P, KD, XK])
            vwo = sb("vwo", [P, XT, D])
            dqk = sb("dqk", [P, KD, HS])
            dqb = sb("dqb", [P, MS])
            phase(fold_weights, qc, a["ctx_768"], xattn("Wq"), xattn("Wk"), xattn("Wv"), xattn("Wout"), ffn("slot_query"),
                         ffn("d_Wq"), ffn("d_Wk"), ffn("d_bq"), ffn("d_bk"), vw_sc, wkx, vwo, dqk, dqb)
            phase(cross_attention, a["x"], a_sc, attn("Wo_w"), attn("Wo_b"), xattn("bout"), wkx, vwo, dqk, dqb,
                            x2_sc, xn_sc, xT_sc, slot_scores)
        o2 = ffn_memory.enter_context(nc.sbuf_tensor("o2", [R, D], F32))
        with ExitStack() as expert_memory:
            sb = lambda name, shape: expert_memory.enter_context(nc.sbuf_tensor(name, shape, F32))
            ring = sb("ring", [P, PIECES, F])
            o = sb("o", [R, D])
            hT = sb("hT", [P, KD, R])
            bT = sb("bT", [P, 2, NS, NT, CF])
            piece_loaded = [nc.alloc_semaphore(f"piece_loaded{n}") for n in range(PIECES)]
            phase(dispatch, slot_scores, spare, xn_sc, ffn("slot_query"), ffn("d_Wv"), ffn("d_bv"), ffn("d_Wo"), ffn("d_bo"),
                     ffn("e_ln_g"), ffn("e_ln_b"), ffn("e_b1"), ffn("e_bg"), ffn("e_W1"), ffn("e_Wg"), ffn("e_W2"),
                     ring, piece_loaded, o, hT, bT)
            phase(experts, ffn("e_W1"), ffn("e_Wg"), ffn("e_W2"), ffn("e_b2"), xT_sc, ffn("c_Wq"), ffn("c_bq"),
                    ring, piece_loaded, o, hT, bT, qc, o2)
        phase(combine, o2, qc, ffn("c_Wk"), ffn("c_bk"), ffn("c_Wv"), ffn("c_bv"), ffn("c_Wo"), ffn("c_bo"), x2_sc, out)


_INS = ["x",
        "ctx_768",
        "L0_attn_Wq",
        "L0_attn_Wk",
        "L0_attn_Wv",
        "L0_attn_Wo_w",
        "L0_attn_Wo_b",
        "L0_attn_span_w",
        "L0_attn_span_b",
        "L0_xattn_Wq",
        "L0_xattn_Wk",
        "L0_xattn_Wv",
        "L0_xattn_Wout",
        "L0_xattn_bout",
        "L0_ffn_slot_query",
        "L0_ffn_d_Wq",
        "L0_ffn_d_Wk",
        "L0_ffn_d_Wv",
        "L0_ffn_d_Wo",
        "L0_ffn_d_bq",
        "L0_ffn_d_bk",
        "L0_ffn_d_bv",
        "L0_ffn_d_bo",
        "L0_ffn_c_Wq",
        "L0_ffn_c_Wk",
        "L0_ffn_c_Wv",
        "L0_ffn_c_Wo",
        "L0_ffn_c_bq",
        "L0_ffn_c_bk",
        "L0_ffn_c_bv",
        "L0_ffn_c_bo",
        "L0_ffn_e_ln_g",
        "L0_ffn_e_ln_b",
        "L0_ffn_e_W1",
        "L0_ffn_e_b1",
        "L0_ffn_e_Wg",
        "L0_ffn_e_bg",
        "L0_ffn_e_W2",
        "L0_ffn_e_b2"]


def kernel(**inputs):
    import numpy as _np
    import concourse.bacc as _bacc
    from concourse import mybir as _mybir
    from concourse.bass_utils import run_bass_kernel_spmd as _run

    nc = _bacc.Bacc("TRN2", target_bir_lowering=False, num_devices=1)
    arrays, args = {}, []
    for name in _INS:
        a = _np.ascontiguousarray(inputs[name])
        arrays[f"in_{name}_dram"] = a
        args.append(nc.dram_tensor(f"in_{name}_dram", a.shape, _mybir.dt.from_np(a.dtype), kind="ExternalInput").ap())
    args.append(nc.dram_tensor("out_0_dram", (2, 2048, 512), _mybir.dt.float32, kind="ExternalOutput").ap())
    decoder_layer(nc, _INS, args)
    r = _run(nc, [arrays], core_ids=[0])
    return r.results[0]["out_0_dram"]
```
